# Optimizing a Trainium2 kernel written in Bass

```python
import numpy as np
import jax
import jax.numpy as jnp

def _softmax(x, axis=-1):
    return jax.nn.softmax(x, axis=axis)
def _gelu(x):
    return jax.nn.gelu(x, approximate=True)
def _silu(x):
    return jax.nn.silu(x)
def _sigmoid(x):
    return jax.nn.sigmoid(x)
def _layernorm(x, axis=-1, eps=1e-5):
    m = jnp.mean(x, axis=axis, keepdims=True)
    v = jnp.var(x, axis=axis, keepdims=True)
    return (x - m) / jnp.sqrt(v + eps)
def _scatter_add(tgt, idx, src, axis=0):
    return tgt.at[idx].add(src)
def _segment_sum(src, seg, n):
    return jax.ops.segment_sum(src, seg, n)

kernel_name = 'mk_adj_resnorm_d1_adj_256_c81e37'

def setup_inputs(seed: int = 0):
    np.random.seed(seed)
    _w = jnp.asarray
    def _rec_inputs():
        import jax
        import jax.numpy as jnp
        _gk = jax.random.key(seed)
        x = -0.0005207 + 1.001 * jax.random.normal(jax.random.fold_in(_gk, 1), (8192, 256), jnp.float32)
        _a = jax.random.bernoulli(jax.random.fold_in(_gk, 2), 0.000976562, (8192, 8192))
        _a = jnp.logical_or(_a, jnp.swapaxes(_a, -1, -2))
        _a = jnp.logical_or(_a, jnp.eye(8192, dtype=bool))
        adj = _a.astype(jnp.int32)
        return x, adj
    x, adj = _rec_inputs()
    def _L0_gnn_setup():
        import jax, jax.numpy as jnp
        import numpy as np
        N = 8192
        F_IN = 256
        F_OUT = 256
        S = 128
        D_INNER = 512

        def _ln(x, g, b, eps=1e-05):
            m = x.mean(-1, keepdims=True)
            v = ((x - m) ** 2).mean(-1, keepdims=True)
            return (x - m) / jnp.sqrt(v + eps) * g + b
        key = jax.random.key(seed)
        ks = jax.random.split(key, 20)
        s = 0.05
        d = {}
        d['h'] = jax.random.normal(ks[0], (N, F_IN), dtype=jnp.float32)
        d['adj'] = jax.random.randint(ks[1], (N, N), 0, 2, dtype=jnp.int32)
        d['W'] = jax.random.normal(ks[2], (F_IN, F_OUT), dtype=jnp.float32) * s
        d['a_src'] = jax.random.normal(ks[3], (F_OUT, 1), dtype=jnp.float32) * s
        d['a_dst'] = jax.random.normal(ks[4], (F_OUT, 1), dtype=jnp.float32) * s
        d['W_bcdt'] = jax.random.normal(ks[5], (F_OUT, 3 * S), dtype=jnp.float32) * s
        d['b_bcdt'] = jnp.zeros((3 * S,), jnp.float32)
        d['abp_w'] = jax.random.normal(ks[6], (S, F_OUT), dtype=jnp.float32) * s
        d['abp_b'] = jnp.zeros((F_OUT,), jnp.float32)
        d['cp_w'] = jax.random.normal(ks[7], (S, 1), dtype=jnp.float32) * s
        d['cp_b'] = jnp.zeros((1,), jnp.float32)
        d['W_hz'] = jax.random.normal(ks[8], (F_OUT, 2 * D_INNER), dtype=jnp.float32) * s
        d['b_hz'] = jnp.zeros((2 * D_INNER,), jnp.float32)
        d['out_w'] = jax.random.normal(ks[9], (D_INNER, F_OUT), dtype=jnp.float32) * s
        d['out_b'] = jnp.zeros((F_OUT,), jnp.float32)
        d['fe1_w'] = jax.random.normal(ks[10], (F_OUT, D_INNER), dtype=jnp.float32) * s
        d['fe1_b'] = jnp.zeros((D_INNER,), jnp.float32)
        d['fe_ln_g'] = jnp.ones((D_INNER,), jnp.float32)
        d['fe_ln_b'] = jnp.zeros((D_INNER,), jnp.float32)
        d['fe2_w'] = jax.random.normal(ks[11], (D_INNER, F_OUT), dtype=jnp.float32) * s
        d['fe2_b'] = jnp.zeros((F_OUT,), jnp.float32)
        d['A'] = jax.random.uniform(ks[12], (S,), minval=1.0, maxval=64.0, dtype=jnp.float32)
        d['D'] = jnp.ones((1,), jnp.float32)
        d['g1_w'] = jax.random.normal(ks[13], (2 * F_OUT, 2 * F_OUT), dtype=jnp.float32) * s
        d['g1_b'] = jnp.zeros((2 * F_OUT,), jnp.float32)
        d['g_ln_g'] = jnp.ones((2 * F_OUT,), jnp.float32)
        d['g_ln_b'] = jnp.zeros((2 * F_OUT,), jnp.float32)
        d['g2_w'] = jax.random.normal(ks[14], (2 * F_OUT, F_OUT), dtype=jnp.float32) * s
        d['g2_b'] = jnp.zeros((F_OUT,), jnp.float32)
        d['ln_g'] = jnp.ones((F_OUT,), jnp.float32)
        d['ln_b'] = jnp.zeros((F_OUT,), jnp.float32)
        return d
    _L0_gnn_all = _L0_gnn_setup()
    _L0_gnn_in = {k: v for k, v in _L0_gnn_all.items() if k in ('W', 'a_src', 'a_dst', 'W_bcdt', 'b_bcdt', 'abp_w', 'abp_b', 'cp_w', 'cp_b', 'W_hz', 'b_hz', 'out_w', 'out_b', 'fe1_w', 'fe1_b', 'fe_ln_g', 'fe_ln_b', 'fe2_w', 'fe2_b', 'A', 'D', 'g1_w', 'g1_b', 'g_ln_g', 'g_ln_b', 'g2_w', 'g2_b', 'ln_g', 'ln_b', )}
    del _L0_gnn_all

    return {
        "x": x,
        "adj": adj,
        "L0_gnn_W": _L0_gnn_in["W"],
        "L0_gnn_a_src": _L0_gnn_in["a_src"],
        "L0_gnn_a_dst": _L0_gnn_in["a_dst"],
        "L0_gnn_W_bcdt": _L0_gnn_in["W_bcdt"],
        "L0_gnn_b_bcdt": _L0_gnn_in["b_bcdt"],
        "L0_gnn_abp_w": _L0_gnn_in["abp_w"],
        "L0_gnn_abp_b": _L0_gnn_in["abp_b"],
        "L0_gnn_cp_w": _L0_gnn_in["cp_w"],
        "L0_gnn_cp_b": _L0_gnn_in["cp_b"],
        "L0_gnn_W_hz": _L0_gnn_in["W_hz"],
        "L0_gnn_b_hz": _L0_gnn_in["b_hz"],
        "L0_gnn_out_w": _L0_gnn_in["out_w"],
        "L0_gnn_out_b": _L0_gnn_in["out_b"],
        "L0_gnn_fe1_w": _L0_gnn_in["fe1_w"],
        "L0_gnn_fe1_b": _L0_gnn_in["fe1_b"],
        "L0_gnn_fe_ln_g": _L0_gnn_in["fe_ln_g"],
        "L0_gnn_fe_ln_b": _L0_gnn_in["fe_ln_b"],
        "L0_gnn_fe2_w": _L0_gnn_in["fe2_w"],
        "L0_gnn_fe2_b": _L0_gnn_in["fe2_b"],
        "L0_gnn_A": _L0_gnn_in["A"],
        "L0_gnn_D": _L0_gnn_in["D"],
        "L0_gnn_g1_w": _L0_gnn_in["g1_w"],
        "L0_gnn_g1_b": _L0_gnn_in["g1_b"],
        "L0_gnn_g_ln_g": _L0_gnn_in["g_ln_g"],
        "L0_gnn_g_ln_b": _L0_gnn_in["g_ln_b"],
        "L0_gnn_g2_w": _L0_gnn_in["g2_w"],
        "L0_gnn_g2_b": _L0_gnn_in["g2_b"],
        "L0_gnn_ln_g": _L0_gnn_in["ln_g"],
        "L0_gnn_ln_b": _L0_gnn_in["ln_b"],
    }

def reference(x, adj, L0_gnn_W, L0_gnn_a_src, L0_gnn_a_dst, L0_gnn_W_bcdt, L0_gnn_b_bcdt, L0_gnn_abp_w, L0_gnn_abp_b, L0_gnn_cp_w, L0_gnn_cp_b, L0_gnn_W_hz, L0_gnn_b_hz, L0_gnn_out_w, L0_gnn_out_b, L0_gnn_fe1_w, L0_gnn_fe1_b, L0_gnn_fe_ln_g, L0_gnn_fe_ln_b, L0_gnn_fe2_w, L0_gnn_fe2_b, L0_gnn_A, L0_gnn_D, L0_gnn_g1_w, L0_gnn_g1_b, L0_gnn_g_ln_g, L0_gnn_g_ln_b, L0_gnn_g2_w, L0_gnn_g2_b, L0_gnn_ln_g, L0_gnn_ln_b):
    import jax
    import jax.numpy as jnp
    def _L0_gnn_ref(h, adj, W, a_src, a_dst, W_bcdt, b_bcdt, abp_w, abp_b, cp_w, cp_b, W_hz, b_hz, out_w, out_b, fe1_w, fe1_b, fe_ln_g, fe_ln_b, fe2_w, fe2_b, A, D, g1_w, g1_b, g_ln_g, g_ln_b, g2_w, g2_b, ln_g, ln_b):
        import jax, jax.numpy as jnp
        import numpy as np
        N = 8192
        F_IN = 256
        F_OUT = 256
        S = 128
        D_INNER = 512

        def _ln(x, g, b, eps=1e-05):
            m = x.mean(-1, keepdims=True)
            v = ((x - m) ** 2).mean(-1, keepdims=True)
            return (x - m) / jnp.sqrt(v + eps) * g + b
        Wh = h @ W
        e = Wh @ a_src + (Wh @ a_dst).T
        e = jnp.where(e > 0, e, 0.2 * e)
        e = jnp.where(adj > 0, e, jnp.float32(-9000000000000000.0))
        attn = jax.nn.softmax(e, axis=1)
        h_attn = attn @ Wh
        h_enh = jax.nn.silu(_ln(Wh @ fe1_w + fe1_b, fe_ln_g, fe_ln_b)) @ fe2_w + fe2_b
        BCdt = Wh @ W_bcdt + b_bcdt
        B, C, dt = jnp.split(BCdt, 3, axis=1)
        Asm = jax.nn.softmax(dt + A[None, :], axis=1)
        ab = Asm * B @ abp_w + abp_b
        hs = Wh * ab
        hz = hs @ W_hz + b_hz
        h_part, z = jnp.split(hz, 2, axis=1)
        hs = (h_part * jax.nn.silu(z) + h_part * D) @ out_w + out_b
        c_proj = C @ cp_w + cp_b
        hs = hs * (1.0 + c_proj)
        comb = jnp.concatenate([h_attn, hs], axis=1)
        g = jax.nn.sigmoid(jax.nn.silu(_ln(comb @ g1_w + g1_b, g_ln_g, g_ln_b)) @ g2_w + g2_b)
        fused = g * h_attn + (1.0 - g) * hs + h_enh
        return _ln(fused, ln_g, ln_b)

    x = _layernorm(x + _L0_gnn_ref(x, adj, L0_gnn_W, L0_gnn_a_src, L0_gnn_a_dst, L0_gnn_W_bcdt, L0_gnn_b_bcdt, L0_gnn_abp_w, L0_gnn_abp_b, L0_gnn_cp_w, L0_gnn_cp_b, L0_gnn_W_hz, L0_gnn_b_hz, L0_gnn_out_w, L0_gnn_out_b, L0_gnn_fe1_w, L0_gnn_fe1_b, L0_gnn_fe_ln_g, L0_gnn_fe_ln_b, L0_gnn_fe2_w, L0_gnn_fe2_b, L0_gnn_A, L0_gnn_D, L0_gnn_g1_w, L0_gnn_g1_b, L0_gnn_g_ln_g, L0_gnn_g_ln_b, L0_gnn_g2_w, L0_gnn_g2_b, L0_gnn_ln_g, L0_gnn_ln_b), axis=-1)
    return x


_drawn_inputs = setup_inputs


def setup_inputs(seed=0):
    import zlib

    import numpy as np

    out = dict(_drawn_inputs(seed))
    spreads = {'L0_gnn_b_bcdt': (0.0, 0.647),
     'L0_gnn_abp_b': (0.0, 0.46),
     'L0_gnn_b_hz': (0.0, 0.308),
     'L0_gnn_out_b': (0.0, 0.333),
     'L0_gnn_fe1_b': (0.0, 0.1),
     'L0_gnn_fe_ln_g': (1.0, 0.2),
     'L0_gnn_fe_ln_b': (0.0, 0.1),
     'L0_gnn_fe2_b': (0.0, 0.1),
     'L0_gnn_g1_b': (0.0, 0.418),
     'L0_gnn_g_ln_g': (1.0, 0.6),
     'L0_gnn_g_ln_b': (0.0, 2.0),
     'L0_gnn_g2_b': (0.0, 0.8),
     'L0_gnn_ln_g': (1.0, 0.2),
     'L0_gnn_ln_b': (0.0, 0.1)}
    factors = {'L0_gnn_a_src': 3.551, 'L0_gnn_abp_w': 8.0, 'L0_gnn_A': 8.0, 'L0_gnn_g1_w': 2.711}
    for name, (base, spread) in spreads.items():
        noise = np.random.default_rng([zlib.crc32(name.encode()), seed]).standard_normal(out[name].shape)
        drawn = base * np.exp(spread * noise) if base else spread * noise
        out[name] = jnp.asarray(drawn.astype(out[name].dtype))
    for name, factor in factors.items():
        out[name] = (out[name] * factor).astype(out[name].dtype)
    return out
```

```python
from contextlib import ExitStack

import concourse.bass as bass
from concourse import mybir

F32 = mybir.dt.float32
F32R = mybir.dt.float32r
BF16 = mybir.dt.bfloat16
I32 = mybir.dt.int32
ALU = mybir.AluOpType
ACT = mybir.ActivationFunctionType
AX = mybir.AxisListType
RED = bass.bass_isa.ReduceOp

P = 128
SLOPE = 0.2
EPS = 1e-5
RANGE_MAX = 64.0
STRIPS = 4
ROWS = STRIPS * P
CHUNK = 4


def build(nc, x, adj, w, out):
    N, F = x.shape
    TILES = N // P
    GROUPS = N // ROWS
    FK = F // P
    FE = F + 2
    NCH = TILES // CHUNK
    with ExitStack() as ctx:
        dims = dict(N=N, F=F, TILES=TILES, GROUPS=GROUPS, FK=FK, FE=FE, NCH=NCH)
        wh_rows = nc.dram_tensor("wh_rows", [N, FE], F32, kind="Internal").ap()
        att_rows = nc.dram_tensor("att_rows", [N, FE], F32, kind="Internal").ap()
        r_row = nc.dram_tensor("r_row", [N], F32, kind="Internal").ap()
        dsh_row = nc.dram_tensor("dsh_row", [N], F32, kind="Internal").ap()

        def sb(name, shape, dt=F32):
            return ctx.enter_context(nc.sbuf_tensor(name, shape, dt))

        keep = dict(
            ident=sb("ident", [P, P]), identb=sb("identb", [P, P], BF16),
            s=sb("s_all", [P, TILES]), d=sb("d_all", [P, TILES]),
            q=sb("q_all", [P, TILES]), f=sb("f_all", [P, TILES]),
            ext=sb("ext", [P, 2]), flag=sb("flag", [P, 1], I32), whsum=sb("whsum", [P, F]),
        )
        project(nc, dims, x, w, keep, wh_rows, r_row, dsh_row)
        attend(nc, dims, adj, keep, wh_rows, att_rows, r_row, dsh_row)
        fuse(nc, dims, x, w, keep, wh_rows, att_rows, out)


def clear(nc, sems):
    with nc.Block() as block:
        @block.sync
        def _(sp):
            for s in sems:
                sp.sem_clear(s)


def project(nc, dims, x, w, keep, wh_rows, r_row, dsh_row):
    F, TILES, FK, FE = dims["F"], dims["TILES"], dims["FK"], dims["FE"]
    SLOTS = 2
    ident, identb, s_all, d_all = keep["ident"], keep["identb"], keep["s"], keep["d"]
    q_all, f_all, ext, flag, whsum = keep["q"], keep["f"], keep["ext"], keep["flag"], keep["whsum"]
    with ExitStack() as ctx:
        def sb(name, shape, dt=F32):
            return ctx.enter_context(nc.sbuf_tensor(name, shape, dt))

        sems = []

        def sem(name):
            sems.append(ctx.enter_context(nc.semaphore(name)))
            return sems[-1]

        w_sb = sb("w_sb", [P, FK, F])
        a_bc = sb("a_bc", [P, 2, F])
        xin = sb("xin", [P, SLOTS, F])
        xt = sb("xt", [P, SLOTS, FK, P])
        wh = sb("wh", [P, SLOTS, FE])
        junk = sb("junk", [P, SLOTS, 2, F])
        wsum = sb("wsum", [P, F])
        ones = sb("ones", [P, P])
        loc = sb("loc", [P, 3])
        bias = sb("bias", [P, 2])
        rarg = sb("rarg", [P, 2, TILES])
        rd = sb("rd", [P, 2, TILES])
        rdt = sb("rdt", [P, P])
        rng = sb("rng", [P, 1])
        ps_x = ctx.enter_context(nc.psum_tensor("ps_x", [P, SLOTS, 512], F32))
        ps_w = ctx.enter_context(nc.psum_tensor("ps_w", [P, SLOTS, 512], F32))
        ps_r = ctx.enter_context(nc.psum_tensor("ps_r", [P, 512], F32))
        ps_s = ctx.enter_context(nc.psum_tensor("ps_s", [P, 512], F32))

        weights_in = sem("pr_weights_in")
        x_in = [sem(f"pr_x_in{k}") for k in range(SLOTS)]
        cleared = sem("pr_cleared")
        ident_ready = sem("pr_ident_ready")
        x_turned = sem("pr_x_turned")
        xt_ready = sem("pr_xt_ready")
        wh_made = sem("pr_wh_made")
        wh_ready = sem("pr_wh_ready")
        sd_done = sem("pr_sd_done")
        sum_done = sem("pr_sum_done")
        wh_stored = [sem(f"pr_wh_stored{k}") for k in range(SLOTS)]
        stat = sem("pr_stat")
        ext_ready = sem("pr_ext_ready")
        bias_ready = sem("pr_bias_ready")
        rarg_ready = sem("pr_rarg_ready")
        exp_done = sem("pr_exp_done")
        rd_turned = sem("pr_rd_turned")
        sum_spread = sem("pr_sum_spread")
        rdt_ready = sem("pr_rdt_ready")
        r_stored = sem("pr_r_stored")

        with nc.Block() as block:
            @block.sync
            def _(sp):
                sp.dma_start(w_sb[:, :, :], w["W"].rearrange("(k p) n -> p k n", p=P)).then_inc(weights_in, 16)
                sp.dma_start(a_bc[:, 0, :], w["a_src"].rearrange("f o -> (f o)").partition_broadcast(P)).then_inc(weights_in, 16)
                sp.dma_start(a_bc[:, 1, :], w["a_dst"].rearrange("f o -> (f o)").partition_broadcast(P)).then_inc(weights_in, 16)
                for k in range(SLOTS):
                    sp.dma_start(xin[:, k, :], x[k * P:(k + 1) * P, :]).then_inc(x_in[k], 16)
                def store(i, k):
                    sp.wait_ge(wh_ready, i * SLOTS + k + 1 + SLOTS)
                    sp.dma_start(wh_rows[bass.ds((i * SLOTS + k) * P, P), :], wh[:, k, :]).then_inc(wh_stored[k], 16)

                with sp.Fori(1, TILES // SLOTS) as i:
                    for k in range(SLOTS):
                        sp.wait_ge(x_turned, (i - 1) * SLOTS + k + 1)
                        sp.dma_start(xin[:, k, :], x[bass.ds((i * SLOTS + k) * P, P), :]).then_inc(x_in[k], 16)
                    for k in range(SLOTS):
                        store(i - 1, k)
                for k in range(SLOTS):
                    store(TILES // SLOTS - 1, k)
                for k in range(SLOTS):
                    sp.wait_ge(wh_stored[k], 16 * (TILES // SLOTS + 1))
                sp.wait_ge(rdt_ready, 1)
                sp.dma_start(r_row.rearrange("(t p) -> t p", p=P), rdt[0:TILES, :]).then_inc(r_stored, 16)
                sp.dma_start(dsh_row.rearrange("(t p) -> t p", p=P), rdt[TILES:2 * TILES, :]).then_inc(r_stored, 16)
                sp.wait_ge(r_stored, 32)

            @block.gpsimd
            def _(pool):
                pool.sem_inc(sum_done, SLOTS)
                nc.gpsimd.memset(ident[:, :], 0.0).then_inc(cleared, 1)
                nc.gpsimd.memset(identb[:, :], 0.0).then_inc(cleared, 1)
                nc.gpsimd.memset(wh[:, :, F:F + 1], 1.0).then_inc(cleared, 1)
                nc.gpsimd.memset(wh[:, :, F + 1:F + 2], 0.0).then_inc(cleared, 1)
                nc.gpsimd.memset(wsum[:, :], 0.0).then_inc(cleared, 1)
                nc.gpsimd.memset(ones[:, :], 1.0).then_inc(cleared, 1)
                pool.wait_ge(cleared, 6)
                for t in (ident, identb):
                    nc.gpsimd.affine_select(out=t[:, :], in_=t[:, :], compare_op=ALU.not_equal, fill=1.0,
                                            base=0, pattern=[[-1, P]], channel_multiplier=1).then_inc(ident_ready, 1)
                with pool.Fori(0, TILES // SLOTS) as i:
                    for k in range(SLOTS):
                        pool.wait_ge(wh_ready, i * SLOTS + k + 1 + SLOTS)
                        pool.wait_ge(sum_done, i * SLOTS + k + SLOTS)
                        nc.gpsimd.tensor_tensor(wsum[:, :], wsum[:, :], wh[:, k, 0:F], ALU.add).then_inc(sum_done, 1)
                pool.wait_ge(stat, 3)
                nc.gpsimd.partition_all_reduce(ext[:, :], loc[:, 0:2], P, RED.max).then_inc(ext_ready, 1)

            @block.tensor
            def _(pe):
                pe.wait_ge(ident_ready, 2)
                pe.wait_ge(weights_in, 48)
                with pe.Fori(0, TILES // SLOTS) as i:
                    for k in range(SLOTS):
                        pe.wait_ge(x_in[k], i * 16 + 16)
                        for c in range(FK):
                            last = nc.tensor.transpose(ps_x[:, k, c * P:(c + 1) * P], xin[:, k, c * P:(c + 1) * P], ident[:, :])
                        last.then_inc(x_turned, 1)
                    for k in range(SLOTS):
                        pe.wait_ge(xt_ready, i * SLOTS + k + 1)
                        pe.wait_ge(wh_ready, i * SLOTS + k + 1)
                        for c in range(FK):
                            last = nc.tensor.matmul(ps_w[:, k, 0:F], xt[:, k, c, :], w_sb[:, c, :],
                                                    start=(c == 0), stop=(c == FK - 1))
                        last.then_inc(wh_made, 1)
                pe.wait_ge(exp_done, 1)
                pe.wait_ge(rarg_ready, 2)
                nc.tensor.transpose(ps_r[:, 0:P], rd[:, :, :].rearrange("p a t -> p (a t)"), ident[:, :]).then_inc(rd_turned, 1)
                pe.wait_ge(sum_done, TILES + SLOTS)
                nc.tensor.matmul(ps_s[:, 0:F], ones[:, :], wsum[:, :], start=True, stop=True).then_inc(sum_spread, 1)

            @block.scalar
            def _(act):
                act.sem_inc(wh_ready, SLOTS)
                for k in range(SLOTS):
                    act.sem_inc(wh_stored[k], 16)
                act.wait_ge(cleared, 6)
                with act.Fori(0, TILES // SLOTS) as i:
                    for k in range(SLOTS):
                        act.wait_ge(x_turned, i * SLOTS + k + 1)
                        nc.scalar.copy(xt[:, k, :, :].rearrange("p c n -> p (c n)"), ps_x[:, k, 0:F]).then_inc(xt_ready, 1)
                    for k in range(SLOTS):
                        act.wait_ge(wh_made, i * SLOTS + k + 1)
                        act.wait_ge(wh_stored[k], i * 16 + 16)
                        act.wait_ge(sd_done, i * SLOTS + k + 1)
                        act.wait_ge(sum_done, i * SLOTS + k + 1)
                        nc.scalar.copy(wh[:, k, 0:F], ps_w[:, k, 0:F]).then_inc(wh_ready, 1)
                act.wait_ge(bias_ready, 2)
                act.wait_ge(rarg_ready, 1)
                nc.scalar.activation(rd[:, 0, :], rarg[:, 1, :], ACT.Exp).then_inc(exp_done, 1)
                nc.scalar.activation(q_all[:, :], d_all[:, :], ACT.Exp, bias=bias[:, 0:1], scale=1.0 - SLOPE).then_inc(exp_done, 1)
                nc.scalar.activation(f_all[:, :], d_all[:, :], ACT.Exp, bias=bias[:, 1:2], scale=SLOPE).then_inc(exp_done, 1)

            @block.vector
            def _(dve):
                dve.sem_inc(sd_done, SLOTS)
                dve.wait_ge(weights_in, 48)
                with dve.Fori(0, TILES // SLOTS) as i:
                    for k in range(SLOTS):
                        dve.wait_ge(wh_ready, i * SLOTS + k + 1 + SLOTS)
                        dve.wait_ge(sd_done, i * SLOTS + k + 1)
                        for a, dst in enumerate((s_all, d_all)):
                            last = nc.vector.scalar_tensor_tensor(
                                out=junk[:, k, a, :], in0=wh[:, k, 0:F], scalar=1.0, in1=a_bc[:, a, :],
                                op0=ALU.mult, op1=ALU.mult, accum_out=dst[:, bass.ds(i * SLOTS + k, 1)])
                        last.then_inc(sd_done, 1)
                dve.wait_ge(sd_done, TILES + SLOTS)
                nc.vector.tensor_reduce(loc[:, 0:1], d_all[:, :], AX.X, ALU.max).then_inc(stat, 1)
                nc.vector.tensor_reduce(loc[:, 2:3], d_all[:, :], AX.X, ALU.min).then_inc(stat, 1)
                dve.wait_ge(stat, 2)
                nc.vector.tensor_scalar(loc[:, 1:2], loc[:, 2:3], -1.0, None, ALU.mult).then_inc(stat, 1)
                dve.wait_ge(ext_ready, 1)
                nc.vector.tensor_scalar(bias[:, 0:1], ext[:, 0:1], SLOPE - 1.0, None, ALU.mult).then_inc(bias_ready, 1)
                nc.vector.tensor_scalar(bias[:, 1:2], ext[:, 0:1], -SLOPE, None, ALU.mult).then_inc(bias_ready, 1)
                nc.vector.tensor_tensor(rng[:, :], ext[:, 0:1], ext[:, 1:2], ALU.add).then_inc(bias_ready, 1)
                dve.wait_ge(bias_ready, 3)
                nc.vector.tensor_scalar(flag[:, :], rng[:, :], RANGE_MAX, None, ALU.is_le).then_inc(stat, 1)
                nc.vector.tensor_scalar(rarg[:, 0, :], s_all[:, :], SLOPE - 1.0, bias[:, 0:1], ALU.mult, ALU.add).then_inc(stat, 1)
                dve.wait_ge(stat, 5)
                nc.vector.tensor_scalar(rarg[:, 1, :], rarg[:, 0, :], 0.0, None, ALU.min).then_inc(rarg_ready, 1)
                nc.vector.tensor_scalar(rd[:, 1, :], d_all[:, :], ext[:, 1:2], None, ALU.add).then_inc(rarg_ready, 1)
                dve.wait_ge(rd_turned, 1)
                nc.vector.tensor_copy(rdt[:, :], ps_r[:, 0:P]).then_inc(rdt_ready, 1)
                dve.wait_ge(sum_spread, 1)
                nc.vector.tensor_copy(whsum[:, :], ps_s[:, 0:F]).then_inc(stat, 1)
        clear(nc, sems)


def attend(nc, dims, adj, keep, wh_rows, att_rows, r_row, dsh_row):
    F, TILES, GROUPS, FE, NCH = (dims[k] for k in ("F", "TILES", "GROUPS", "FE", "NCH"))
    W = CHUNK * P
    LOADS = 4
    MASKS = 2
    QS = CHUNK
    SPLITS = CHUNK
    identb, ident = keep["identb"], keep["ident"]
    q_all, f_all, flag = keep["q"], keep["f"], keep["flag"]
    with ExitStack() as ctx:
        def sb(name, shape, dt=F32):
            return ctx.enter_context(nc.sbuf_tensor(name, shape, dt))

        sems = []

        def sem(name):
            sems.append(ctx.enter_context(nc.semaphore(name)))
            return sems[-1]

        g_hi = sb("g_hi", [P, TILES, FE], F32R)
        g_lo = sb("g_lo", [P, TILES, FE], F32R)
        adj_sb = sb("adj_sb", [P, LOADS, STRIPS, W], I32)
        mask = sb("mask", [P, MASKS, STRIPS, W], BF16)
        r_bc = sb("r_bc", [P, 2, ROWS])
        qm = sb("qm", [P, QS, ROWS])
        q_hi = sb("q_hi", [P, SPLITS, ROWS], F32R)
        q_lo = sb("q_lo", [P, SPLITS, ROWS], F32R)
        stage = sb("stage", [P, STRIPS, FE])
        acc = ctx.enter_context(nc.psum_tensor("acc", [P, STRIPS, 512], F32))
        turned = ctx.enter_context(nc.psum_tensor("turned", [P, CHUNK, 1024], BF16))

        split_parts(nc, dims, keep, wh_rows, g_hi, g_lo, adj_sb)

        r_in = sem("at_r_in")
        adj_in = [sem(f"at_adj_in{k}") for k in range(LOADS)]
        mask_ready = sem("at_mask_ready")
        mask_begun = sem("at_mask_begun")
        turn_done = sem("at_turn_done")
        q_made = sem("at_q_made")
        hi_ready = sem("at_hi_ready")
        lo_ready = sem("at_lo_ready")
        split_free = sem("at_split_free")
        acc_ready = sem("at_acc_ready")
        acc_free = sem("at_acc_free")
        stage_ready = sem("at_stage_ready")
        stage_stored = sem("at_stage_stored")

        adj_v = adj.rearrange("(g s p) j -> g p s j", s=STRIPS, p=P)
        att_v = att_rows.rearrange("(g s p) c -> g s p c", s=STRIPS, p=P)
        LAST_TILE = GROUPS * TILES
        slow = slow_path(nc, dims, adj, keep, wh_rows, att_rows, dsh_row, sem, sb,
                         dict(adj=adj_sb, mask=mask, r_bc=r_bc, qm=qm, stage=stage), acc, turned)

        with nc.Block() as block:
            @block.sync
            def _(sp):
                def load(g, c, k):
                    sp.dma_start(adj_sb[:, k, :, :],
                                 adj_v[bass.ds(g, 1), :, :, bass.ds(c * W, W)].rearrange("g p s j -> (g p) s j")
                                 ).then_inc(adj_in[k], 16)

                def load_r(g, slot):
                    sp.dma_start(r_bc[:, slot, :], r_row[bass.ds(g * ROWS, ROWS)].partition_broadcast(P)).then_inc(r_in, 16)

                fast = sp.value_load(flag[0:1, 0:1], min_val=0, max_val=1)
                with sp.If(fast == 1):
                    load_r(0, 0)
                    for k in range(LOADS):
                        load(0, k, k)
                    with sp.Fori(1, NCH // LOADS) as b:
                        for k in range(LOADS):
                            sp.wait_ge(mask_ready, b * LOADS + (k + 1 - LOADS))
                            load(0, b * LOADS + k, k)
                    with sp.Fori(1, GROUPS) as g:
                        sp.wait_ge(q_made, (g - 1) * TILES + CHUNK)
                        sp.dma_start(r_bc[:, bass.ds(g % 2, 1), :],
                                     r_row[bass.ds(g * ROWS, ROWS)].partition_broadcast(P)).then_inc(r_in, 16)
                        with sp.Fori(0, NCH // LOADS) as b:
                            for k in range(LOADS):
                                sp.wait_ge(mask_ready, g * NCH + b * LOADS + (k + 1 - LOADS))
                                load(g, b * LOADS + k, k)
                with sp.Else():
                    slow["sync"](sp)

            @block.gpsimd
            def _(pool):
                fast = pool.value_load(flag[0:1, 0:1], min_val=0, max_val=1)
                with pool.If(fast == 1):
                    with pool.Fori(0, GROUPS * NCH // LOADS) as b:
                        for k in range(LOADS):
                            pool.wait_ge(adj_in[k], b * 16 + 16)
                            pool.wait_ge(turn_done, (b * LOADS + k + 1) * CHUNK)
                            pool.sem_inc(mask_begun, 1)
                            nc.gpsimd.tensor_scalar(mask[:, k % MASKS, :, :].rearrange("p s j -> p (s j)"),
                                                    adj_sb[:, k, :, :].rearrange("p s j -> p (s j)"),
                                                    0.0, None, ALU.is_gt).then_inc(mask_ready, 1)
                    nc.gpsimd.drain().then_inc(mask_ready, 1)
                with pool.Else():
                    slow["pool"](pool)

            @block.tensor
            def _(pe):
                def turn(n, m, k):
                    if k == 0:
                        pe.wait_ge(mask_ready, n + 1)
                    pe.wait_ge(q_made, n * CHUNK + k + 1)
                    for s in range(STRIPS):
                        last = nc.tensor.transpose(turned[:, k, s * P:(s + 1) * P], mask[:, m, s, k * P:(k + 1) * P], identb[:, :])
                    last.then_inc(turn_done, 1)

                def products(n, c, g, k, first=False, final=False):
                    j = c * CHUNK + k
                    t = n * CHUNK + k
                    pe.wait_ge(hi_ready, t + 1)
                    for s in range(STRIPS):
                        if first:
                            pe.wait_ge(acc_free, g * STRIPS + s + 1)
                        cols = slice(s * P, (s + 1) * P)
                        nc.tensor.matmul(acc[:, s, 0:FE], q_hi[:, k, cols], g_hi[:, bass.ds(j, 1), :].rearrange("p a f -> p (a f)"),
                                         start=first, stop=False)
                        nc.tensor.matmul(acc[:, s, 0:FE], q_hi[:, k, cols], g_lo[:, bass.ds(j, 1), :].rearrange("p a f -> p (a f)"),
                                         start=False, stop=False)
                    pe.wait_ge(lo_ready, t + 1 + QS)
                    for s in range(STRIPS):
                        cols = slice(s * P, (s + 1) * P)
                        last = nc.tensor.matmul(acc[:, s, 0:FE], q_lo[:, k, cols], g_hi[:, bass.ds(j, 1), :].rearrange("p a f -> p (a f)"),
                                                start=False, stop=final)
                    last.then_inc(split_free, 1)

                def pair(g, c, first=False, final=False):
                    for m in range(2):
                        for k in range(CHUNK):
                            turn(g * NCH + c + (m + 1), (m + 1) % MASKS, k)
                            products(g * NCH + c + m, c + m, g, k, first=first and m == 0 and k == 0,
                                     final=final and m == 1 and k == CHUNK - 1)

                fast = pe.value_load(flag[0:1, 0:1], min_val=0, max_val=1)
                with pe.If(fast == 1):
                    pe.sem_inc(turn_done, MASKS * CHUNK)
                    pe.sem_inc(split_free, SPLITS)
                    for k in range(CHUNK):
                        turn(0, 0, k)
                    with pe.Fori(0, GROUPS) as g:
                        pair(g, 0, first=True)
                        with pe.Fori(1, NCH // 2 - 1) as b:
                            pair(g, b * 2)
                        pair(g, NCH - 2, final=True)
                with pe.Else():
                    slow["tensor"](pe)

            @block.vector
            def _(dve):
                BODY = 2 * CHUNK

                def mul_mask(t, j, slot, k):
                    dve.wait_ge(turn_done, t + 1 + MASKS * CHUNK)
                    dve.wait_ge(lo_ready, t + 1)
                    nc.vector.scalar_tensor_tensor(
                        out=qm[:, k % QS, :], in0=r_bc[:, slot, :], scalar=q_all[:, bass.ds(j, 1)],
                        in1=turned[:, k % CHUNK, 0:ROWS], op0=ALU.max, op1=ALU.mult).then_inc(q_made, 1)

                def low_part(t, k):
                    dve.wait_ge(hi_ready, t + 1)
                    dve.wait_ge(split_free, t + 1)
                    nc.vector.tensor_tensor(q_lo[:, k % SPLITS, :], qm[:, k % QS, :], q_hi[:, k % SPLITS, :].bitcast(F32),
                                            ALU.subtract).then_inc(lo_ready, 1)

                fast = dve.value_load(flag[0:1, 0:1], min_val=0, max_val=1)
                with dve.If(fast == 1):
                    dve.sem_inc(q_made, CHUNK)
                    dve.sem_inc(lo_ready, QS)
                    with dve.Fori(0, GROUPS // 2) as gg:
                        for slot in range(2):
                            with dve.Fori(0, TILES // BODY) as b:
                                dve.wait_ge(r_in, gg * 32 + 16 * (slot + 1))
                                base = gg * (2 * TILES) + slot * TILES + b * BODY
                                for k in range(BODY):
                                    mul_mask(base + k, b * BODY + k, slot, k)
                                    if k >= 1:
                                        low_part(base + (k - 1), k - 1)
                                low_part(base + (BODY - 1), BODY - 1)
                with dve.Else():
                    slow["vector"](dve)

            @block.scalar
            def _(act):
                BODY = 2 * CHUNK

                def high_part(t, k):
                    act.wait_ge(q_made, t + 1 + CHUNK)
                    act.wait_ge(split_free, t + 1)
                    nc.scalar.copy(q_hi[:, k % SPLITS, :], qm[:, k % QS, :]).then_inc(hi_ready, 1)

                def evacuate(g):
                    for s in range(STRIPS):
                        if s == 0:
                            act.wait_ge(stage_stored, (g + 1) * (16 * STRIPS))
                            act.wait_ge(split_free, (g + 1) * TILES + SPLITS)
                        nc.scalar.copy(stage[:, s, :], acc[:, s, 0:FE]).then_inc(acc_free, 1)
                    for s in range(STRIPS):
                        act.wait_ge(acc_free, g * STRIPS + s + 1 + STRIPS)
                        act.dma_start(att_v[bass.ds(g, 1), s, :, :].rearrange("g p c -> (g p) c"), stage[:, s, :]).then_inc(stage_stored, 16)

                def body(base, g_out=None):
                    for k in range(BODY):
                        high_part(base + k, k)
                        if g_out is not None and k == 3:
                            evacuate(g_out)

                fast = act.value_load(flag[0:1, 0:1], min_val=0, max_val=1)
                with act.If(fast == 1):
                    act.sem_inc(acc_free, STRIPS)
                    act.sem_inc(stage_stored, 16 * STRIPS)
                    for k in range(BODY):
                        high_part(k, k)
                    with act.Fori(0, GROUPS - 1) as g:
                        with act.Fori(1, TILES // BODY) as b:
                            body(g * TILES + b * BODY)
                        body(g * TILES + TILES, g_out=g)
                    with act.Fori(1, TILES // BODY) as b:
                        body((GROUPS - 1) * TILES + b * BODY)
                    evacuate(GROUPS - 1)
                    act.wait_ge(stage_stored, 16 * STRIPS * (GROUPS + 1))
                with act.Else():
                    slow["scalar"](act)
        clear(nc, sems)


def split_parts(nc, dims, keep, wh_rows, g_hi, g_lo, adj_sb):
    TILES, FE = dims["TILES"], dims["FE"]
    f_all = keep["f"]
    SLOTS, PER = 2, 4
    with ExitStack() as ctx:
        sems = []

        def sem(name):
            sems.append(ctx.enter_context(nc.semaphore(name)))
            return sems[-1]

        def slot(k):
            return adj_sb[:, k, :, :].rearrange("p s j -> p (s j)").bitcast(F32)[:, 0:PER * FE].rearrange("p (t f) -> p t f", t=PER)

        rows_in = [sem(f"sp_rows_in{k}") for k in range(SLOTS)]
        hi_made = sem("sp_hi_made")
        lo_made = sem("sp_lo_made")
        wh_v = wh_rows.rearrange("(b t p) f -> b p t f", t=PER, p=P)
        STEPS = TILES // PER // SLOTS
        with nc.Block() as block:
            @block.sync
            def _(sp):
                for k in range(SLOTS):
                    sp.dma_start(slot(k), wh_v[k]).then_inc(rows_in[k], 16)
                with sp.Fori(1, STEPS) as i:
                    for k in range(SLOTS):
                        sp.wait_ge(lo_made, (i - 1) * (SLOTS * PER) + (k + 1) * PER)
                        sp.dma_start(slot(k), wh_v[bass.ds(i * SLOTS + k, 1)].rearrange("b p t f -> (b p) t f")).then_inc(rows_in[k], 16)

            @block.scalar
            def _(act):
                with act.Fori(0, STEPS) as i:
                    for k in range(SLOTS):
                        act.wait_ge(rows_in[k], i * 16 + 16)
                        for t in range(PER):
                            tile = i * (SLOTS * PER) + (k * PER + t)
                            nc.scalar.activation(g_hi[:, bass.ds(tile, 1), :].rearrange("p a f -> p (a f)"), slot(k)[:, t, :], ACT.Copy,
                                                 scale=f_all[:, bass.ds(tile, 1)]).then_inc(hi_made, 1)

            @block.vector
            def _(dve):
                with dve.Fori(0, STEPS) as i:
                    for k in range(SLOTS):
                        for t in range(PER):
                            tile = i * (SLOTS * PER) + (k * PER + t)
                            dve.wait_ge(hi_made, tile + 1)
                            nc.vector.scalar_tensor_tensor(
                                out=g_lo[:, bass.ds(tile, 1), :].rearrange("p a f -> p (a f)"), in0=slot(k)[:, t, :],
                                scalar=f_all[:, bass.ds(tile, 1)],
                                in1=g_hi[:, bass.ds(tile, 1), :].rearrange("p a f -> p (a f)").bitcast(F32),
                                op0=ALU.mult, op1=ALU.subtract).then_inc(lo_made, 1)


def slow_path(nc, dims, adj, keep, wh_rows, att_rows, dsh_row, sem, sb, buf, acc, turned):
    F, TILES, FE = dims["F"], dims["TILES"], dims["FE"]
    W = CHUNK * P
    C = dims["N"] // W
    ident, s_all, ext = keep["ident"], keep["s"], keep["ext"]
    nbr = buf["adj"][:, 0, 0, :]
    whc = buf["adj"][:, 1, :, :].rearrange("p s j -> p (s j)").bitcast(F32)[:, 0:CHUNK * FE].rearrange("p (k f) -> p k f", k=CHUNK)
    dsh, wt = buf["r_bc"][:, 0, :], buf["r_bc"][:, 1, :]
    picked, z, lz, ex = (buf["qm"][:, i, :] for i in range(4))
    total = buf["stage"][:, 0, :]
    ps_t = turned[:, 0, :].bitcast(F32)
    mx = sb("sl_mx", [P, C])
    row = sb("sl_row", [P, 6])

    in1, in2, stored = sem("sl_in1"), sem("sl_in2"), sem("sl_stored")
    pick1 = sem("sl_pick1")
    max_done = sem("sl_max_done")
    row_step = sem("sl_row_step")
    z_done, lz_done, ex_done, pick2 = sem("sl_z_done"), sem("sl_lz_done"), sem("sl_ex_done"), sem("sl_pick2")
    turn, wt_done, prod = sem("sl_turn"), sem("sl_wt_done"), sem("sl_prod")
    add_done = sem("sl_add_done")
    zeroed = sem("sl_zeroed")
    settled = sem("sl_settled")

    def sync(sp):
        def load(t, c, signal):
            sp.dma_start(nbr, adj[bass.ds(t * P, P), bass.ds(c * W, W)]).then_inc(signal, 16)
            sp.dma_start(dsh, dsh_row[bass.ds(c * W, W)].partition_broadcast(P)).then_inc(signal, 16)

        with sp.Fori(0, TILES) as t:
            with sp.Fori(0, C) as c:
                sp.wait_ge(max_done, t * C + c + 1)
                sp.sem_inc(settled, 1)
                sp.wait_ge(add_done, t * C + 1)
                sp.sem_inc(settled, 1)
                load(t, c, in1)
            with sp.Fori(0, C) as c:
                sp.wait_ge(max_done, t * C + C + 1)
                sp.sem_inc(settled, 1)
                sp.wait_ge(add_done, t * C + c + 1)
                sp.sem_inc(settled, 1)
                load(t, c, in2)
                sp.dma_start(whc, wh_rows[bass.ds(c * W, W), :].rearrange("(k p) f -> p k f", p=P)).then_inc(in2, 16)
            sp.wait_ge(add_done, t * C + C + 1)
            sp.sem_inc(settled, 1)
            sp.dma_start(att_rows[bass.ds(t * P, P), :], total).then_inc(stored, 16)
        sp.wait_ge(stored, 16 * (TILES + 1))

    def pool(eng):
        eng.sem_inc(stored, 16)
        eng.sem_inc(max_done, 1)
        eng.sem_inc(add_done, 1)
        eng.sem_inc(row_step, 6)

    def tensor(pe):
        with pe.Fori(0, TILES) as t:
            with pe.Fori(0, C) as c:
                n = t * C + c
                pe.wait_ge(pick2, n + 1)
                for k in range(CHUNK):
                    last = nc.tensor.transpose(ps_t[:, k * P:(k + 1) * P], picked[:, k * P:(k + 1) * P], ident[:, :])
                last.then_inc(turn, 1)
                pe.wait_ge(wt_done, n + 1)
                for k in range(CHUNK):
                    last = nc.tensor.matmul(acc[:, 0, 0:FE], wt[:, k * P:(k + 1) * P], whc[:, k, :],
                                            start=(k == 0), stop=(k == CHUNK - 1))
                last.then_inc(prod, 1)

    def scalar(act):
        with act.Fori(0, TILES) as t:
            with act.Fori(0, C) as c:
                act.wait_ge(lz_done, t * C + c + 1)
                nc.scalar.activation(ex, lz, ACT.Exp, bias=row[:, 5:6]).then_inc(ex_done, 1)

    def vector(dve):
        def neighbours(src, signal, count):
            nc.vector.scalar_tensor_tensor(out=picked, in0=nbr, scalar=0.0, in1=src, op0=ALU.is_gt, op1=ALU.mult).then_inc(signal, 1)
            dve.wait_ge(signal, count)

        with dve.Fori(0, TILES) as t:
            with dve.Fori(0, C) as c:
                dve.wait_ge(in1, (t * C + c) * 32 + 32)
                neighbours(dsh, pick1, t * C + c + 1)
                nc.vector.tensor_reduce(mx[:, bass.ds(c, 1)], picked, AX.X, ALU.max).then_inc(max_done, 1)

            def step(i, ins):
                ins.then_inc(row_step, 1)
                dve.wait_ge(row_step, t * 6 + (i + 7))

            dve.wait_ge(max_done, t * C + C + 1)
            step(0, nc.vector.tensor_scalar(row[:, 0:1], s_all[:, bass.ds(t, 1)], ext[:, 1:2], None, ALU.subtract))
            step(1, nc.vector.tensor_reduce(row[:, 1:2], mx[:, :], AX.X, ALU.max))
            step(2, nc.vector.tensor_tensor(row[:, 2:3], row[:, 0:1], row[:, 1:2], ALU.add))
            step(3, nc.vector.tensor_scalar(row[:, 3:4], row[:, 2:3], 1.0, None, ALU.add))
            step(4, nc.vector.scalar_tensor_tensor(out=row[:, 4:5], in0=row[:, 2:3], scalar=SLOPE, in1=row[:, 2:3],
                                                   op0=ALU.mult, op1=ALU.max))
            step(5, nc.vector.tensor_scalar(row[:, 5:6], row[:, 4:5], -1.0, None, ALU.mult))
            dve.wait_ge(stored, t * 16 + 16)
            nc.vector.memset(total, 0.0).then_inc(zeroed, 1)
            with dve.Fori(0, C) as c:
                n = t * C + c
                dve.wait_ge(in2, n * 48 + 48)
                nc.vector.tensor_scalar(z, dsh, row[:, 0:1], row[:, 3:4], ALU.add, ALU.min).then_inc(z_done, 1)
                dve.wait_ge(z_done, n + 1)
                nc.vector.scalar_tensor_tensor(out=lz, in0=z, scalar=SLOPE, in1=z, op0=ALU.mult, op1=ALU.max).then_inc(lz_done, 1)
                dve.wait_ge(ex_done, n + 1)
                neighbours(ex, pick2, n + 1)
                dve.wait_ge(turn, n + 1)
                nc.vector.tensor_copy(wt, ps_t[:, :]).then_inc(wt_done, 1)
                dve.wait_ge(prod, n + 1)
                dve.wait_ge(zeroed, t + 1)
                dve.wait_ge(add_done, n + 1)
                nc.vector.tensor_tensor(total, total, acc[:, 0, 0:FE], ALU.add).then_inc(add_done, 1)

    return dict(sync=sync, pool=pool, tensor=tensor, scalar=scalar, vector=vector)


def fuse(nc, dims, x, w, keep, wh_rows, att_rows, out):
    F, TILES, GROUPS, FE, FK, N = (dims[k] for k in ("F", "TILES", "GROUPS", "FE", "FK", "N"))
    S = w["abp_w"].shape[0]
    DI = w["fe1_w"].shape[1]
    G1 = w["g1_w"].shape[1]
    ident, whsum = keep["ident"], keep["whsum"]
    mats = {n: (w[n], w[n].shape[0] // P, w[n].shape[1])
            for n in ("fe1_w", "W_bcdt", "abp_w", "fe2_w", "W_hz", "out_w", "g1_w", "g2_w")}
    bias_of = {"fe1_w": "fe1_b", "W_bcdt": "b_bcdt", "abp_w": "abp_b", "fe2_w": "fe2_b", "W_hz": "b_hz",
               "out_w": "out_b", "g1_w": "g1_b", "g2_w": "g2_b"}
    bias_at, NB = {}, 0
    for n in mats:
        bias_at[n] = NB
        NB += mats[n][2]
    spread = ("fe_ln_g", "fe_ln_b", "g_ln_g", "g_ln_b", "ln_g", "ln_b")
    LO_ROW = 32

    with ExitStack() as ctx:
        def sb(name, shape, dt=F32):
            return ctx.enter_context(nc.sbuf_tensor(name, shape, dt))

        hi = {n: sb(n + "_hi", [P, k, c], F32R) for n, (_, k, c) in mats.items()}
        lo = {n: sb(n + "_lo", [P, k, c], F32R) for n, (_, k, c) in mats.items()}
        brow = sb("brow", [P, NB], F32R)
        ones = sb("ones_r", [P, P], F32R)
        vec = {n: sb(n + "_bc", [P, w[n].shape[0]]) for n in spread}
        cpw = sb("cpw_bc", [P, S])
        cpb1 = sb("cpb1", [P, 1])
        d2 = sb("d2", [P, 1])
        half = sb("minus_half", [P, 1])
        prepare(nc, w, mats, bias_of, bias_at, NB, LO_ROW, hi, lo, brow, ones, vec, cpw, cpb1, d2, half)

        def rows(name, width, dt=F32):
            return sb(name, [P, STRIPS, width], dt)

        wh, xr, num = rows("wh_in", FE), rows("x_in", F), rows("att_in", FE)
        wht_hi, wht_lo = rows("wht_hi", F, F32R), rows("wht_lo", F, F32R)
        vt_hi, vt_lo = rows("vt_hi", DI, F32R), rows("vt_lo", DI, F32R)
        abt_hi, abt_lo = rows("abt_hi", S, F32R), rows("abt_lo", S, F32R)
        v, th = rows("v", DI), rows("th", DI)
        ab, e = rows("ab", S), rows("e", S)
        hs0 = rows("hs0", F)
        ha, hs, he, fused = rows("ha", F), rows("hs", F), rows("he", F), rows("fused", F)
        tg = rows("tg", F)
        cj = rows("cj", S)
        st = {n: rows("st_" + n, 6) for n in ("fe", "g", "f", "o")}
        mv = {n: rows("mv_" + n, 2) for n in ("fe", "g", "f", "o")}
        ve = {n: rows("ve_" + n, 3) for n in ("fe", "g", "f", "o")}
        sc = rows("sc", 8)
        ps = ctx.enter_context(nc.psum_tensor("ps", [P, 8, 512], F32))

        steps = ["in_wh", "in_x", "in_att",
                 "t_wh", "hi_wh", "lo_wh", "fe1", "fe_st", "fe_mv", "fe_ve", "fe_rs", "fe_nm", "fe_xh", "fe_g", "fe_n", "fe_th", "fe_v",
                 "bc", "mx", "e", "es", "ab", "t_ab", "hi_ab", "lo_ab", "abp", "hs0", "t_fe", "hi_fe", "lo_fe", "fe2", "he",
                 "t_hs0", "hi_hs0", "lo_hs0", "hz_h", "hz_z", "z_th", "w", "u", "t_u", "hi_u", "lo_u", "cd", "c1", "out", "hs",
                 "nn", "ws", "wr", "hn", "ha", "t_co", "hi_co", "lo_co", "g1", "g_st", "g_mv", "g_ve", "g_rs", "g_nm", "g_xh", "g_g", "g_n", "g_th", "g_v",
                 "t_g", "hi_g", "lo_g", "g2", "tg", "dl", "hh", "m", "f", "f_st", "f_mv", "f_ve", "f_rs", "f_nm", "f_xh", "f_g", "f_n", "y",
                 "o_st", "o_mv", "o_ve", "o_rs", "o_nm", "o_out", "settled", "stored"]
        dma_steps = ("in_wh", "in_x", "in_att", "stored")
        sems = {n: ctx.enter_context(nc.semaphore("fu_" + n)) for n in steps if n not in dma_steps}
        for n in dma_steps:
            for s in range(STRIPS):
                sems[n, s] = ctx.enter_context(nc.semaphore(f"fu_{n}{s}"))

        class Strip:
            def __init__(self, eng, g, s):
                self.eng, self.g, self.s = eng, g, s

            def need(self, *names):
                for n in names:
                    if n in dma_steps:
                        self.eng.wait_ge(sems[n, self.s], self.g * 16 + 32)
                    else:
                        self.eng.wait_ge(sems[n], self.g * STRIPS + (self.s + 1 + STRIPS))

            def free(self, *names):
                for n in names:
                    if n in dma_steps:
                        self.eng.wait_ge(sems[n, self.s], self.g * 16 + 16)
                    else:
                        self.eng.wait_ge(sems[n], self.g * STRIPS + (self.s + 1))

            def settle(self):
                self.eng.sem_inc(sems["settled"], 1)

            def done(self, name, ins):
                if name in dma_steps:
                    ins.then_inc(sems[name, self.s], 16)
                else:
                    ins.then_inc(sems[name], 1)

        with nc.Block() as block:
            @block.sync
            def _(sp):
                for n in steps:
                    if n in dma_steps:
                        for s in range(STRIPS):
                            sp.sem_inc(sems[n, s], 16)
                    else:
                        sp.sem_inc(sems[n], STRIPS)

        xg = x.rearrange("(g s p) f -> g s p f", s=STRIPS, p=P)
        whg = wh_rows.rearrange("(g s p) f -> g s p f", s=STRIPS, p=P)
        attg = att_rows.rearrange("(g s p) f -> g s p f", s=STRIPS, p=P)
        outg = out.rearrange("(g s p) f -> g s p f", s=STRIPS, p=P)

        with nc.Block() as block:
            @block.sync
            def _(sp):
                with sp.Fori(0, GROUPS) as g:
                    for s in range(STRIPS):
                        k = Strip(sp, g, s)
                        k.free("hs0", "t_wh")
                        k.done("in_wh", sp.dma_start(wh[:, s, :], whg[bass.ds(g, 1), s].rearrange("g p f -> (g p) f")))
                    for s in range(STRIPS):
                        k = Strip(sp, g, s)
                        k.free("hn", "wr")
                        k.done("in_att", sp.dma_start(num[:, s, :], attg[bass.ds(g, 1), s].rearrange("g p f -> (g p) f")))
                    for s in range(STRIPS):
                        k = Strip(sp, g, s)
                        k.free("y")
                        k.done("in_x", sp.dma_start(xr[:, s, :], xg[bass.ds(g, 1), s].rearrange("g p f -> (g p) f")))

            @block.tensor
            def _(pe):
                place = {n: i for i, n in enumerate(
                    ("t_wh", "fe1", "bc", "t_ab", "abp", "t_fe", "fe2", "t_hs0", "hz_h", "hz_z", "t_u", "out", "t_co", "g1", "t_g", "g2"))}

                def bank(name, s):
                    return ps[:, place[name] % 2 * STRIPS + s, :]

                def turn(k, name, blocks):
                    for i, b in enumerate(blocks):
                        last = nc.tensor.transpose(bank(name, k.s)[:, i * P:(i + 1) * P], b, ident[:, :])
                    k.done(name, last)

                def product(k, name, mat, left_hi, left_lo, c0=0, c1=None):
                    _, nk, nc_ = mats[mat]
                    c1 = nc_ if c1 is None else c1
                    o = bank(name, k.s)[:, 0:c1 - c0]
                    nc.tensor.matmul(o, ones[:, :], brow[:, bias_at[mat] + c0:bias_at[mat] + c1], start=True, stop=False)
                    for i in range(nk):
                        a_hi, a_lo = left_hi[:, k.s, i * P:(i + 1) * P], left_lo[:, k.s, i * P:(i + 1) * P]
                        nc.tensor.matmul(o, a_hi, hi[mat][:, i, c0:c1], start=False, stop=False)
                        nc.tensor.matmul(o, a_hi, lo[mat][:, i, c0:c1], start=False, stop=False)
                        last = nc.tensor.matmul(o, a_lo, hi[mat][:, i, c0:c1], start=False, stop=i == nk - 1)
                    k.done(name, last)

                with pe.Fori(0, GROUPS) as g:
                    strips = [Strip(pe, g, s) for s in range(STRIPS)]
                    for k in strips:
                        k.need("in_wh")
                        k.free("lo_g")
                        turn(k, "t_wh", [wh[:, k.s, i * P:(i + 1) * P] for i in range(FK)])
                    for k in strips:
                        k.need("lo_wh")
                        k.free("tg")
                        product(k, "fe1", "fe1_w", wht_hi, wht_lo)
                    for k in strips:
                        product(k, "bc", "W_bcdt", wht_hi, wht_lo)
                    for k in strips:
                        k.need("ab", "fe_xh")
                        turn(k, "t_ab", [ab[:, k.s, :]])
                    for k in strips:
                        k.need("lo_ab")
                        product(k, "abp", "abp_w", abt_hi, abt_lo)
                    for k in strips:
                        k.need("fe_v")
                        turn(k, "t_fe", [v[:, k.s, i * P:(i + 1) * P] for i in range(DI // P)])
                    for k in strips:
                        k.need("lo_fe", "hs0")
                        product(k, "fe2", "fe2_w", vt_hi, vt_lo)
                    for k in strips:
                        turn(k, "t_hs0", [hs0[:, k.s, i * P:(i + 1) * P] for i in range(FK)])
                    for k in strips:
                        k.need("lo_hs0", "he")
                        product(k, "hz_h", "W_hz", wht_hi, wht_lo, 0, DI)
                    for k in strips:
                        product(k, "hz_z", "W_hz", wht_hi, wht_lo, DI, 2 * DI)
                    for k in strips:
                        k.need("u")
                        turn(k, "t_u", [v[:, k.s, i * P:(i + 1) * P] for i in range(DI // P)])
                    for k in strips:
                        k.need("lo_u")
                        product(k, "out", "out_w", vt_hi, vt_lo)
                    for k in strips:
                        k.need("hs", "ha")
                        turn(k, "t_co", [t[:, k.s, i * P:(i + 1) * P] for t in (ha, hs) for i in range(FK)])
                    for k in strips:
                        k.need("lo_co")
                        product(k, "g1", "g1_w", vt_hi, vt_lo)
                    for k in strips:
                        k.need("g_v")
                        turn(k, "t_g", [v[:, k.s, i * P:(i + 1) * P] for i in range(G1 // P)])
                    for k in strips:
                        k.need("lo_g")
                        product(k, "g2", "g2_w", vt_hi, vt_lo)

            def bank_of(i, s):
                return ps[:, i % 2 * STRIPS + s, :]

            @block.scalar
            def _(act):
                def high(k, name, src_step, dst, src, width, scale=1.0):
                    k.need(src_step)
                    k.done(name, nc.scalar.activation(dst[:, k.s, 0:width], src[:, 0:width], ACT.Copy, scale=scale))

                with act.Fori(0, GROUPS) as g:
                    strips = [Strip(act, g, s) for s in range(STRIPS)]
                    for k in strips:
                        k.free("hz_z")
                        high(k, "hi_wh", "t_wh", wht_hi, bank_of(0, k.s), F)
                    for k in strips:
                        k.need("fe_nm")
                        k.done("fe_xh", nc.scalar.activation(v[:, k.s, :], bank_of(1, k.s), ACT.Identity,
                                                             scale=ve["fe"][:, k.s, 1:2], bias=ve["fe"][:, k.s, 2:3]))
                    for k in strips:
                        k.need("mx")
                        k.done("e", nc.scalar.activation(e[:, k.s, :], bank_of(2, k.s)[:, 2 * S:3 * S], ACT.Exp,
                                                         bias=sc[:, k.s, 0:1], accum_out=sc[:, k.s, 1:2]))
                    for k in strips:
                        high(k, "hi_ab", "t_ab", abt_hi, bank_of(3, k.s), S)
                    for k in strips:
                        k.need("fe_n")
                        k.done("fe_th", nc.scalar.activation(th[:, k.s, :], v[:, k.s, :], ACT.Tanh, scale=0.5))
                    for k in strips:
                        high(k, "hi_fe", "t_fe", vt_hi, bank_of(5, k.s), DI, 0.5)
                    for k in strips:
                        high(k, "hi_hs0", "t_hs0", wht_hi, bank_of(7, k.s), F)
                    for k in strips:
                        k.need("fe2")
                        k.done("he", nc.scalar.copy(he[:, k.s, :], bank_of(6, k.s)[:, 0:F]))
                    for k in strips:
                        k.need("hz_z", "fe_v")
                        k.done("z_th", nc.scalar.activation(th[:, k.s, :], bank_of(9, k.s), ACT.Tanh, scale=0.5))
                    for k in strips:
                        k.need("fe2")
                        high(k, "hi_u", "t_u", vt_hi, bank_of(10, k.s), DI, 0.5)
                    for k in strips:
                        k.need("out", "c1")
                        k.done("hs", nc.scalar.activation(hs[:, k.s, :], bank_of(11, k.s)[:, 0:F], ACT.Copy, scale=sc[:, k.s, 4:5]))
                    for k in strips:
                        high(k, "hi_co", "t_co", vt_hi, bank_of(12, k.s), G1)
                    for k in strips:
                        k.need("g_nm")
                        k.done("g_xh", nc.scalar.activation(v[:, k.s, :], bank_of(13, k.s), ACT.Identity,
                                                            scale=ve["g"][:, k.s, 1:2], bias=ve["g"][:, k.s, 2:3]))
                    for k in strips:
                        k.need("g_n")
                        k.done("g_th", nc.scalar.activation(th[:, k.s, :], v[:, k.s, :], ACT.Tanh, scale=0.5))
                    for k in strips:
                        high(k, "hi_g", "t_g", vt_hi, bank_of(14, k.s), G1, 0.5)
                    for k in strips:
                        k.need("g2")
                        k.done("tg", nc.scalar.activation(tg[:, k.s, :], bank_of(15, k.s)[:, 0:F], ACT.Tanh, scale=0.5))
                    for k in strips:
                        k.need("f_nm")
                        k.done("f_xh", nc.scalar.activation(fused[:, k.s, :], fused[:, k.s, :], ACT.Identity,
                                                            scale=ve["f"][:, k.s, 1:2], bias=ve["f"][:, k.s, 2:3]))
                    for k in strips:
                        k.need("o_nm")
                        k.done("o_out", nc.scalar.activation(fused[:, k.s, :], fused[:, k.s, :], ACT.Identity,
                                                             scale=ve["o"][:, k.s, 1:2], bias=ve["o"][:, k.s, 2:3]))
                        k.need("o_out")
                        k.done("stored", act.dma_start(outg[bass.ds(g, 1), k.s].rearrange("g p f -> (g p) f"), fused[:, k.s, :]))
                for s in range(STRIPS):
                    act.wait_ge(sems["stored", s], 16 * (GROUPS + 1))

            @block.gpsimd
            def _(pool):
                def inverse_std(k, n):
                    k.need(n + "_mv")
                    k.settle()
                    k.done(n + "_ve", nc.gpsimd.tensor_scalar(ve[n][:, k.s, 0:1], mv[n][:, k.s, 1:2], EPS, None, ALU.add))
                    k.need(n + "_ve")
                    k.done(n + "_rs", nc.gpsimd.tensor_tensor(ve[n][:, k.s, 1:2], ve[n][:, k.s, 0:1], half[:, :], ALU.pow))
                    k.need(n + "_rs")
                    k.settle()
                    k.done(n + "_nm", nc.gpsimd.tensor_scalar(ve[n][:, k.s, 2:3], mv[n][:, k.s, 0:1], ve[n][:, k.s, 1:2], -1.0,
                                                              ALU.mult, ALU.mult))

                with pool.Fori(0, GROUPS) as g:
                    strips = [Strip(pool, g, s) for s in range(STRIPS)]
                    for k in strips:
                        inverse_std(k, "fe")
                    for k in strips:
                        inverse_std(k, "g")
                    for k in strips:
                        k.need("hs", "ha", "he")
                        k.done("dl", nc.gpsimd.tensor_tensor(ha[:, k.s, :], ha[:, k.s, :], hs[:, k.s, :], ALU.subtract))
                        k.done("hh", nc.gpsimd.tensor_tensor(he[:, k.s, :], he[:, k.s, :], hs[:, k.s, :], ALU.add))
                    for k in strips:
                        inverse_std(k, "f")
                    for k in strips:
                        inverse_std(k, "o")

            @block.vector
            def _(dve):
                def low(k, name, hi_step, dst, src, hi_t, width, scale=1.0):
                    k.need(hi_step)
                    k.done(name, nc.vector.scalar_tensor_tensor(out=dst[:, k.s, 0:width], in0=src[:, 0:width], scalar=scale,
                                                                in1=hi_t[:, k.s, 0:width].bitcast(F32), op0=ALU.mult, op1=ALU.subtract))

                def moments(strips, n, src):
                    for k in strips:
                        k.need({"fe": "fe1", "g": "g1", "f": "f", "o": "y"}[n])
                        k.done(n + "_st", nc.vector.bn_stats(st[n][:, k.s, :], src(k)))
                    for k in strips:
                        k.need(n + "_st")
                        k.settle()
                        k.done(n + "_mv", nc.vector.bn_aggr(mv[n][:, k.s, :], st[n][:, k.s, :]))

                def scale_shift(strips, n, t, gain, shift):
                    for k in strips:
                        k.need(n + "_xh")
                        k.done(n + "_g", nc.vector.tensor_tensor(t[:, k.s, :], t[:, k.s, :], vec[gain][:, :], ALU.mult))
                    for k in strips:
                        k.need(n + "_g")
                        k.done(n + "_n", nc.vector.tensor_tensor(t[:, k.s, :], t[:, k.s, :], vec[shift][:, :], ALU.add))

                def twice_silu(strips, n):
                    for k in strips:
                        k.need(n + "_th")
                        k.done(n + "_v", nc.vector.scalar_tensor_tensor(out=v[:, k.s, :], in0=th[:, k.s, :], scalar=1.0, in1=v[:, k.s, :],
                                                                        op0=ALU.add, op1=ALU.mult))

                with dve.Fori(0, GROUPS) as g:
                    strips = [Strip(dve, g, s) for s in range(STRIPS)]
                    for k in strips:
                        low(k, "lo_wh", "hi_wh", wht_lo, bank_of(0, k.s), wht_hi, F)
                    moments(strips, "fe", lambda k: bank_of(1, k.s))
                    for k in strips:
                        k.need("bc")
                        k.done("mx", nc.vector.tensor_reduce(sc[:, k.s, 0:1], bank_of(2, k.s)[:, 2 * S:3 * S], AX.X, ALU.max, negate=True))
                    scale_shift(strips, "fe", v, "fe_ln_g", "fe_ln_b")
                    for k in strips:
                        k.need("e")
                        k.done("es", nc.vector.reciprocal(sc[:, k.s, 2:3], sc[:, k.s, 1:2]))
                    for k in strips:
                        k.free("cd")
                        k.done("cd", nc.vector.scalar_tensor_tensor(out=cj[:, k.s, :], in0=bank_of(2, k.s)[:, S:2 * S], scalar=1.0, in1=cpw[:, :],
                                                                    op0=ALU.mult, op1=ALU.mult, accum_out=sc[:, k.s, 3:4]))
                    for k in strips:
                        k.need("es")
                        k.done("ab", nc.vector.scalar_tensor_tensor(out=ab[:, k.s, :], in0=e[:, k.s, :], scalar=sc[:, k.s, 2:3],
                                                                    in1=bank_of(2, k.s)[:, 0:S], op0=ALU.mult, op1=ALU.mult))
                    for k in strips:
                        k.need("cd")
                        k.done("c1", nc.vector.tensor_tensor(sc[:, k.s, 4:5], sc[:, k.s, 3:4], cpb1[:, :], ALU.add))
                    for k in strips:
                        low(k, "lo_ab", "hi_ab", abt_lo, bank_of(3, k.s), abt_hi, S)
                    twice_silu(strips, "fe")
                    for k in strips:
                        k.need("abp")
                        k.done("hs0", nc.vector.tensor_tensor(hs0[:, k.s, :], bank_of(4, k.s)[:, 0:F], wh[:, k.s, 0:F], ALU.mult))
                    for k in strips:
                        low(k, "lo_fe", "hi_fe", vt_lo, bank_of(5, k.s), vt_hi, DI, 0.5)
                    for k in strips:
                        low(k, "lo_hs0", "hi_hs0", wht_lo, bank_of(7, k.s), wht_hi, F)
                    for k in strips:
                        k.need("in_att")
                        k.done("nn", nc.vector.tensor_scalar(sc[:, k.s, 5:6], num[:, k.s, F:F + 1], 0.0, None, ALU.is_equal))
                    for k in strips:
                        k.need("nn")
                        k.done("ws", nc.vector.scalar_tensor_tensor(out=sc[:, k.s, 6:7], in0=sc[:, k.s, 5:6], scalar=float(N),
                                                                    in1=num[:, k.s, F:F + 1], op0=ALU.mult, op1=ALU.add))
                    for k in strips:
                        k.need("ws")
                        k.done("wr", nc.vector.reciprocal(sc[:, k.s, 7:8], sc[:, k.s, 6:7]))
                    for k in strips:
                        k.done("hn", nc.vector.scalar_tensor_tensor(out=ha[:, k.s, :], in0=whsum[:, :], scalar=sc[:, k.s, 5:6],
                                                                    in1=num[:, k.s, 0:F], op0=ALU.mult, op1=ALU.add))
                    for k in strips:
                        k.need("wr", "hn")
                        k.done("ha", nc.vector.tensor_scalar(ha[:, k.s, :], ha[:, k.s, :], sc[:, k.s, 7:8], None, ALU.mult))
                    for k in strips:
                        k.need("z_th")
                        k.done("w", nc.vector.scalar_tensor_tensor(out=v[:, k.s, :], in0=th[:, k.s, :], scalar=1.0, in1=bank_of(9, k.s),
                                                                   op0=ALU.add, op1=ALU.mult))
                    for k in strips:
                        k.need("w")
                        k.done("u", nc.vector.scalar_tensor_tensor(out=v[:, k.s, :], in0=v[:, k.s, :], scalar=d2[:, :], in1=bank_of(8, k.s),
                                                                   op0=ALU.add, op1=ALU.mult))
                    for k in strips:
                        low(k, "lo_u", "hi_u", vt_lo, bank_of(10, k.s), vt_hi, DI, 0.5)
                    for k in strips:
                        low(k, "lo_co", "hi_co", vt_lo, bank_of(12, k.s), vt_hi, G1)
                    moments(strips, "g", lambda k: bank_of(13, k.s))
                    scale_shift(strips, "g", v, "g_ln_g", "g_ln_b")
                    twice_silu(strips, "g")
                    for k in strips:
                        low(k, "lo_g", "hi_g", vt_lo, bank_of(14, k.s), vt_hi, G1, 0.5)
                    for k in strips:
                        k.need("tg", "dl")
                        k.done("m", nc.vector.scalar_tensor_tensor(out=tg[:, k.s, :], in0=tg[:, k.s, :], scalar=1.0, in1=ha[:, k.s, :],
                                                                   op0=ALU.add, op1=ALU.mult))
                    for k in strips:
                        k.need("m", "hh")
                        k.free("stored")
                        k.done("f", nc.vector.scalar_tensor_tensor(out=fused[:, k.s, :], in0=tg[:, k.s, :], scalar=0.5, in1=he[:, k.s, :],
                                                                   op0=ALU.mult, op1=ALU.add))
                    moments(strips, "f", lambda k: fused[:, k.s, :])
                    scale_shift(strips, "f", fused, "ln_g", "ln_b")
                    for k in strips:
                        k.need("f_n", "in_x")
                        k.done("y", nc.vector.tensor_tensor(fused[:, k.s, :], fused[:, k.s, :], xr[:, k.s, :], ALU.add))
                    moments(strips, "o", lambda k: fused[:, k.s, :])


def prepare(nc, w, mats, bias_of, bias_at, NB, LO_ROW, hi, lo, brow, ones, vec, cpw, cpb1, d2, half):
    WIDE = max(k * c for _, k, c in mats.values())
    SLOTS = 2
    with ExitStack() as ctx:
        def sb(name, shape, dt=F32):
            return ctx.enter_context(nc.sbuf_tensor(name, shape, dt))

        def sem(name):
            return ctx.enter_context(nc.semaphore(name))

        raw = sb("raw", [P, SLOTS, WIDE])
        braw = sb("braw", [LO_ROW + 1, NB])
        bhi = sb("bhi", [LO_ROW + 1, NB], F32R)
        small = sb("small", [P, 2])
        araw = sb("araw", [LO_ROW + 1, cpw.shape[1]])
        raw_in = [sem(f"wp_raw_in{k}") for k in range(SLOTS)]
        vec_in = sem("wp_vec_in")
        bias_in = sem("wp_bias_in")
        cleared = sem("wp_cleared")
        hi_made = sem("wp_hi_made")
        lo_made = sem("wp_lo_made")
        bias_hi = sem("wp_bias_hi")
        summed = sem("wp_summed")
        done = sem("wp_done")
        S = cpw.shape[1]
        DT = bias_at["W_bcdt"] + 2 * S
        n_vec = len(vec) + 3
        n_bias = 2 * len(mats) + 2
        with nc.Block() as block:
            @block.sync
            def _(sp):
                for i, (n, (m, k, c)) in enumerate(mats.items()):
                    if i >= SLOTS:
                        sp.wait_ge(lo_made, i - SLOTS + 1)
                    sp.dma_start(raw[:, i % SLOTS, 0:k * c].rearrange("p (k c) -> p k c", k=k),
                                 m.rearrange("(k p) c -> p k c", p=P)).then_inc(raw_in[i % SLOTS], 16)

            @block.scalar
            def _(act):
                for n in mats:
                    row = w[bias_of[n]].rearrange("(o c) -> o c", o=1)
                    at = slice(bias_at[n], bias_at[n] + mats[n][2])
                    for r in (0, LO_ROW):
                        act.dma_start(braw[r:r + 1, at], row).then_inc(bias_in, 16)
                for r in (0, LO_ROW):
                    act.dma_start(araw[r:r + 1, :], w["A"].rearrange("(o c) -> o c", o=1)).then_inc(bias_in, 16)
                for n, t in vec.items():
                    act.dma_start(t[:, :], w[n].partition_broadcast(P)).then_inc(vec_in, 16)
                act.dma_start(cpw[:, :], w["cp_w"].rearrange("s o -> (s o)").partition_broadcast(P)).then_inc(vec_in, 16)
                act.dma_start(small[:, 0:1], w["cp_b"].partition_broadcast(P)).then_inc(vec_in, 16)
                act.dma_start(small[:, 1:2], w["D"].partition_broadcast(P)).then_inc(vec_in, 16)
                for i, (n, (m, k, c)) in enumerate(mats.items()):
                    act.wait_ge(raw_in[i % SLOTS], 16 * (i // SLOTS + 1))
                    nc.scalar.copy(hi[n][:, :, :].rearrange("p k c -> p (k c)"), raw[:, i % SLOTS, 0:k * c]).then_inc(hi_made, 1)
                act.wait_ge(summed, 2)
                act.wait_ge(cleared, 1)
                nc.scalar.copy(brow[0:1, :], braw[0:1, :]).then_inc(bias_hi, 1)
                nc.scalar.copy(bhi[LO_ROW:LO_ROW + 1, :], braw[LO_ROW:LO_ROW + 1, :]).then_inc(bias_hi, 1)

            @block.gpsimd
            def _(pool):
                nc.gpsimd.memset(brow[:, :].bitcast(F32), 0.0).then_inc(cleared, 1)
                nc.gpsimd.memset(half[:, :], -0.5).then_inc(cleared, 1)

            @block.vector
            def _(dve):
                nc.vector.memset(ones[:, :].bitcast(F32), 1.0).then_inc(done, 1)
                for i, (n, (m, k, c)) in enumerate(mats.items()):
                    dve.wait_ge(hi_made, i + 1)
                    nc.vector.tensor_tensor(lo[n][:, :, :].rearrange("p k c -> p (k c)"), raw[:, i % SLOTS, 0:k * c],
                                            hi[n][:, :, :].rearrange("p k c -> p (k c)").bitcast(F32), ALU.subtract).then_inc(lo_made, 1)
                dve.wait_ge(bias_in, 16 * n_bias)
                for r in (0, LO_ROW):
                    nc.vector.tensor_tensor(braw[r:r + 1, DT:DT + S], braw[r:r + 1, DT:DT + S], araw[r:r + 1, :], ALU.add).then_inc(summed, 1)
                dve.wait_ge(vec_in, 16 * n_vec)
                nc.vector.tensor_scalar(cpb1[:, :], small[:, 0:1], 1.0, None, ALU.add).then_inc(done, 1)
                nc.vector.tensor_scalar(d2[:, :], small[:, 1:2], 2.0, None, ALU.mult).then_inc(done, 1)
                dve.wait_ge(bias_hi, 2)
                nc.vector.tensor_tensor(brow[LO_ROW:LO_ROW + 1, :], braw[LO_ROW:LO_ROW + 1, :], bhi[LO_ROW:LO_ROW + 1, :].bitcast(F32),
                                        ALU.subtract).then_inc(done, 1)


_W = ["W", "a_src", "a_dst", "W_bcdt", "b_bcdt", "abp_w", "abp_b", "cp_w", "cp_b", "W_hz", "b_hz", "out_w", "out_b",
      "fe1_w", "fe1_b", "fe_ln_g", "fe_ln_b", "fe2_w", "fe2_b", "A", "D", "g1_w", "g1_b", "g_ln_g", "g_ln_b", "g2_w",
      "g2_b", "ln_g", "ln_b"]


def kernel(**inputs):
    import numpy as _np
    import concourse.bacc as _bacc
    from concourse import mybir as _mybir
    from concourse.bass_utils import run_bass_kernel_spmd as _run

    nc = _bacc.Bacc("TRN2", target_bir_lowering=False, num_devices=1)
    arrays, aps = {}, {}
    for name in ["x", "adj"] + ["L0_gnn_" + n for n in _W]:
        a = _np.ascontiguousarray(inputs[name])
        arrays[f"in_{name}"] = a
        aps[name] = nc.dram_tensor(f"in_{name}", a.shape, _mybir.dt.from_np(a.dtype), kind="ExternalInput").ap()
    out = nc.dram_tensor("out_0", aps["x"].shape, _mybir.dt.float32, kind="ExternalOutput").ap()
    build(nc, aps["x"], aps["adj"], {n: aps["L0_gnn_" + n] for n in _W}, out)
    r = _run(nc, [arrays], core_ids=[0])
    return r.results[0]["out_0"]
```

```python
from contextlib import ExitStack

import concourse.bass as bass
from concourse import mybir

F32 = mybir.dt.float32
F32R = mybir.dt.float32r
BF16 = mybir.dt.bfloat16
I32 = mybir.dt.int32
ALU = mybir.AluOpType
ACT = mybir.ActivationFunctionType
AX = mybir.AxisListType
RED = bass.bass_isa.ReduceOp

P = 128
SLOPE = 0.2
EPS = 1e-5
RANGE_MAX = 64.0
STRIPS = 4
ROWS = STRIPS * P
CHUNK = 4


def build(nc, x, adj, w, out):
    N, F = x.shape
    TILES = N // P
    GROUPS = N // ROWS
    FK = F // P
    FE = F + 2
    NCH = TILES // CHUNK
    with ExitStack() as ctx:
        dims = dict(N=N, F=F, TILES=TILES, GROUPS=GROUPS, FK=FK, FE=FE, NCH=NCH)
        wh_rows = nc.dram_tensor("wh_rows", [N, FE], F32, kind="Internal").ap()
        att_rows = nc.dram_tensor("att_rows", [N, FE], F32, kind="Internal").ap()
        r_row = nc.dram_tensor("r_row", [N], F32, kind="Internal").ap()
        dsh_row = nc.dram_tensor("dsh_row", [N], F32, kind="Internal").ap()

        def sb(name, shape, dt=F32):
            return ctx.enter_context(nc.sbuf_tensor(name, shape, dt))

        keep = dict(
            ident=sb("ident", [P, P]), identb=sb("identb", [P, P], BF16),
            s=sb("s_all", [P, TILES]), d=sb("d_all", [P, TILES]),
            q=sb("q_all", [P, TILES]), f=sb("f_all", [P, TILES]),
            ext=sb("ext", [P, 2]), flag=sb("flag", [P, 1], I32), whsum=sb("whsum", [P, F]),
        )
        project(nc, dims, x, w, keep, wh_rows, r_row, dsh_row)
        attend(nc, dims, adj, keep, wh_rows, att_rows, r_row, dsh_row)
        fuse(nc, dims, x, w, keep, wh_rows, att_rows, out)


def clear(nc, sems):
    with nc.Block() as block:
        @block.sync
        def _(sp):
            for s in sems:
                sp.sem_clear(s)


def project(nc, dims, x, w, keep, wh_rows, r_row, dsh_row):
    F, TILES, FK, FE = dims["F"], dims["TILES"], dims["FK"], dims["FE"]
    SLOTS = 2
    ident, identb, s_all, d_all = keep["ident"], keep["identb"], keep["s"], keep["d"]
    q_all, f_all, ext, flag, whsum = keep["q"], keep["f"], keep["ext"], keep["flag"], keep["whsum"]
    with ExitStack() as ctx:
        def sb(name, shape, dt=F32):
            return ctx.enter_context(nc.sbuf_tensor(name, shape, dt))

        sems = []

        def sem(name):
            sems.append(ctx.enter_context(nc.semaphore(name)))
            return sems[-1]

        w_sb = sb("w_sb", [P, FK, F])
        a_bc = sb("a_bc", [P, 2, F])
        xin = sb("xin", [P, SLOTS, F])
        xt = sb("xt", [P, SLOTS, FK, P])
        wh = sb("wh", [P, SLOTS, FE])
        junk = sb("junk", [P, SLOTS, 2, F])
        wsum = sb("wsum", [P, F])
        ones = sb("ones", [P, P])
        loc = sb("loc", [P, 3])
        bias = sb("bias", [P, 2])
        rarg = sb("rarg", [P, 2, TILES])
        rd = sb("rd", [P, 2, TILES])
        rdt = sb("rdt", [P, P])
        rng = sb("rng", [P, 1])
        ps_x = ctx.enter_context(nc.psum_tensor("ps_x", [P, SLOTS, 512], F32))
        ps_w = ctx.enter_context(nc.psum_tensor("ps_w", [P, SLOTS, 512], F32))
        ps_r = ctx.enter_context(nc.psum_tensor("ps_r", [P, 512], F32))
        ps_s = ctx.enter_context(nc.psum_tensor("ps_s", [P, 512], F32))

        weights_in = sem("pr_weights_in")
        x_in = [sem(f"pr_x_in{k}") for k in range(SLOTS)]
        cleared = sem("pr_cleared")
        ident_ready = sem("pr_ident_ready")
        x_turned = sem("pr_x_turned")
        xt_ready = sem("pr_xt_ready")
        wh_made = sem("pr_wh_made")
        wh_ready = sem("pr_wh_ready")
        sd_done = sem("pr_sd_done")
        sum_done = sem("pr_sum_done")
        wh_stored = [sem(f"pr_wh_stored{k}") for k in range(SLOTS)]
        stat = sem("pr_stat")
        ext_ready = sem("pr_ext_ready")
        bias_ready = sem("pr_bias_ready")
        rarg_ready = sem("pr_rarg_ready")
        exp_done = sem("pr_exp_done")
        rd_turned = sem("pr_rd_turned")
        sum_spread = sem("pr_sum_spread")
        rdt_ready = sem("pr_rdt_ready")
        r_stored = sem("pr_r_stored")

        with nc.Block() as block:
            @block.sync
            def _(sp):
                sp.dma_start(w_sb[:, :, :], w["W"].rearrange("(k p) n -> p k n", p=P)).then_inc(weights_in, 16)
                sp.dma_start(a_bc[:, 0, :], w["a_src"].rearrange("f o -> (f o)").partition_broadcast(P)).then_inc(weights_in, 16)
                sp.dma_start(a_bc[:, 1, :], w["a_dst"].rearrange("f o -> (f o)").partition_broadcast(P)).then_inc(weights_in, 16)
                for k in range(SLOTS):
                    sp.dma_start(xin[:, k, :], x[k * P:(k + 1) * P, :]).then_inc(x_in[k], 16)
                def store(i, k):
                    sp.wait_ge(wh_ready, i * SLOTS + k + 1 + SLOTS)
                    sp.dma_start(wh_rows[bass.ds((i * SLOTS + k) * P, P), :], wh[:, k, :]).then_inc(wh_stored[k], 16)

                with sp.Fori(1, TILES // SLOTS) as i:
                    for k in range(SLOTS):
                        sp.wait_ge(x_turned, (i - 1) * SLOTS + k + 1)
                        sp.dma_start(xin[:, k, :], x[bass.ds((i * SLOTS + k) * P, P), :]).then_inc(x_in[k], 16)
                    for k in range(SLOTS):
                        store(i - 1, k)
                for k in range(SLOTS):
                    store(TILES // SLOTS - 1, k)
                for k in range(SLOTS):
                    sp.wait_ge(wh_stored[k], 16 * (TILES // SLOTS + 1))
                sp.wait_ge(rdt_ready, 1)
                sp.dma_start(r_row.rearrange("(t p) -> t p", p=P), rdt[0:TILES, :]).then_inc(r_stored, 16)
                sp.dma_start(dsh_row.rearrange("(t p) -> t p", p=P), rdt[TILES:2 * TILES, :]).then_inc(r_stored, 16)
                sp.wait_ge(r_stored, 32)

            @block.gpsimd
            def _(pool):
                pool.sem_inc(sum_done, SLOTS)
                nc.gpsimd.memset(ident[:, :], 0.0).then_inc(cleared, 1)
                nc.gpsimd.memset(identb[:, :], 0.0).then_inc(cleared, 1)
                nc.gpsimd.memset(wh[:, :, F:F + 1], 1.0).then_inc(cleared, 1)
                nc.gpsimd.memset(wh[:, :, F + 1:F + 2], 0.0).then_inc(cleared, 1)
                nc.gpsimd.memset(wsum[:, :], 0.0).then_inc(cleared, 1)
                nc.gpsimd.memset(ones[:, :], 1.0).then_inc(cleared, 1)
                pool.wait_ge(cleared, 6)
                for t in (ident, identb):
                    nc.gpsimd.affine_select(out=t[:, :], in_=t[:, :], compare_op=ALU.not_equal, fill=1.0,
                                            base=0, pattern=[[-1, P]], channel_multiplier=1).then_inc(ident_ready, 1)
                with pool.Fori(0, TILES // SLOTS) as i:
                    for k in range(SLOTS):
                        pool.wait_ge(wh_ready, i * SLOTS + k + 1 + SLOTS)
                        pool.wait_ge(sum_done, i * SLOTS + k + SLOTS)
                        nc.gpsimd.tensor_tensor(wsum[:, :], wsum[:, :], wh[:, k, 0:F], ALU.add).then_inc(sum_done, 1)
                pool.wait_ge(stat, 3)
                nc.gpsimd.partition_all_reduce(ext[:, :], loc[:, 0:2], P, RED.max).then_inc(ext_ready, 1)

            @block.tensor
            def _(pe):
                pe.wait_ge(ident_ready, 2)
                pe.wait_ge(weights_in, 48)
                with pe.Fori(0, TILES // SLOTS) as i:
                    for k in range(SLOTS):
                        pe.wait_ge(x_in[k], i * 16 + 16)
                        for c in range(FK):
                            last = nc.tensor.transpose(ps_x[:, k, c * P:(c + 1) * P], xin[:, k, c * P:(c + 1) * P], ident[:, :])
                        last.then_inc(x_turned, 1)
                    for k in range(SLOTS):
                        pe.wait_ge(xt_ready, i * SLOTS + k + 1)
                        pe.wait_ge(wh_ready, i * SLOTS + k + 1)
                        for c in range(FK):
                            last = nc.tensor.matmul(ps_w[:, k, 0:F], xt[:, k, c, :], w_sb[:, c, :],
                                                    start=(c == 0), stop=(c == FK - 1))
                        last.then_inc(wh_made, 1)
                pe.wait_ge(exp_done, 1)
                pe.wait_ge(rarg_ready, 2)
                nc.tensor.transpose(ps_r[:, 0:P], rd[:, :, :].rearrange("p a t -> p (a t)"), ident[:, :]).then_inc(rd_turned, 1)
                pe.wait_ge(sum_done, TILES + SLOTS)
                nc.tensor.matmul(ps_s[:, 0:F], ones[:, :], wsum[:, :], start=True, stop=True).then_inc(sum_spread, 1)

            @block.scalar
            def _(act):
                act.sem_inc(wh_ready, SLOTS)
                for k in range(SLOTS):
                    act.sem_inc(wh_stored[k], 16)
                act.wait_ge(cleared, 6)
                with act.Fori(0, TILES // SLOTS) as i:
                    for k in range(SLOTS):
                        act.wait_ge(x_turned, i * SLOTS + k + 1)
                        nc.scalar.copy(xt[:, k, :, :].rearrange("p c n -> p (c n)"), ps_x[:, k, 0:F]).then_inc(xt_ready, 1)
                    for k in range(SLOTS):
                        act.wait_ge(wh_made, i * SLOTS + k + 1)
                        act.wait_ge(wh_stored[k], i * 16 + 16)
                        act.wait_ge(sd_done, i * SLOTS + k + 1)
                        act.wait_ge(sum_done, i * SLOTS + k + 1)
                        nc.scalar.copy(wh[:, k, 0:F], ps_w[:, k, 0:F]).then_inc(wh_ready, 1)
                act.wait_ge(bias_ready, 2)
                act.wait_ge(rarg_ready, 1)
                nc.scalar.activation(rd[:, 0, :], rarg[:, 1, :], ACT.Exp).then_inc(exp_done, 1)
                nc.scalar.activation(q_all[:, :], d_all[:, :], ACT.Exp, bias=bias[:, 0:1], scale=1.0 - SLOPE).then_inc(exp_done, 1)
                nc.scalar.activation(f_all[:, :], d_all[:, :], ACT.Exp, bias=bias[:, 1:2], scale=SLOPE).then_inc(exp_done, 1)

            @block.vector
            def _(dve):
                dve.sem_inc(sd_done, SLOTS)
                dve.wait_ge(weights_in, 48)
                with dve.Fori(0, TILES // SLOTS) as i:
                    for k in range(SLOTS):
                        dve.wait_ge(wh_ready, i * SLOTS + k + 1 + SLOTS)
                        dve.wait_ge(sd_done, i * SLOTS + k + 1)
                        for a, dst in enumerate((s_all, d_all)):
                            last = nc.vector.scalar_tensor_tensor(
                                out=junk[:, k, a, :], in0=wh[:, k, 0:F], scalar=1.0, in1=a_bc[:, a, :],
                                op0=ALU.mult, op1=ALU.mult, accum_out=dst[:, bass.ds(i * SLOTS + k, 1)])
                        last.then_inc(sd_done, 1)
                dve.wait_ge(sd_done, TILES + SLOTS)
                nc.vector.tensor_reduce(loc[:, 0:1], d_all[:, :], AX.X, ALU.max).then_inc(stat, 1)
                nc.vector.tensor_reduce(loc[:, 2:3], d_all[:, :], AX.X, ALU.min).then_inc(stat, 1)
                dve.wait_ge(stat, 2)
                nc.vector.tensor_scalar(loc[:, 1:2], loc[:, 2:3], -1.0, None, ALU.mult).then_inc(stat, 1)
                dve.wait_ge(ext_ready, 1)
                nc.vector.tensor_scalar(bias[:, 0:1], ext[:, 0:1], SLOPE - 1.0, None, ALU.mult).then_inc(bias_ready, 1)
                nc.vector.tensor_scalar(bias[:, 1:2], ext[:, 0:1], -SLOPE, None, ALU.mult).then_inc(bias_ready, 1)
                nc.vector.tensor_tensor(rng[:, :], ext[:, 0:1], ext[:, 1:2], ALU.add).then_inc(bias_ready, 1)
                dve.wait_ge(bias_ready, 3)
                nc.vector.tensor_scalar(flag[:, :], rng[:, :], RANGE_MAX, None, ALU.is_le).then_inc(stat, 1)
                nc.vector.tensor_scalar(rarg[:, 0, :], s_all[:, :], SLOPE - 1.0, bias[:, 0:1], ALU.mult, ALU.add).then_inc(stat, 1)
                dve.wait_ge(stat, 5)
                nc.vector.tensor_scalar(rarg[:, 1, :], rarg[:, 0, :], 0.0, None, ALU.min).then_inc(rarg_ready, 1)
                nc.vector.tensor_scalar(rd[:, 1, :], d_all[:, :], ext[:, 1:2], None, ALU.add).then_inc(rarg_ready, 1)
                dve.wait_ge(rd_turned, 1)
                nc.vector.tensor_copy(rdt[:, :], ps_r[:, 0:P]).then_inc(rdt_ready, 1)
                dve.wait_ge(sum_spread, 1)
                nc.vector.tensor_copy(whsum[:, :], ps_s[:, 0:F]).then_inc(stat, 1)
        clear(nc, sems)


def attend(nc, dims, adj, keep, wh_rows, att_rows, r_row, dsh_row):
    F, TILES, GROUPS, FE, NCH = (dims[k] for k in ("F", "TILES", "GROUPS", "FE", "NCH"))
    W = CHUNK * P
    LOADS = 4
    MASKS = 2
    QS = CHUNK
    SPLITS = CHUNK
    identb, ident = keep["identb"], keep["ident"]
    q_all, f_all, flag = keep["q"], keep["f"], keep["flag"]
    with ExitStack() as ctx:
        def sb(name, shape, dt=F32):
            return ctx.enter_context(nc.sbuf_tensor(name, shape, dt))

        sems = []

        def sem(name):
            sems.append(ctx.enter_context(nc.semaphore(name)))
            return sems[-1]

        g_hi = sb("g_hi", [P, TILES, FE], F32R)
        g_lo = sb("g_lo", [P, TILES, FE], F32R)
        adj_sb = sb("adj_sb", [P, LOADS, STRIPS, W], I32)
        mask = sb("mask", [P, MASKS, STRIPS, W], BF16)
        r_bc = sb("r_bc", [P, 2, ROWS])
        qm = sb("qm", [P, QS, ROWS])
        q_hi = sb("q_hi", [P, SPLITS, ROWS], F32R)
        q_lo = sb("q_lo", [P, SPLITS, ROWS], F32R)
        stage = sb("stage", [P, STRIPS, FE])
        acc = ctx.enter_context(nc.psum_tensor("acc", [P, STRIPS, 512], F32))
        turned = ctx.enter_context(nc.psum_tensor("turned", [P, CHUNK, 1024], BF16))

        split_parts(nc, dims, keep, wh_rows, g_hi, g_lo, adj_sb)

        r_in = sem("at_r_in")
        adj_in = [sem(f"at_adj_in{k}") for k in range(LOADS)]
        mask_ready = sem("at_mask_ready")
        mask_begun = sem("at_mask_begun")
        turn_done = sem("at_turn_done")
        q_made = sem("at_q_made")
        hi_ready = sem("at_hi_ready")
        lo_ready = sem("at_lo_ready")
        split_free = sem("at_split_free")
        acc_ready = sem("at_acc_ready")
        acc_free = sem("at_acc_free")
        stage_ready = sem("at_stage_ready")
        stage_stored = sem("at_stage_stored")

        adj_v = adj.rearrange("(g s p) j -> g p s j", s=STRIPS, p=P)
        att_v = att_rows.rearrange("(g s p) c -> g s p c", s=STRIPS, p=P)
        LAST_TILE = GROUPS * TILES
        slow = slow_path(nc, dims, adj, keep, wh_rows, att_rows, dsh_row, sem, sb,
                         dict(adj=adj_sb, mask=mask, r_bc=r_bc, qm=qm, stage=stage), acc, turned)

        with nc.Block() as block:
            @block.sync
            def _(sp):
                def load(g, c, k):
                    sp.dma_start(adj_sb[:, k, :, :],
                                 adj_v[bass.ds(g, 1), :, :, bass.ds(c * W, W)].rearrange("g p s j -> (g p) s j")
                                 ).then_inc(adj_in[k], 16)

                def load_r(g, slot):
                    sp.dma_start(r_bc[:, slot, :], r_row[bass.ds(g * ROWS, ROWS)].partition_broadcast(P)).then_inc(r_in, 16)

                fast = sp.value_load(flag[0:1, 0:1], min_val=0, max_val=1)
                with sp.If(fast == 1):
                    load_r(0, 0)
                    for k in range(LOADS):
                        load(0, k, k)
                    with sp.Fori(1, NCH // LOADS) as b:
                        for k in range(LOADS):
                            sp.wait_ge(mask_ready, b * LOADS + (k + 1 - LOADS))
                            load(0, b * LOADS + k, k)
                    with sp.Fori(1, GROUPS) as g:
                        sp.wait_ge(q_made, (g - 1) * TILES + CHUNK)
                        sp.dma_start(r_bc[:, bass.ds(g % 2, 1), :],
                                     r_row[bass.ds(g * ROWS, ROWS)].partition_broadcast(P)).then_inc(r_in, 16)
                        with sp.Fori(0, NCH // LOADS) as b:
                            for k in range(LOADS):
                                sp.wait_ge(mask_ready, g * NCH + b * LOADS + (k + 1 - LOADS))
                                load(g, b * LOADS + k, k)
                with sp.Else():
                    slow["sync"](sp)

            @block.gpsimd
            def _(pool):
                fast = pool.value_load(flag[0:1, 0:1], min_val=0, max_val=1)
                with pool.If(fast == 1):
                    with pool.Fori(0, GROUPS * NCH // LOADS) as b:
                        for k in range(LOADS):
                            pool.wait_ge(adj_in[k], b * 16 + 16)
                            pool.wait_ge(turn_done, (b * LOADS + k + 1) * CHUNK)
                            pool.sem_inc(mask_begun, 1)
                            nc.gpsimd.tensor_scalar(mask[:, k % MASKS, :, :].rearrange("p s j -> p (s j)"),
                                                    adj_sb[:, k, :, :].rearrange("p s j -> p (s j)"),
                                                    0.0, None, ALU.is_gt).then_inc(mask_ready, 1)
                    nc.gpsimd.drain().then_inc(mask_ready, 1)
                with pool.Else():
                    slow["pool"](pool)

            @block.tensor
            def _(pe):
                def turn(n, m, k):
                    if k == 0:
                        pe.wait_ge(mask_ready, n + 1)
                    pe.wait_ge(q_made, n * CHUNK + k + 1)
                    for s in range(STRIPS):
                        last = nc.tensor.transpose(turned[:, k, s * P:(s + 1) * P], mask[:, m, s, k * P:(k + 1) * P], identb[:, :])
                    last.then_inc(turn_done, 1)

                def products(n, c, g, k, first=False, final=False):
                    j = c * CHUNK + k
                    t = n * CHUNK + k
                    pe.wait_ge(hi_ready, t + 1)
                    for s in range(STRIPS):
                        if first:
                            pe.wait_ge(acc_free, g * STRIPS + s + 1)
                        cols = slice(s * P, (s + 1) * P)
                        nc.tensor.matmul(acc[:, s, 0:FE], q_hi[:, k, cols], g_hi[:, bass.ds(j, 1), :].rearrange("p a f -> p (a f)"),
                                         start=first, stop=False)
                        nc.tensor.matmul(acc[:, s, 0:FE], q_hi[:, k, cols], g_lo[:, bass.ds(j, 1), :].rearrange("p a f -> p (a f)"),
                                         start=False, stop=False)
                    pe.wait_ge(lo_ready, t + 1 + QS)
                    for s in range(STRIPS):
                        cols = slice(s * P, (s + 1) * P)
                        last = nc.tensor.matmul(acc[:, s, 0:FE], q_lo[:, k, cols], g_hi[:, bass.ds(j, 1), :].rearrange("p a f -> p (a f)"),
                                                start=False, stop=final)
                    last.then_inc(split_free, 1)

                def pair(g, c, first=False, final=False):
                    for m in range(2):
                        for k in range(CHUNK):
                            turn(g * NCH + c + (m + 1), (m + 1) % MASKS, k)
                            products(g * NCH + c + m, c + m, g, k, first=first and m == 0 and k == 0,
                                     final=final and m == 1 and k == CHUNK - 1)

                fast = pe.value_load(flag[0:1, 0:1], min_val=0, max_val=1)
                with pe.If(fast == 1):
                    pe.sem_inc(turn_done, MASKS * CHUNK)
                    pe.sem_inc(split_free, SPLITS)
                    for k in range(CHUNK):
                        turn(0, 0, k)
                    with pe.Fori(0, GROUPS) as g:
                        pair(g, 0, first=True)
                        with pe.Fori(1, NCH // 2 - 1) as b:
                            pair(g, b * 2)
                        pair(g, NCH - 2, final=True)
                with pe.Else():
                    slow["tensor"](pe)

            @block.vector
            def _(dve):
                BODY = 2 * CHUNK

                def mul_mask(t, j, slot, k):
                    dve.wait_ge(turn_done, t + 1 + MASKS * CHUNK)
                    dve.wait_ge(lo_ready, t + 1)
                    nc.vector.scalar_tensor_tensor(
                        out=qm[:, k % QS, :], in0=r_bc[:, slot, :], scalar=q_all[:, bass.ds(j, 1)],
                        in1=turned[:, k % CHUNK, 0:ROWS], op0=ALU.max, op1=ALU.mult).then_inc(q_made, 1)

                def low_part(t, k):
                    dve.wait_ge(hi_ready, t + 1)
                    dve.wait_ge(split_free, t + 1)
                    nc.vector.tensor_tensor(q_lo[:, k % SPLITS, :], qm[:, k % QS, :], q_hi[:, k % SPLITS, :].bitcast(F32),
                                            ALU.subtract).then_inc(lo_ready, 1)

                fast = dve.value_load(flag[0:1, 0:1], min_val=0, max_val=1)
                with dve.If(fast == 1):
                    dve.sem_inc(q_made, CHUNK)
                    dve.sem_inc(lo_ready, QS)
                    with dve.Fori(0, GROUPS // 2) as gg:
                        for slot in range(2):
                            with dve.Fori(0, TILES // BODY) as b:
                                dve.wait_ge(r_in, gg * 32 + 16 * (slot + 1))
                                base = gg * (2 * TILES) + slot * TILES + b * BODY
                                for k in range(BODY):
                                    mul_mask(base + k, b * BODY + k, slot, k)
                                    if k >= 1:
                                        low_part(base + (k - 1), k - 1)
                                low_part(base + (BODY - 1), BODY - 1)
                with dve.Else():
                    slow["vector"](dve)

            @block.scalar
            def _(act):
                BODY = 2 * CHUNK

                def high_part(t, k):
                    act.wait_ge(q_made, t + 1 + CHUNK)
                    act.wait_ge(split_free, t + 1)
                    nc.scalar.copy(q_hi[:, k % SPLITS, :], qm[:, k % QS, :]).then_inc(hi_ready, 1)

                def evacuate(g):
                    for s in range(STRIPS):
                        if s == 0:
                            act.wait_ge(stage_stored, (g + 1) * (16 * STRIPS))
                            act.wait_ge(split_free, (g + 1) * TILES + SPLITS)
                        nc.scalar.copy(stage[:, s, :], acc[:, s, 0:FE]).then_inc(acc_free, 1)
                    for s in range(STRIPS):
                        act.wait_ge(acc_free, g * STRIPS + s + 1 + STRIPS)
                        act.dma_start(att_v[bass.ds(g, 1), s, :, :].rearrange("g p c -> (g p) c"), stage[:, s, :]).then_inc(stage_stored, 16)

                def body(base, g_out=None):
                    for k in range(BODY):
                        high_part(base + k, k)
                        if g_out is not None and k == 3:
                            evacuate(g_out)

                fast = act.value_load(flag[0:1, 0:1], min_val=0, max_val=1)
                with act.If(fast == 1):
                    act.sem_inc(acc_free, STRIPS)
                    act.sem_inc(stage_stored, 16 * STRIPS)
                    for k in range(BODY):
                        high_part(k, k)
                    with act.Fori(0, GROUPS - 1) as g:
                        with act.Fori(1, TILES // BODY) as b:
                            body(g * TILES + b * BODY)
                        body(g * TILES + TILES, g_out=g)
                    with act.Fori(1, TILES // BODY) as b:
                        body((GROUPS - 1) * TILES + b * BODY)
                    evacuate(GROUPS - 1)
                    act.wait_ge(stage_stored, 16 * STRIPS * (GROUPS + 1))
                with act.Else():
                    slow["scalar"](act)
        clear(nc, sems)


def split_parts(nc, dims, keep, wh_rows, g_hi, g_lo, adj_sb):
    TILES, FE = dims["TILES"], dims["FE"]
    f_all = keep["f"]
    SLOTS, PER = 2, 4
    with ExitStack() as ctx:
        sems = []

        def sem(name):
            sems.append(ctx.enter_context(nc.semaphore(name)))
            return sems[-1]

        def slot(k):
            return adj_sb[:, k, :, :].rearrange("p s j -> p (s j)").bitcast(F32)[:, 0:PER * FE].rearrange("p (t f) -> p t f", t=PER)

        rows_in = [sem(f"sp_rows_in{k}") for k in range(SLOTS)]
        hi_made = sem("sp_hi_made")
        lo_made = sem("sp_lo_made")
        wh_v = wh_rows.rearrange("(b t p) f -> b p t f", t=PER, p=P)
        STEPS = TILES // PER // SLOTS
        with nc.Block() as block:
            @block.sync
            def _(sp):
                for k in range(SLOTS):
                    sp.dma_start(slot(k), wh_v[k]).then_inc(rows_in[k], 16)
                with sp.Fori(1, STEPS) as i:
                    for k in range(SLOTS):
                        sp.wait_ge(lo_made, (i - 1) * (SLOTS * PER) + (k + 1) * PER)
                        sp.dma_start(slot(k), wh_v[bass.ds(i * SLOTS + k, 1)].rearrange("b p t f -> (b p) t f")).then_inc(rows_in[k], 16)

            @block.scalar
            def _(act):
                with act.Fori(0, STEPS) as i:
                    for k in range(SLOTS):
                        act.wait_ge(rows_in[k], i * 16 + 16)
                        for t in range(PER):
                            tile = i * (SLOTS * PER) + (k * PER + t)
                            nc.scalar.activation(g_hi[:, bass.ds(tile, 1), :].rearrange("p a f -> p (a f)"), slot(k)[:, t, :], ACT.Copy,
                                                 scale=f_all[:, bass.ds(tile, 1)]).then_inc(hi_made, 1)

            @block.vector
            def _(dve):
                with dve.Fori(0, STEPS) as i:
                    for k in range(SLOTS):
                        for t in range(PER):
                            tile = i * (SLOTS * PER) + (k * PER + t)
                            dve.wait_ge(hi_made, tile + 1)
                            nc.vector.scalar_tensor_tensor(
                                out=g_lo[:, bass.ds(tile, 1), :].rearrange("p a f -> p (a f)"), in0=slot(k)[:, t, :],
                                scalar=f_all[:, bass.ds(tile, 1)],
                                in1=g_hi[:, bass.ds(tile, 1), :].rearrange("p a f -> p (a f)").bitcast(F32),
                                op0=ALU.mult, op1=ALU.subtract).then_inc(lo_made, 1)


def slow_path(nc, dims, adj, keep, wh_rows, att_rows, dsh_row, sem, sb, buf, acc, turned):
    F, TILES, FE = dims["F"], dims["TILES"], dims["FE"]
    W = CHUNK * P
    C = dims["N"] // W
    ident, s_all, ext = keep["ident"], keep["s"], keep["ext"]
    nbr = buf["adj"][:, 0, 0, :]
    whc = buf["adj"][:, 1, :, :].rearrange("p s j -> p (s j)").bitcast(F32)[:, 0:CHUNK * FE].rearrange("p (k f) -> p k f", k=CHUNK)
    dsh, wt = buf["r_bc"][:, 0, :], buf["r_bc"][:, 1, :]
    picked, z, lz, ex = (buf["qm"][:, i, :] for i in range(4))
    total = buf["stage"][:, 0, :]
    ps_t = turned[:, 0, :].bitcast(F32)
    mx = sb("sl_mx", [P, C])
    row = sb("sl_row", [P, 6])

    in1, in2, stored = sem("sl_in1"), sem("sl_in2"), sem("sl_stored")
    pick1 = sem("sl_pick1")
    max_done = sem("sl_max_done")
    row_step = sem("sl_row_step")
    z_done, lz_done, ex_done, pick2 = sem("sl_z_done"), sem("sl_lz_done"), sem("sl_ex_done"), sem("sl_pick2")
    turn, wt_done, prod = sem("sl_turn"), sem("sl_wt_done"), sem("sl_prod")
    add_done = sem("sl_add_done")
    zeroed = sem("sl_zeroed")
    settled = sem("sl_settled")

    def sync(sp):
        def load(t, c, signal):
            sp.dma_start(nbr, adj[bass.ds(t * P, P), bass.ds(c * W, W)]).then_inc(signal, 16)
            sp.dma_start(dsh, dsh_row[bass.ds(c * W, W)].partition_broadcast(P)).then_inc(signal, 16)

        with sp.Fori(0, TILES) as t:
            with sp.Fori(0, C) as c:
                sp.wait_ge(max_done, t * C + c + 1)
                sp.sem_inc(settled, 1)
                sp.wait_ge(add_done, t * C + 1)
                sp.sem_inc(settled, 1)
                load(t, c, in1)
            with sp.Fori(0, C) as c:
                sp.wait_ge(max_done, t * C + C + 1)
                sp.sem_inc(settled, 1)
                sp.wait_ge(add_done, t * C + c + 1)
                sp.sem_inc(settled, 1)
                load(t, c, in2)
                sp.dma_start(whc, wh_rows[bass.ds(c * W, W), :].rearrange("(k p) f -> p k f", p=P)).then_inc(in2, 16)
            sp.wait_ge(add_done, t * C + C + 1)
            sp.sem_inc(settled, 1)
            sp.dma_start(att_rows[bass.ds(t * P, P), :], total).then_inc(stored, 16)
        sp.wait_ge(stored, 16 * (TILES + 1))

    def pool(eng):
        eng.sem_inc(stored, 16)
        eng.sem_inc(max_done, 1)
        eng.sem_inc(add_done, 1)
        eng.sem_inc(row_step, 6)

    def tensor(pe):
        with pe.Fori(0, TILES) as t:
            with pe.Fori(0, C) as c:
                n = t * C + c
                pe.wait_ge(pick2, n + 1)
                for k in range(CHUNK):
                    last = nc.tensor.transpose(ps_t[:, k * P:(k + 1) * P], picked[:, k * P:(k + 1) * P], ident[:, :])
                last.then_inc(turn, 1)
                pe.wait_ge(wt_done, n + 1)
                for k in range(CHUNK):
                    last = nc.tensor.matmul(acc[:, 0, 0:FE], wt[:, k * P:(k + 1) * P], whc[:, k, :],
                                            start=(k == 0), stop=(k == CHUNK - 1))
                last.then_inc(prod, 1)

    def scalar(act):
        with act.Fori(0, TILES) as t:
            with act.Fori(0, C) as c:
                act.wait_ge(lz_done, t * C + c + 1)
                nc.scalar.activation(ex, lz, ACT.Exp, bias=row[:, 5:6]).then_inc(ex_done, 1)

    def vector(dve):
        def neighbours(src, signal, count):
            nc.vector.scalar_tensor_tensor(out=picked, in0=nbr, scalar=0.0, in1=src, op0=ALU.is_gt, op1=ALU.mult).then_inc(signal, 1)
            dve.wait_ge(signal, count)

        with dve.Fori(0, TILES) as t:
            with dve.Fori(0, C) as c:
                dve.wait_ge(in1, (t * C + c) * 32 + 32)
                neighbours(dsh, pick1, t * C + c + 1)
                nc.vector.tensor_reduce(mx[:, bass.ds(c, 1)], picked, AX.X, ALU.max).then_inc(max_done, 1)

            def step(i, ins):
                ins.then_inc(row_step, 1)
                dve.wait_ge(row_step, t * 6 + (i + 7))

            dve.wait_ge(max_done, t * C + C + 1)
            step(0, nc.vector.tensor_scalar(row[:, 0:1], s_all[:, bass.ds(t, 1)], ext[:, 1:2], None, ALU.subtract))
            step(1, nc.vector.tensor_reduce(row[:, 1:2], mx[:, :], AX.X, ALU.max))
            step(2, nc.vector.tensor_tensor(row[:, 2:3], row[:, 0:1], row[:, 1:2], ALU.add))
            step(3, nc.vector.tensor_scalar(row[:, 3:4], row[:, 2:3], 1.0, None, ALU.add))
            step(4, nc.vector.scalar_tensor_tensor(out=row[:, 4:5], in0=row[:, 2:3], scalar=SLOPE, in1=row[:, 2:3],
                                                   op0=ALU.mult, op1=ALU.max))
            step(5, nc.vector.tensor_scalar(row[:, 5:6], row[:, 4:5], -1.0, None, ALU.mult))
            dve.wait_ge(stored, t * 16 + 16)
            nc.vector.memset(total, 0.0).then_inc(zeroed, 1)
            with dve.Fori(0, C) as c:
                n = t * C + c
                dve.wait_ge(in2, n * 48 + 48)
                nc.vector.tensor_scalar(z, dsh, row[:, 0:1], row[:, 3:4], ALU.add, ALU.min).then_inc(z_done, 1)
                dve.wait_ge(z_done, n + 1)
                nc.vector.scalar_tensor_tensor(out=lz, in0=z, scalar=SLOPE, in1=z, op0=ALU.mult, op1=ALU.max).then_inc(lz_done, 1)
                dve.wait_ge(ex_done, n + 1)
                neighbours(ex, pick2, n + 1)
                dve.wait_ge(turn, n + 1)
                nc.vector.tensor_copy(wt, ps_t[:, :]).then_inc(wt_done, 1)
                dve.wait_ge(prod, n + 1)
                dve.wait_ge(zeroed, t + 1)
                dve.wait_ge(add_done, n + 1)
                nc.vector.tensor_tensor(total, total, acc[:, 0, 0:FE], ALU.add).then_inc(add_done, 1)

    return dict(sync=sync, pool=pool, tensor=tensor, scalar=scalar, vector=vector)


def fuse(nc, dims, x, w, keep, wh_rows, att_rows, out):
    F, TILES, GROUPS, FE, FK, N = (dims[k] for k in ("F", "TILES", "GROUPS", "FE", "FK", "N"))
    S = w["abp_w"].shape[0]
    DI = w["fe1_w"].shape[1]
    G1 = w["g1_w"].shape[1]
    ident, whsum = keep["ident"], keep["whsum"]
    mats = {n: (w[n], w[n].shape[0] // P, w[n].shape[1])
            for n in ("fe1_w", "W_bcdt", "abp_w", "fe2_w", "W_hz", "out_w", "g1_w", "g2_w")}
    bias_of = {"fe1_w": "fe1_b", "W_bcdt": "b_bcdt", "abp_w": "abp_b", "fe2_w": "fe2_b", "W_hz": "b_hz",
               "out_w": "out_b", "g1_w": "g1_b", "g2_w": "g2_b"}
    bias_at, NB = {}, 0
    for n in mats:
        bias_at[n] = NB
        NB += mats[n][2]
    spread = ("fe_ln_g", "fe_ln_b", "g_ln_g", "g_ln_b", "ln_g", "ln_b")
    LO_ROW = 32

    with ExitStack() as ctx:
        def sb(name, shape, dt=F32):
            return ctx.enter_context(nc.sbuf_tensor(name, shape, dt))

        hi = {n: sb(n + "_hi", [P, k, c], F32R) for n, (_, k, c) in mats.items()}
        lo = {n: sb(n + "_lo", [P, k, c], F32R) for n, (_, k, c) in mats.items()}
        brow = sb("brow", [P, NB], F32R)
        ones = sb("ones_r", [P, P], F32R)
        vec = {n: sb(n + "_bc", [P, w[n].shape[0]]) for n in spread}
        cpw = sb("cpw_bc", [P, S])
        cpb1 = sb("cpb1", [P, 1])
        d2 = sb("d2", [P, 1])
        half = sb("minus_half", [P, 1])
        prepare(nc, w, mats, bias_of, bias_at, NB, LO_ROW, hi, lo, brow, ones, vec, cpw, cpb1, d2, half)

        def rows(name, width, dt=F32):
            return sb(name, [P, STRIPS, width], dt)

        wh, xr, num = rows("wh_in", FE), rows("x_in", F), rows("att_in", FE)
        wht_hi, wht_lo = rows("wht_hi", F, F32R), rows("wht_lo", F, F32R)
        vt_hi, vt_lo = rows("vt_hi", DI, F32R), rows("vt_lo", DI, F32R)
        abt_hi, abt_lo = rows("abt_hi", S, F32R), rows("abt_lo", S, F32R)
        v, th = rows("v", DI), rows("th", DI)
        ab, e = rows("ab", S), rows("e", S)
        hs0 = rows("hs0", F)
        ha, hs, he, fused = rows("ha", F), rows("hs", F), rows("he", F), rows("fused", F)
        tg = rows("tg", F)
        cj = rows("cj", S)
        st = {n: rows("st_" + n, 6) for n in ("fe", "g", "f", "o")}
        mv = {n: rows("mv_" + n, 2) for n in ("fe", "g", "f", "o")}
        ve = {n: rows("ve_" + n, 3) for n in ("fe", "g", "f", "o")}
        sc = rows("sc", 8)
        ps = ctx.enter_context(nc.psum_tensor("ps", [P, 8, 512], F32))

        steps = ["in_wh", "in_x", "in_att",
                 "t_wh", "hi_wh", "lo_wh", "fe1", "fe_st", "fe_mv", "fe_ve", "fe_rs", "fe_nm", "fe_xh", "fe_g", "fe_n", "fe_th", "fe_v",
                 "bc", "mx", "e", "es", "ab", "t_ab", "hi_ab", "lo_ab", "abp", "hs0", "t_fe", "hi_fe", "lo_fe", "fe2", "he",
                 "t_hs0", "hi_hs0", "lo_hs0", "hz_h", "hz_z", "z_th", "w", "u", "t_u", "hi_u", "lo_u", "cd", "c1", "out", "hs",
                 "nn", "ws", "wr", "hn", "ha", "t_co", "hi_co", "lo_co", "g1", "g_st", "g_mv", "g_ve", "g_rs", "g_nm", "g_xh", "g_g", "g_n", "g_th", "g_v",
                 "t_g", "hi_g", "lo_g", "g2", "tg", "dl", "hh", "m", "f", "f_st", "f_mv", "f_ve", "f_rs", "f_nm", "f_xh", "f_g", "f_n", "y",
                 "o_st", "o_mv", "o_ve", "o_rs", "o_nm", "o_out", "settled", "stored"]
        dma_steps = ("in_wh", "in_x", "in_att", "stored")
        sems = {n: ctx.enter_context(nc.semaphore("fu_" + n)) for n in steps if n not in dma_steps}
        for n in dma_steps:
            for s in range(STRIPS):
                sems[n, s] = ctx.enter_context(nc.semaphore(f"fu_{n}{s}"))

        class Strip:
            def __init__(self, eng, g, s):
                self.eng, self.g, self.s = eng, g, s

            def need(self, *names):
                for n in names:
                    if n in dma_steps:
                        self.eng.wait_ge(sems[n, self.s], self.g * 16 + 32)
                    else:
                        self.eng.wait_ge(sems[n], self.g * STRIPS + (self.s + 1 + STRIPS))

            def free(self, *names):
                for n in names:
                    if n in dma_steps:
                        self.eng.wait_ge(sems[n, self.s], self.g * 16 + 16)
                    else:
                        self.eng.wait_ge(sems[n], self.g * STRIPS + (self.s + 1))

            def settle(self):
                self.eng.sem_inc(sems["settled"], 1)

            def done(self, name, ins):
                if name in dma_steps:
                    ins.then_inc(sems[name, self.s], 16)
                else:
                    ins.then_inc(sems[name], 1)

        with nc.Block() as block:
            @block.sync
            def _(sp):
                for n in steps:
                    if n in dma_steps:
                        for s in range(STRIPS):
                            sp.sem_inc(sems[n, s], 16)
                    else:
                        sp.sem_inc(sems[n], STRIPS)

        xg = x.rearrange("(g s p) f -> g s p f", s=STRIPS, p=P)
        whg = wh_rows.rearrange("(g s p) f -> g s p f", s=STRIPS, p=P)
        attg = att_rows.rearrange("(g s p) f -> g s p f", s=STRIPS, p=P)
        outg = out.rearrange("(g s p) f -> g s p f", s=STRIPS, p=P)

        with nc.Block() as block:
            @block.sync
            def _(sp):
                with sp.Fori(0, GROUPS) as g:
                    for s in range(STRIPS):
                        k = Strip(sp, g, s)
                        k.free("hs0", "t_wh")
                        k.done("in_wh", sp.dma_start(wh[:, s, :], whg[bass.ds(g, 1), s].rearrange("g p f -> (g p) f")))
                    for s in range(STRIPS):
                        k = Strip(sp, g, s)
                        k.free("hn", "wr")
                        k.done("in_att", sp.dma_start(num[:, s, :], attg[bass.ds(g, 1), s].rearrange("g p f -> (g p) f")))
                    for s in range(STRIPS):
                        k = Strip(sp, g, s)
                        k.free("y")
                        k.done("in_x", sp.dma_start(xr[:, s, :], xg[bass.ds(g, 1), s].rearrange("g p f -> (g p) f")))

            half_of = dict(t_wh=0, fe1=1, bc=0, t_fe=1, fe2=0, t_ab=1, abp=0, t_hs0=1, hz_h=0, hz_z=1, t_u=0, out=1,
                           t_co=0, g1=1, t_g=0, g2=1)

            def bank(name, k):
                return ps[:, half_of[name] * STRIPS + k.s, :]

            def blocks(t, k, n):
                return [t[:, k.s, i * P:(i + 1) * P] for i in range(n)]

            @block.tensor
            def _(pe):
                def turn(k, name, parts):
                    for i, b in enumerate(parts):
                        last = nc.tensor.transpose(bank(name, k)[:, i * P:(i + 1) * P], b, ident[:, :])
                    k.done(name, last)

                def product(k, name, mat, left_hi, left_lo, c0=0, c1=None):
                    _, nk, nc_ = mats[mat]
                    c1 = nc_ if c1 is None else c1
                    o = bank(name, k)[:, 0:c1 - c0]
                    nc.tensor.matmul(o, ones[:, :], brow[:, bias_at[mat] + c0:bias_at[mat] + c1], start=True, stop=False)
                    for i in range(nk):
                        a_hi, a_lo = left_hi[:, k.s, i * P:(i + 1) * P], left_lo[:, k.s, i * P:(i + 1) * P]
                        nc.tensor.matmul(o, a_hi, hi[mat][:, i, c0:c1], start=False, stop=False)
                        nc.tensor.matmul(o, a_hi, lo[mat][:, i, c0:c1], start=False, stop=False)
                        last = nc.tensor.matmul(o, a_lo, hi[mat][:, i, c0:c1], start=False, stop=i == nk - 1)
                    k.done(name, last)

                def t_wh(k):
                    k.need("in_wh")
                    k.free("lo_g")
                    turn(k, "t_wh", blocks(wh, k, FK))

                def fe1(k):
                    k.need("lo_wh")
                    k.free("tg")
                    product(k, "fe1", "fe1_w", wht_hi, wht_lo)

                def bc(k):
                    product(k, "bc", "W_bcdt", wht_hi, wht_lo)

                def t_fe(k):
                    k.need("fe_v")
                    turn(k, "t_fe", blocks(v, k, DI // P))

                def fe2(k):
                    k.need("lo_fe", "ab")
                    product(k, "fe2", "fe2_w", vt_hi, vt_lo)

                def t_ab(k):
                    turn(k, "t_ab", [ab[:, k.s, :]])

                def abp(k):
                    k.need("lo_ab", "he")
                    product(k, "abp", "abp_w", abt_hi, abt_lo)

                def t_hs0(k):
                    k.need("hs0")
                    turn(k, "t_hs0", blocks(hs0, k, FK))

                def hz(k):
                    k.need("lo_hs0")
                    product(k, "hz_h", "W_hz", wht_hi, wht_lo, 0, DI)
                    product(k, "hz_z", "W_hz", wht_hi, wht_lo, DI, 2 * DI)

                def t_u(k):
                    k.need("u")
                    turn(k, "t_u", blocks(v, k, DI // P))

                def out_(k):
                    k.need("lo_u")
                    product(k, "out", "out_w", vt_hi, vt_lo)

                def t_co(k):
                    k.need("hs", "ha")
                    turn(k, "t_co", blocks(ha, k, FK) + blocks(hs, k, FK))

                def g1(k):
                    k.need("lo_co")
                    product(k, "g1", "g1_w", vt_hi, vt_lo)

                def t_g(k):
                    k.need("g_v")
                    turn(k, "t_g", blocks(v, k, G1 // P))

                def g2(k):
                    k.need("lo_g")
                    product(k, "g2", "g2_w", vt_hi, vt_lo)

                with pe.Fori(0, GROUPS) as g:
                    a, b, c, d = (Strip(pe, g, s) for s in range(STRIPS))
                    t_wh(a), t_wh(b), fe1(a), t_wh(c), fe1(b), t_wh(d), fe1(c), fe1(d)
                    bc(a), bc(b), bc(c), t_fe(a), bc(d), t_fe(b)
                    fe2(a), t_ab(a), t_fe(c), fe2(b), t_ab(b), t_fe(d), abp(a), fe2(c), t_ab(c), abp(b)
                    t_hs0(a), fe2(d), t_ab(d), abp(c), t_hs0(b)
                    hz(a), abp(d), t_hs0(c), hz(b), t_hs0(d), hz(c), t_u(a), hz(d), t_u(b)
                    out_(a), t_u(c), out_(b), t_u(d), out_(c), t_co(a), out_(d), t_co(b)
                    g1(a), t_co(c), g1(b), t_co(d), g1(c), t_g(a), g1(d)
                    g2(a), t_g(b), g2(b), t_g(c), g2(c), t_g(d), g2(d)

            @block.scalar
            def _(act):
                def high(k, name, dst, width, scale=1.0):
                    k.need("t_" + name)
                    k.done("hi_" + name, nc.scalar.activation(dst[:, k.s, 0:width], bank("t_" + name, k)[:, 0:width], ACT.Copy, scale=scale))

                def normal(k, n, dst, src):
                    k.need(n + "_nm")
                    k.done({"fe": "fe_xh", "g": "g_xh", "f": "f_xh", "o": "o_out"}[n],
                           nc.scalar.activation(dst, src, ACT.Identity, scale=ve[n][:, k.s, 1:2], bias=ve[n][:, k.s, 2:3]))

                def hi_wh(k):
                    k.free("hz_z")
                    high(k, "wh", wht_hi, F)

                def fe_xh(k):
                    k.free("t_g")
                    normal(k, "fe", v[:, k.s, :], bank("fe1", k))

                def e_(k):
                    k.need("mx")
                    k.done("e", nc.scalar.activation(e[:, k.s, :], bank("bc", k)[:, 2 * S:3 * S], ACT.Exp,
                                                     bias=sc[:, k.s, 0:1], accum_out=sc[:, k.s, 1:2]))

                def fe_th(k):
                    k.need("fe_n")
                    k.done("fe_th", nc.scalar.activation(th[:, k.s, :], v[:, k.s, :], ACT.Tanh, scale=0.5))

                def hi_fe(k):
                    k.free("g2")
                    high(k, "fe", vt_hi, DI, 0.5)

                def hi_ab(k):
                    high(k, "ab", abt_hi, S)

                def he_(k):
                    k.need("fe2")
                    k.free("f")
                    k.done("he", nc.scalar.copy(he[:, k.s, :], bank("fe2", k)[:, 0:F]))

                def hi_hs0(k):
                    high(k, "hs0", wht_hi, F)

                def z_th(k):
                    k.need("hz_z", "fe_v")
                    k.done("z_th", nc.scalar.activation(th[:, k.s, :], bank("hz_z", k), ACT.Tanh, scale=0.5))

                def hi_u(k):
                    high(k, "u", vt_hi, DI, 0.5)

                def hs_(k):
                    k.need("out", "c1")
                    k.done("hs", nc.scalar.activation(hs[:, k.s, :], bank("out", k)[:, 0:F], ACT.Copy, scale=sc[:, k.s, 4:5]))

                def hi_co(k):
                    high(k, "co", vt_hi, G1)

                def g_xh(k):
                    normal(k, "g", v[:, k.s, :], bank("g1", k))

                def g_th(k):
                    k.need("g_n")
                    k.done("g_th", nc.scalar.activation(th[:, k.s, :], v[:, k.s, :], ACT.Tanh, scale=0.5))

                def hi_g(k):
                    high(k, "g", vt_hi, G1, 0.5)

                def tg_(k):
                    k.need("g2")
                    k.free("m")
                    k.done("tg", nc.scalar.activation(tg[:, k.s, :], bank("g2", k)[:, 0:F], ACT.Tanh, scale=0.5))

                def f_xh(k):
                    normal(k, "f", fused[:, k.s, :], fused[:, k.s, :])

                def store(k):
                    normal(k, "o", fused[:, k.s, :], fused[:, k.s, :])
                    k.need("o_out")
                    k.done("stored", act.dma_start(outg[bass.ds(k.g, 1), k.s].rearrange("g p f -> (g p) f"), fused[:, k.s, :]))

                def body(g, tail):
                    a, b, c, d = (Strip(act, g, s) for s in range(STRIPS))
                    prev = [Strip(act, g - 1, s) for s in range(STRIPS)]

                    def last(step, i):
                        if tail:
                            step(prev[i])

                    hi_wh(a), hi_wh(b), hi_wh(c), hi_wh(d)
                    fe_xh(a), fe_xh(b), fe_xh(c), fe_th(a), fe_xh(d)
                    e_(a), fe_th(b), e_(b), last(f_xh, 0), fe_th(c), e_(c), hi_fe(a), fe_th(d), e_(d), last(f_xh, 1)
                    hi_fe(b), he_(a), hi_ab(a), hi_fe(c), he_(b), hi_ab(b), hi_fe(d), he_(c), hi_ab(c), hi_hs0(a)
                    he_(d), hi_ab(d), hi_hs0(b), z_th(a), hi_hs0(c), last(f_xh, 2), z_th(b), hi_hs0(d), last(f_xh, 3), z_th(c), hi_u(a), z_th(d), hi_u(b)
                    hs_(a), hi_u(c), hs_(b), hi_u(d), hs_(c), hi_co(a), hs_(d), hi_co(b)
                    hi_co(c), last(store, 0), g_xh(a), hi_co(d), last(store, 1), g_th(a), g_xh(b), last(store, 2), g_th(b), g_xh(c), hi_g(a), last(store, 3), g_th(c), g_xh(d)
                    hi_g(b), tg_(a), g_th(d), hi_g(c), tg_(b), hi_g(d), tg_(c), tg_(d)

                body(0, False)
                with act.Fori(1, GROUPS) as g:
                    body(g, True)
                for s in range(STRIPS):
                    f_xh(Strip(act, GROUPS - 1, s))
                for s in range(STRIPS):
                    store(Strip(act, GROUPS - 1, s))
                for s in range(STRIPS):
                    act.wait_ge(sems["stored", s], 16 * (GROUPS + 1))

            @block.gpsimd
            def _(pool):
                def inverse_std(k, n):
                    k.need(n + "_mv")
                    k.settle()
                    k.done(n + "_ve", nc.gpsimd.tensor_scalar(ve[n][:, k.s, 0:1], mv[n][:, k.s, 1:2], EPS, None, ALU.add))
                    k.need(n + "_ve")
                    k.done(n + "_rs", nc.gpsimd.tensor_tensor(ve[n][:, k.s, 1:2], ve[n][:, k.s, 0:1], half[:, :], ALU.pow))
                    k.need(n + "_rs")
                    k.settle()
                    k.done(n + "_nm", nc.gpsimd.tensor_scalar(ve[n][:, k.s, 2:3], mv[n][:, k.s, 0:1], ve[n][:, k.s, 1:2], -1.0,
                                                              ALU.mult, ALU.mult))

                def fe_n(k):
                    k.need("fe_g")
                    k.done("fe_n", nc.gpsimd.tensor_tensor(v[:, k.s, :], v[:, k.s, :], vec["fe_ln_b"][:, :], ALU.add))

                def f_n(k):
                    k.need("f_g")
                    k.done("f_n", nc.gpsimd.tensor_tensor(fused[:, k.s, :], fused[:, k.s, :], vec["ln_b"][:, :], ALU.add))

                def y(k):
                    k.need("f_n", "in_x")
                    k.done("y", nc.gpsimd.tensor_tensor(fused[:, k.s, :], fused[:, k.s, :], xr[:, k.s, :], ALU.add))

                def differences(k):
                    k.need("hs", "ha", "he", "t_co")
                    k.done("dl", nc.gpsimd.tensor_tensor(ha[:, k.s, :], ha[:, k.s, :], hs[:, k.s, :], ALU.subtract))
                    k.done("hh", nc.gpsimd.tensor_tensor(he[:, k.s, :], he[:, k.s, :], hs[:, k.s, :], ALU.add))

                def body(g, tail):
                    a, b, c, d = (Strip(pool, g, s) for s in range(STRIPS))
                    prev = [Strip(pool, g - 1, s) for s in range(STRIPS)] if tail else []
                    inverse_std(a, "fe"), inverse_std(b, "fe"), fe_n(a), inverse_std(c, "fe"), fe_n(b), inverse_std(d, "fe"), fe_n(c), fe_n(d)
                    for k in prev:
                        inverse_std(k, "f")
                    for k in prev:
                        f_n(k), y(k)
                    for k in prev:
                        inverse_std(k, "o")
                    differences(a), differences(b)
                    inverse_std(a, "g"), differences(c), inverse_std(b, "g"), differences(d), inverse_std(c, "g"), inverse_std(d, "g")

                body(0, False)
                with pool.Fori(1, GROUPS) as g:
                    body(g, True)
                prev = [Strip(pool, GROUPS - 1, s) for s in range(STRIPS)]
                for k in prev:
                    inverse_std(k, "f")
                for k in prev:
                    f_n(k), y(k)
                for k in prev:
                    inverse_std(k, "o")

            @block.vector
            def _(dve):
                def low(k, name, dst, hi_t, width, scale=1.0):
                    k.need("hi_" + name)
                    k.done("lo_" + name, nc.vector.scalar_tensor_tensor(
                        out=dst[:, k.s, 0:width], in0=bank("t_" + name, k)[:, 0:width], scalar=scale,
                        in1=hi_t[:, k.s, 0:width].bitcast(F32), op0=ALU.mult, op1=ALU.subtract))

                def moments(k, n, made, src):
                    k.need(made)
                    k.done(n + "_st", nc.vector.bn_stats(st[n][:, k.s, :], src))

                def mean_var(k, n):
                    k.need(n + "_st")
                    k.settle()
                    k.done(n + "_mv", nc.vector.bn_aggr(mv[n][:, k.s, :], st[n][:, k.s, :]))

                def gain(k, n, t, by):
                    k.need(n + "_xh")
                    k.done(n + "_g", nc.vector.tensor_tensor(t[:, k.s, :], t[:, k.s, :], vec[by][:, :], ALU.mult))

                def twice_silu(k, n):
                    k.need(n + "_th")
                    k.done(n + "_v", nc.vector.scalar_tensor_tensor(out=v[:, k.s, :], in0=th[:, k.s, :], scalar=1.0, in1=v[:, k.s, :],
                                                                    op0=ALU.add, op1=ALU.mult))

                def lo_wh(k):
                    low(k, "wh", wht_lo, wht_hi, F)

                def fe_st(k):
                    moments(k, "fe", "fe1", bank("fe1", k))

                def fe_mv(k):
                    mean_var(k, "fe")

                def fe_g(k):
                    gain(k, "fe", v, "fe_ln_g")

                def mx(k):
                    k.need("bc")
                    k.done("mx", nc.vector.tensor_reduce(sc[:, k.s, 0:1], bank("bc", k)[:, 2 * S:3 * S], AX.X, ALU.max, negate=True))

                def c_dot(k):
                    k.need("e")
                    k.free("cd")
                    k.done("cd", nc.vector.scalar_tensor_tensor(out=cj[:, k.s, :], in0=bank("bc", k)[:, S:2 * S], scalar=1.0, in1=cpw[:, :],
                                                                op0=ALU.mult, op1=ALU.mult, accum_out=sc[:, k.s, 3:4]))

                def ab_(k):
                    k.done("es", nc.vector.reciprocal(sc[:, k.s, 2:3], sc[:, k.s, 1:2]))
                    k.need("es")
                    k.done("ab", nc.vector.scalar_tensor_tensor(out=ab[:, k.s, :], in0=e[:, k.s, :], scalar=sc[:, k.s, 2:3],
                                                                in1=bank("bc", k)[:, 0:S], op0=ALU.mult, op1=ALU.mult))

                def c1(k):
                    k.need("cd")
                    k.done("c1", nc.vector.tensor_tensor(sc[:, k.s, 4:5], sc[:, k.s, 3:4], cpb1[:, :], ALU.add))

                def fe_v(k):
                    twice_silu(k, "fe")

                def lo_fe(k):
                    low(k, "fe", vt_lo, vt_hi, DI, 0.5)

                def lo_ab(k):
                    low(k, "ab", abt_lo, abt_hi, S)

                def hs0_(k):
                    k.need("abp")
                    k.done("hs0", nc.vector.tensor_tensor(hs0[:, k.s, :], bank("abp", k)[:, 0:F], wh[:, k.s, 0:F], ALU.mult))

                def lo_hs0(k):
                    low(k, "hs0", wht_lo, wht_hi, F)

                def attention(ks):
                    for k in ks:
                        k.need("in_att")
                        k.done("nn", nc.vector.tensor_scalar(sc[:, k.s, 5:6], num[:, k.s, F:F + 1], 0.0, None, ALU.is_equal))
                    for k in ks:
                        k.need("nn")
                        k.done("ws", nc.vector.scalar_tensor_tensor(out=sc[:, k.s, 6:7], in0=sc[:, k.s, 5:6], scalar=float(N),
                                                                    in1=num[:, k.s, F:F + 1], op0=ALU.mult, op1=ALU.add))
                    for k in ks:
                        k.need("ws")
                        k.done("wr", nc.vector.reciprocal(sc[:, k.s, 7:8], sc[:, k.s, 6:7]))
                    for k in ks:
                        k.done("hn", nc.vector.scalar_tensor_tensor(out=ha[:, k.s, :], in0=whsum[:, :], scalar=sc[:, k.s, 5:6],
                                                                    in1=num[:, k.s, 0:F], op0=ALU.mult, op1=ALU.add))
                    for k in ks:
                        k.need("wr", "hn")
                        k.done("ha", nc.vector.tensor_scalar(ha[:, k.s, :], ha[:, k.s, :], sc[:, k.s, 7:8], None, ALU.mult))

                def u_(k):
                    k.need("z_th")
                    k.done("w", nc.vector.scalar_tensor_tensor(out=v[:, k.s, :], in0=th[:, k.s, :], scalar=1.0, in1=bank("hz_z", k),
                                                               op0=ALU.add, op1=ALU.mult))
                    k.need("w")
                    k.done("u", nc.vector.scalar_tensor_tensor(out=v[:, k.s, :], in0=v[:, k.s, :], scalar=d2[:, :], in1=bank("hz_h", k),
                                                               op0=ALU.add, op1=ALU.mult))

                def lo_u(k):
                    low(k, "u", vt_lo, vt_hi, DI, 0.5)

                def lo_co(k):
                    low(k, "co", vt_lo, vt_hi, G1)

                def g_st(k):
                    moments(k, "g", "g1", bank("g1", k))

                def g_mv(k):
                    mean_var(k, "g")

                def g_gn(k):
                    gain(k, "g", v, "g_ln_g")
                    k.need("g_g")
                    k.done("g_n", nc.vector.tensor_tensor(v[:, k.s, :], v[:, k.s, :], vec["g_ln_b"][:, :], ALU.add))

                def g_v(k):
                    twice_silu(k, "g")

                def lo_g(k):
                    low(k, "g", vt_lo, vt_hi, G1, 0.5)

                def m(k):
                    k.need("tg", "dl")
                    k.done("m", nc.vector.scalar_tensor_tensor(out=tg[:, k.s, :], in0=tg[:, k.s, :], scalar=1.0, in1=ha[:, k.s, :],
                                                               op0=ALU.add, op1=ALU.mult))

                def f(k):
                    k.need("m", "hh")
                    k.free("stored")
                    k.done("f", nc.vector.scalar_tensor_tensor(out=fused[:, k.s, :], in0=tg[:, k.s, :], scalar=0.5, in1=he[:, k.s, :],
                                                               op0=ALU.mult, op1=ALU.add))

                def f_st(k):
                    moments(k, "f", "f", fused[:, k.s, :])

                def f_mv(k):
                    mean_var(k, "f")

                def f_g(k):
                    gain(k, "f", fused, "ln_g")

                def o_st(k):
                    moments(k, "o", "y", fused[:, k.s, :])

                def o_mv(k):
                    mean_var(k, "o")

                def body(g, tail):
                    a, b, c, d = (Strip(dve, g, s) for s in range(STRIPS))
                    prev = [Strip(dve, g - 1, s) for s in range(STRIPS)]

                    def last(step, *of):
                        for i in of if tail else ():
                            step(prev[i])

                    lo_wh(a), lo_wh(b), last(m, 0), lo_wh(c), last(m, 1), lo_wh(d)
                    fe_st(a), fe_mv(a), last(m, 2), fe_st(b), fe_mv(b), fe_g(a), fe_st(c), fe_mv(c), fe_g(b), last(m, 3)
                    fe_st(d), fe_mv(d), fe_g(c), mx(a), last(f, 0), fe_g(d), mx(b), last(f, 1), last(f_st, 0), c_dot(a), ab_(a)
                    mx(c), fe_v(a), last(f, 2), last(f_st, 1), last(f_mv, 0, 1), c_dot(b), ab_(b), fe_v(b), last(f, 3), mx(d), lo_fe(a)
                    c_dot(c), ab_(c), fe_v(c), lo_fe(b), lo_ab(a), c_dot(d), ab_(d), fe_v(d), lo_fe(c), lo_ab(b), hs0_(a), last(f_st, 2, 3), last(f_mv, 2, 3), lo_fe(d)
                    lo_ab(c), hs0_(b), lo_hs0(a), lo_ab(d), hs0_(c), lo_hs0(b), hs0_(d), lo_hs0(c), lo_hs0(d)
                    c1(a), c1(b), c1(c), c1(d)
                    last(f_g, 0, 1), u_(a), last(f_g, 2, 3), u_(b), lo_u(a), attention([a, b]), u_(c), lo_u(b), u_(d)
                    lo_u(c), attention([c, d]), lo_u(d), last(o_st, 0), last(o_mv, 0), lo_co(a), last(o_st, 1), last(o_mv, 1), lo_co(b), lo_co(c)
                    last(o_st, 2, 3), last(o_mv, 2, 3), g_st(a), g_mv(a), lo_co(d)
                    g_gn(a), g_st(b), g_mv(b), g_v(a), g_gn(b), g_st(c), g_mv(c), g_v(b), lo_g(a), g_gn(c), g_st(d), g_mv(d), g_v(c), lo_g(b), g_gn(d)
                    g_v(d), lo_g(c), lo_g(d)

                body(0, False)
                with dve.Fori(1, GROUPS) as g:
                    body(g, True)
                prev = [Strip(dve, GROUPS - 1, s) for s in range(STRIPS)]
                for step in (m, f, f_st, f_mv, f_g, o_st, o_mv):
                    for k in prev:
                        step(k)


def prepare(nc, w, mats, bias_of, bias_at, NB, LO_ROW, hi, lo, brow, ones, vec, cpw, cpb1, d2, half):
    WIDE = max(k * c for _, k, c in mats.values())
    SLOTS = 2
    with ExitStack() as ctx:
        def sb(name, shape, dt=F32):
            return ctx.enter_context(nc.sbuf_tensor(name, shape, dt))

        def sem(name):
            return ctx.enter_context(nc.semaphore(name))

        raw = sb("raw", [P, SLOTS, WIDE])
        braw = sb("braw", [LO_ROW + 1, NB])
        bhi = sb("bhi", [LO_ROW + 1, NB], F32R)
        small = sb("small", [P, 2])
        araw = sb("araw", [LO_ROW + 1, cpw.shape[1]])
        raw_in = [sem(f"wp_raw_in{k}") for k in range(SLOTS)]
        vec_in = sem("wp_vec_in")
        bias_in = sem("wp_bias_in")
        cleared = sem("wp_cleared")
        hi_made = sem("wp_hi_made")
        lo_made = sem("wp_lo_made")
        bias_hi = sem("wp_bias_hi")
        summed = sem("wp_summed")
        done = sem("wp_done")
        S = cpw.shape[1]
        DT = bias_at["W_bcdt"] + 2 * S
        n_vec = len(vec) + 3
        n_bias = 2 * len(mats) + 2
        with nc.Block() as block:
            @block.sync
            def _(sp):
                for i, (n, (m, k, c)) in enumerate(mats.items()):
                    if i >= SLOTS:
                        sp.wait_ge(lo_made, i - SLOTS + 1)
                    sp.dma_start(raw[:, i % SLOTS, 0:k * c].rearrange("p (k c) -> p k c", k=k),
                                 m.rearrange("(k p) c -> p k c", p=P)).then_inc(raw_in[i % SLOTS], 16)

            @block.scalar
            def _(act):
                for n in mats:
                    row = w[bias_of[n]].rearrange("(o c) -> o c", o=1)
                    at = slice(bias_at[n], bias_at[n] + mats[n][2])
                    for r in (0, LO_ROW):
                        act.dma_start(braw[r:r + 1, at], row).then_inc(bias_in, 16)
                for r in (0, LO_ROW):
                    act.dma_start(araw[r:r + 1, :], w["A"].rearrange("(o c) -> o c", o=1)).then_inc(bias_in, 16)
                for n, t in vec.items():
                    act.dma_start(t[:, :], w[n].partition_broadcast(P)).then_inc(vec_in, 16)
                act.dma_start(cpw[:, :], w["cp_w"].rearrange("s o -> (s o)").partition_broadcast(P)).then_inc(vec_in, 16)
                act.dma_start(small[:, 0:1], w["cp_b"].partition_broadcast(P)).then_inc(vec_in, 16)
                act.dma_start(small[:, 1:2], w["D"].partition_broadcast(P)).then_inc(vec_in, 16)
                for i, (n, (m, k, c)) in enumerate(mats.items()):
                    act.wait_ge(raw_in[i % SLOTS], 16 * (i // SLOTS + 1))
                    nc.scalar.copy(hi[n][:, :, :].rearrange("p k c -> p (k c)"), raw[:, i % SLOTS, 0:k * c]).then_inc(hi_made, 1)
                act.wait_ge(summed, 2)
                act.wait_ge(cleared, 1)
                nc.scalar.copy(brow[0:1, :], braw[0:1, :]).then_inc(bias_hi, 1)
                nc.scalar.copy(bhi[LO_ROW:LO_ROW + 1, :], braw[LO_ROW:LO_ROW + 1, :]).then_inc(bias_hi, 1)

            @block.gpsimd
            def _(pool):
                nc.gpsimd.memset(brow[:, :].bitcast(F32), 0.0).then_inc(cleared, 1)
                nc.gpsimd.memset(half[:, :], -0.5).then_inc(cleared, 1)

            @block.vector
            def _(dve):
                nc.vector.memset(ones[:, :].bitcast(F32), 1.0).then_inc(done, 1)
                for i, (n, (m, k, c)) in enumerate(mats.items()):
                    dve.wait_ge(hi_made, i + 1)
                    nc.vector.tensor_tensor(lo[n][:, :, :].rearrange("p k c -> p (k c)"), raw[:, i % SLOTS, 0:k * c],
                                            hi[n][:, :, :].rearrange("p k c -> p (k c)").bitcast(F32), ALU.subtract).then_inc(lo_made, 1)
                dve.wait_ge(bias_in, 16 * n_bias)
                for r in (0, LO_ROW):
                    nc.vector.tensor_tensor(braw[r:r + 1, DT:DT + S], braw[r:r + 1, DT:DT + S], araw[r:r + 1, :], ALU.add).then_inc(summed, 1)
                dve.wait_ge(vec_in, 16 * n_vec)
                nc.vector.tensor_scalar(cpb1[:, :], small[:, 0:1], 1.0, None, ALU.add).then_inc(done, 1)
                nc.vector.tensor_scalar(d2[:, :], small[:, 1:2], 2.0, None, ALU.mult).then_inc(done, 1)
                dve.wait_ge(bias_hi, 2)
                nc.vector.tensor_tensor(brow[LO_ROW:LO_ROW + 1, :], braw[LO_ROW:LO_ROW + 1, :], bhi[LO_ROW:LO_ROW + 1, :].bitcast(F32),
                                        ALU.subtract).then_inc(done, 1)


_W = ["W", "a_src", "a_dst", "W_bcdt", "b_bcdt", "abp_w", "abp_b", "cp_w", "cp_b", "W_hz", "b_hz", "out_w", "out_b",
      "fe1_w", "fe1_b", "fe_ln_g", "fe_ln_b", "fe2_w", "fe2_b", "A", "D", "g1_w", "g1_b", "g_ln_g", "g_ln_b", "g2_w",
      "g2_b", "ln_g", "ln_b"]


def kernel(**inputs):
    import numpy as _np
    import concourse.bacc as _bacc
    from concourse import mybir as _mybir
    from concourse.bass_utils import run_bass_kernel_spmd as _run

    nc = _bacc.Bacc("TRN2", target_bir_lowering=False, num_devices=1)
    arrays, aps = {}, {}
    for name in ["x", "adj"] + ["L0_gnn_" + n for n in _W]:
        a = _np.ascontiguousarray(inputs[name])
        arrays[f"in_{name}"] = a
        aps[name] = nc.dram_tensor(f"in_{name}", a.shape, _mybir.dt.from_np(a.dtype), kind="ExternalInput").ap()
    out = nc.dram_tensor("out_0", aps["x"].shape, _mybir.dt.float32, kind="ExternalOutput").ap()
    build(nc, aps["x"], aps["adj"], {n: aps["L0_gnn_" + n] for n in _W}, out)
    r = _run(nc, [arrays], core_ids=[0])
    return r.results[0]["out_0"]
```

```python
from contextlib import ExitStack

import concourse.bass as bass
from concourse import mybir

F32 = mybir.dt.float32
F32R = mybir.dt.float32r
BF16 = mybir.dt.bfloat16
I32 = mybir.dt.int32
ALU = mybir.AluOpType
ACT = mybir.ActivationFunctionType
AX = mybir.AxisListType
RED = bass.bass_isa.ReduceOp

P = 128
SLOPE = 0.2
EPS = 1e-5
RANGE_MAX = 64.0
STRIPS = 4
ROWS = STRIPS * P
CHUNK = 4


def build(nc, x, adj, w, out):
    N, F = x.shape
    TILES = N // P
    GROUPS = N // ROWS
    FK = F // P
    FE = F + 2
    NCH = TILES // CHUNK
    with ExitStack() as ctx:
        dims = dict(N=N, F=F, TILES=TILES, GROUPS=GROUPS, FK=FK, FE=FE, NCH=NCH)
        wh_rows = nc.dram_tensor("wh_rows", [N, FE], F32, kind="Internal").ap()
        att_rows = nc.dram_tensor("att_rows", [N, FE], F32, kind="Internal").ap()
        r_row = nc.dram_tensor("r_row", [N], F32, kind="Internal").ap()
        dsh_row = nc.dram_tensor("dsh_row", [N], F32, kind="Internal").ap()

        def sb(name, shape, dt=F32):
            return ctx.enter_context(nc.sbuf_tensor(name, shape, dt))

        keep = dict(
            ident=sb("ident", [P, P]), identb=sb("identb", [P, P], BF16),
            s=sb("s_all", [P, TILES]), d=sb("d_all", [P, TILES]),
            q=sb("q_all", [P, TILES]), f=sb("f_all", [P, TILES]),
            ext=sb("ext", [P, 2]), flag=sb("flag", [P, 1], I32), whsum=sb("whsum", [P, F]),
        )
        with ExitStack() as parts:
            with nc.sbuf_tensor("wh_all", [P, TILES, FE], F32, side="right") as wh_all:
                project(nc, dims, x, w, keep, wh_all, wh_rows, r_row, dsh_row)
                g_hi, g_lo = (parts.enter_context(nc.sbuf_tensor(n, [P, TILES, FE], F32R)) for n in ("g_hi", "g_lo"))
                split_parts(nc, dims, keep, wh_all, g_hi, g_lo)
            attend(nc, dims, adj, keep, g_hi, g_lo, wh_rows, att_rows, r_row, dsh_row)
        fuse(nc, dims, x, w, keep, wh_rows, att_rows, out)


def clear(nc, sems):
    with nc.Block() as block:
        @block.sync
        def _(sp):
            for s in sems:
                sp.sem_clear(s)


def project(nc, dims, x, w, keep, wh, wh_rows, r_row, dsh_row):
    F, TILES, FK = dims["F"], dims["TILES"], dims["FK"]
    LOAD = 8
    BODY = 2 * LOAD
    SLOTS = 4
    STEPS = TILES // BODY
    ident, identb, s_all, d_all = keep["ident"], keep["identb"], keep["s"], keep["d"]
    q_all, f_all, ext, flag, whsum = keep["q"], keep["f"], keep["ext"], keep["flag"], keep["whsum"]
    with ExitStack() as ctx:
        def sb(name, shape, dt=F32):
            return ctx.enter_context(nc.sbuf_tensor(name, shape, dt))

        sems = []

        def sem(name):
            sems.append(ctx.enter_context(nc.semaphore(name)))
            return sems[-1]

        w_sb = sb("w_sb", [P, FK, F])
        a_bc = sb("a_bc", [P, 2, F])
        xin = sb("xin", [P, BODY, F])
        xt = sb("xt", [P, SLOTS, FK, P])
        junk = sb("junk", [P, SLOTS, 2, F])
        wsum = sb("wsum", [P, F])
        ones = sb("ones", [P, P])
        loc = sb("loc", [P, 3])
        bias = sb("bias", [P, 2])
        rarg = sb("rarg", [P, 2, TILES])
        rd = sb("rd", [P, 2, TILES])
        rdt = sb("rdt", [P, P])
        rng = sb("rng", [P, 1])
        ps_x = ctx.enter_context(nc.psum_tensor("ps_x", [P, SLOTS, 512], F32))
        ps_w = ctx.enter_context(nc.psum_tensor("ps_w", [P, SLOTS, 512], F32))
        ps_r, ps_s = ps_x[:, 0, :], ps_w[:, 0, :]

        weights_in = sem("pr_weights_in")
        x_in = [sem(f"pr_x_in{k}") for k in range(2)]
        cleared = sem("pr_cleared")
        ident_ready = sem("pr_ident_ready")
        x_turned = sem("pr_x_turned")
        xt_ready = sem("pr_xt_ready")
        wh_made = sem("pr_wh_made")
        wh_ready = sem("pr_wh_ready")
        sd_done = sem("pr_sd_done")
        sum_done = sem("pr_sum_done")
        wh_stored = sem("pr_wh_stored")
        stat = sem("pr_stat")
        ext_ready = sem("pr_ext_ready")
        bias_ready = sem("pr_bias_ready")
        rarg_ready = sem("pr_rarg_ready")
        exp_done = sem("pr_exp_done")
        rd_turned = sem("pr_rd_turned")
        sum_spread = sem("pr_sum_spread")
        rdt_ready = sem("pr_rdt_ready")
        r_stored = sem("pr_r_stored")

        with nc.Block() as block:
            @block.sync
            def _(sp):
                sp.dma_start(w_sb[:, :, :], w["W"].rearrange("(k p) n -> p k n", p=P)).then_inc(weights_in, 16)
                sp.dma_start(a_bc[:, 0, :], w["a_src"].rearrange("f o -> (f o)").partition_broadcast(P)).then_inc(weights_in, 16)
                sp.dma_start(a_bc[:, 1, :], w["a_dst"].rearrange("f o -> (f o)").partition_broadcast(P)).then_inc(weights_in, 16)
                xv = x.rearrange("(b t p) f -> b p t f", t=LOAD, p=P)
                whv = wh_rows.rearrange("(b t p) f -> b p t f", t=LOAD, p=P)
                for h in range(2):
                    sp.dma_start(xin[:, h * LOAD:(h + 1) * LOAD, :], xv[h]).then_inc(x_in[h], 16)

                def store(b):
                    sp.wait_ge(wh_ready, b * LOAD + (LOAD + SLOTS))
                    sp.dma_start(whv[bass.ds(b, 1)].rearrange("b p t f -> (b p) t f"), wh[:, bass.ds(b * LOAD, LOAD), :]).then_inc(wh_stored, 16)

                with sp.Fori(1, STEPS) as i:
                    for h in range(2):
                        sp.wait_ge(x_turned, (i - 1) * BODY + (h + 1) * LOAD)
                        sp.dma_start(xin[:, h * LOAD:(h + 1) * LOAD, :], xv[bass.ds(i * 2 + h, 1)].rearrange("b p t f -> (b p) t f")).then_inc(x_in[h], 16)
                        store((i - 1) * 2 + h)
                for h in range(2):
                    store((STEPS - 1) * 2 + h)
                sp.wait_ge(wh_stored, 16 * (TILES // LOAD))
                sp.wait_ge(rdt_ready, 1)
                sp.dma_start(r_row.rearrange("(t p) -> t p", p=P), rdt[0:TILES, :]).then_inc(r_stored, 16)
                sp.dma_start(dsh_row.rearrange("(t p) -> t p", p=P), rdt[TILES:2 * TILES, :]).then_inc(r_stored, 16)
                sp.wait_ge(r_stored, 32)

            @block.gpsimd
            def _(pool):
                pool.sem_inc(sum_done, 1)
                nc.gpsimd.memset(ident[:, :], 0.0).then_inc(cleared, 1)
                nc.gpsimd.memset(identb[:, :], 0.0).then_inc(cleared, 1)
                nc.gpsimd.memset(wh[:, :, F:F + 1], 1.0).then_inc(cleared, 1)
                nc.gpsimd.memset(wh[:, :, F + 1:F + 2], 0.0).then_inc(cleared, 1)
                nc.gpsimd.memset(wsum[:, :], 0.0).then_inc(cleared, 1)
                nc.gpsimd.memset(ones[:, :], 1.0).then_inc(cleared, 1)
                pool.wait_ge(cleared, 6)
                for t in (ident, identb):
                    nc.gpsimd.affine_select(out=t[:, :], in_=t[:, :], compare_op=ALU.not_equal, fill=1.0,
                                            base=0, pattern=[[-1, P]], channel_multiplier=1).then_inc(ident_ready, 1)
                with pool.Fori(0, TILES // SLOTS) as i:
                    for t in (i * SLOTS + k for k in range(SLOTS)):
                        pool.wait_ge(wh_ready, t + 1 + SLOTS)
                        pool.wait_ge(sum_done, t + 1)
                        nc.gpsimd.tensor_tensor(wsum[:, :], wsum[:, :], wh[:, bass.ds(t, 1), 0:F].rearrange("p a f -> p (a f)"), ALU.add).then_inc(sum_done, 1)
                pool.wait_ge(stat, 3)
                nc.gpsimd.partition_all_reduce(ext[:, :], loc[:, 0:2], P, RED.max).then_inc(ext_ready, 1)

            @block.tensor
            def _(pe):
                pe.wait_ge(ident_ready, 2)
                pe.wait_ge(weights_in, 48)
                with pe.Fori(0, STEPS) as i:
                    def turn(k):
                        if k % LOAD == 0:
                            pe.wait_ge(x_in[k // LOAD], i * 16 + 16)
                        for c in range(FK):
                            last = nc.tensor.transpose(ps_x[:, k % SLOTS, c * P:(c + 1) * P], xin[:, k, c * P:(c + 1) * P], ident[:, :])
                        last.then_inc(x_turned, 1)

                    def product(k):
                        pe.wait_ge(xt_ready, i * BODY + k + 1)
                        pe.wait_ge(wh_ready, i * BODY + k + 1)
                        for c in range(FK):
                            last = nc.tensor.matmul(ps_w[:, k % SLOTS, 0:F], xt[:, k % SLOTS, c, :], w_sb[:, c, :],
                                                    start=(c == 0), stop=(c == FK - 1))
                        last.then_inc(wh_made, 1)

                    turn(0)
                    for k in range(1, BODY):
                        turn(k)
                        product(k - 1)
                    product(BODY - 1)
                pe.wait_ge(exp_done, 1)
                pe.wait_ge(rarg_ready, 2)
                nc.tensor.transpose(ps_r[:, 0:P], rd[:, :, :].rearrange("p a t -> p (a t)"), ident[:, :]).then_inc(rd_turned, 1)
                pe.wait_ge(sum_done, TILES + 1)
                nc.tensor.matmul(ps_s[:, 0:F], ones[:, :], wsum[:, :], start=True, stop=True).then_inc(sum_spread, 1)

            @block.scalar
            def _(act):
                act.sem_inc(wh_ready, SLOTS)
                with act.Fori(0, STEPS) as i:
                    def turned_copy(k):
                        act.wait_ge(x_turned, i * BODY + k + 1)
                        nc.scalar.copy(xt[:, k % SLOTS, :, :].rearrange("p c n -> p (c n)"), ps_x[:, k % SLOTS, 0:F]).then_inc(xt_ready, 1)

                    def wh_copy(k):
                        act.wait_ge(wh_made, i * BODY + k + 1)
                        nc.scalar.copy(wh[:, bass.ds(i * BODY + k, 1), 0:F].rearrange("p a f -> p (a f)"), ps_w[:, k % SLOTS, 0:F]).then_inc(wh_ready, 1)

                    turned_copy(0)
                    for k in range(1, BODY):
                        turned_copy(k)
                        wh_copy(k - 1)
                    wh_copy(BODY - 1)
                act.wait_ge(bias_ready, 2)
                act.wait_ge(rarg_ready, 1)
                nc.scalar.activation(rd[:, 0, :], rarg[:, 1, :], ACT.Exp).then_inc(exp_done, 1)
                nc.scalar.activation(q_all[:, :], d_all[:, :], ACT.Exp, bias=bias[:, 0:1], scale=1.0 - SLOPE).then_inc(exp_done, 1)
                nc.scalar.activation(f_all[:, :], d_all[:, :], ACT.Exp, bias=bias[:, 1:2], scale=SLOPE).then_inc(exp_done, 1)

            @block.vector
            def _(dve):
                dve.sem_inc(sd_done, SLOTS)
                dve.wait_ge(weights_in, 48)
                with dve.Fori(0, TILES // SLOTS) as i:
                    for k in range(SLOTS):
                        dve.wait_ge(wh_ready, i * SLOTS + k + 1 + SLOTS)
                        dve.wait_ge(sd_done, i * SLOTS + k + 1)
                        for a, dst in enumerate((s_all, d_all)):
                            last = nc.vector.scalar_tensor_tensor(
                                out=junk[:, k, a, :], in0=wh[:, bass.ds(i * SLOTS + k, 1), 0:F].rearrange("p a f -> p (a f)"), scalar=1.0, in1=a_bc[:, a, :],
                                op0=ALU.mult, op1=ALU.mult, accum_out=dst[:, bass.ds(i * SLOTS + k, 1)])
                        last.then_inc(sd_done, 1)
                dve.wait_ge(sd_done, TILES + SLOTS)
                nc.vector.tensor_reduce(loc[:, 0:1], d_all[:, :], AX.X, ALU.max).then_inc(stat, 1)
                nc.vector.tensor_reduce(loc[:, 2:3], d_all[:, :], AX.X, ALU.min).then_inc(stat, 1)
                dve.wait_ge(stat, 2)
                nc.vector.tensor_scalar(loc[:, 1:2], loc[:, 2:3], -1.0, None, ALU.mult).then_inc(stat, 1)
                dve.wait_ge(ext_ready, 1)
                nc.vector.tensor_scalar(bias[:, 0:1], ext[:, 0:1], SLOPE - 1.0, None, ALU.mult).then_inc(bias_ready, 1)
                nc.vector.tensor_scalar(bias[:, 1:2], ext[:, 0:1], -SLOPE, None, ALU.mult).then_inc(bias_ready, 1)
                nc.vector.tensor_tensor(rng[:, :], ext[:, 0:1], ext[:, 1:2], ALU.add).then_inc(bias_ready, 1)
                dve.wait_ge(bias_ready, 3)
                nc.vector.tensor_scalar(flag[:, :], rng[:, :], RANGE_MAX, None, ALU.is_le).then_inc(stat, 1)
                nc.vector.tensor_scalar(rarg[:, 0, :], s_all[:, :], SLOPE - 1.0, bias[:, 0:1], ALU.mult, ALU.add).then_inc(stat, 1)
                dve.wait_ge(stat, 5)
                nc.vector.tensor_scalar(rarg[:, 1, :], rarg[:, 0, :], 0.0, None, ALU.min).then_inc(rarg_ready, 1)
                nc.vector.tensor_scalar(rd[:, 1, :], d_all[:, :], ext[:, 1:2], None, ALU.add).then_inc(rarg_ready, 1)
                dve.wait_ge(rd_turned, 1)
                nc.vector.tensor_copy(rdt[:, :], ps_r[:, 0:P]).then_inc(rdt_ready, 1)
                dve.wait_ge(sum_spread, 1)
                nc.vector.tensor_copy(whsum[:, :], ps_s[:, 0:F]).then_inc(stat, 1)
        clear(nc, sems)


def attend(nc, dims, adj, keep, g_hi, g_lo, wh_rows, att_rows, r_row, dsh_row):
    TILES, GROUPS, FE, NCH = (dims[k] for k in ("TILES", "GROUPS", "FE", "NCH"))
    W = CHUNK * P
    LOADS = 4
    MASKS = 2
    QS = CHUNK
    SPLITS = CHUNK
    identb, q_all, flag = keep["identb"], keep["q"], keep["flag"]
    with ExitStack() as ctx:
        def sb(name, shape, dt=F32):
            return ctx.enter_context(nc.sbuf_tensor(name, shape, dt))

        sems = []

        def sem(name):
            sems.append(ctx.enter_context(nc.semaphore(name)))
            return sems[-1]

        adj_sb = sb("adj_sb", [P, LOADS, STRIPS, W], I32)
        mask = sb("mask", [P, MASKS, STRIPS, W], BF16)
        r_bc = sb("r_bc", [P, 2, ROWS])
        qm = sb("qm", [P, QS, ROWS])
        q_hi = sb("q_hi", [P, SPLITS, ROWS], F32R)
        q_lo = sb("q_lo", [P, SPLITS, ROWS], F32R)
        stage = sb("stage", [P, STRIPS, FE])
        acc = ctx.enter_context(nc.psum_tensor("acc", [P, STRIPS, 512], F32))
        turned = ctx.enter_context(nc.psum_tensor("turned", [P, CHUNK, 1024], BF16))

        r_in = sem("at_r_in")
        adj_in = [sem(f"at_adj_in{k}") for k in range(LOADS)]
        mask_ready = sem("at_mask_ready")
        mask_begun = sem("at_mask_begun")
        turn_done = sem("at_turn_done")
        q_made = sem("at_q_made")
        hi_ready = sem("at_hi_ready")
        lo_ready = sem("at_lo_ready")
        split_free = sem("at_split_free")
        acc_free = sem("at_acc_free")
        stage_stored = sem("at_stage_stored")

        adj_v = adj.rearrange("(g s p) j -> g p s j", s=STRIPS, p=P)
        att_v = att_rows.rearrange("(g s p) c -> g s p c", s=STRIPS, p=P)
        slow = slow_path(nc, dims, adj, keep, wh_rows, att_rows, dsh_row, sem, sb,
                         dict(adj=adj_sb, mask=mask, r_bc=r_bc, qm=qm, stage=stage), acc, turned)

        with nc.Block() as block:
            @block.sync
            def _(sp):
                def load(g, c, k):
                    sp.dma_start(adj_sb[:, k, :, :],
                                 adj_v[bass.ds(g, 1), :, :, bass.ds(c * W, W)].rearrange("g p s j -> (g p) s j")
                                 ).then_inc(adj_in[k], 16)

                def load_r(g, slot):
                    sp.dma_start(r_bc[:, slot, :], r_row[bass.ds(g * ROWS, ROWS)].partition_broadcast(P)).then_inc(r_in, 16)

                fast = sp.value_load(flag[0:1, 0:1], min_val=0, max_val=1)
                with sp.If(fast == 1):
                    load_r(0, 0)
                    for k in range(LOADS):
                        load(0, k, k)
                    with sp.Fori(1, NCH // LOADS) as b:
                        for k in range(LOADS):
                            sp.wait_ge(mask_ready, b * LOADS + (k + 1 - LOADS))
                            load(0, b * LOADS + k, k)
                    with sp.Fori(1, GROUPS) as g:
                        sp.wait_ge(q_made, (g - 1) * TILES + CHUNK)
                        sp.dma_start(r_bc[:, bass.ds(g % 2, 1), :],
                                     r_row[bass.ds(g * ROWS, ROWS)].partition_broadcast(P)).then_inc(r_in, 16)
                        with sp.Fori(0, NCH // LOADS) as b:
                            for k in range(LOADS):
                                sp.wait_ge(mask_ready, g * NCH + b * LOADS + (k + 1 - LOADS))
                                load(g, b * LOADS + k, k)
                with sp.Else():
                    slow["sync"](sp)

            @block.gpsimd
            def _(pool):
                fast = pool.value_load(flag[0:1, 0:1], min_val=0, max_val=1)
                with pool.If(fast == 1):
                    with pool.Fori(0, GROUPS * NCH // LOADS) as b:
                        for k in range(LOADS):
                            pool.wait_ge(adj_in[k], b * 16 + 16)
                            pool.wait_ge(turn_done, (b * LOADS + k + 1) * CHUNK)
                            pool.sem_inc(mask_begun, 1)
                            nc.gpsimd.tensor_scalar(mask[:, k % MASKS, :, :].rearrange("p s j -> p (s j)"),
                                                    adj_sb[:, k, :, :].rearrange("p s j -> p (s j)"),
                                                    0.0, None, ALU.is_gt).then_inc(mask_ready, 1)
                    nc.gpsimd.drain().then_inc(mask_ready, 1)
                with pool.Else():
                    slow["pool"](pool)

            @block.tensor
            def _(pe):
                def turn(n, m, k):
                    if k == 0:
                        pe.wait_ge(mask_ready, n + 1)
                    pe.wait_ge(q_made, n * CHUNK + k + 1)
                    for s in range(STRIPS):
                        last = nc.tensor.transpose(turned[:, k, s * P:(s + 1) * P], mask[:, m, s, k * P:(k + 1) * P], identb[:, :])
                    last.then_inc(turn_done, 1)

                def products(n, c, g, k, first=False, final=False):
                    j = c * CHUNK + k
                    t = n * CHUNK + k
                    pe.wait_ge(hi_ready, t + 1)
                    for s in range(STRIPS):
                        if first:
                            pe.wait_ge(acc_free, g * STRIPS + s + 1)
                        cols = slice(s * P, (s + 1) * P)
                        nc.tensor.matmul(acc[:, s, 0:FE], q_hi[:, k, cols], g_hi[:, bass.ds(j, 1), :].rearrange("p a f -> p (a f)"),
                                         start=first, stop=False)
                        nc.tensor.matmul(acc[:, s, 0:FE], q_hi[:, k, cols], g_lo[:, bass.ds(j, 1), :].rearrange("p a f -> p (a f)"),
                                         start=False, stop=False)
                    pe.wait_ge(lo_ready, t + 1 + QS)
                    for s in range(STRIPS):
                        cols = slice(s * P, (s + 1) * P)
                        last = nc.tensor.matmul(acc[:, s, 0:FE], q_lo[:, k, cols], g_hi[:, bass.ds(j, 1), :].rearrange("p a f -> p (a f)"),
                                                start=False, stop=final)
                    last.then_inc(split_free, 1)

                def pair(g, c, first=False, final=False):
                    for m in range(2):
                        for k in range(CHUNK):
                            turn(g * NCH + c + (m + 1), (m + 1) % MASKS, k)
                            products(g * NCH + c + m, c + m, g, k, first=first and m == 0 and k == 0,
                                     final=final and m == 1 and k == CHUNK - 1)

                fast = pe.value_load(flag[0:1, 0:1], min_val=0, max_val=1)
                with pe.If(fast == 1):
                    pe.sem_inc(turn_done, MASKS * CHUNK)
                    pe.sem_inc(split_free, SPLITS)
                    for k in range(CHUNK):
                        turn(0, 0, k)
                    with pe.Fori(0, GROUPS) as g:
                        pair(g, 0, first=True)
                        with pe.Fori(1, NCH // 2 - 1) as b:
                            pair(g, b * 2)
                        pair(g, NCH - 2, final=True)
                with pe.Else():
                    slow["tensor"](pe)

            @block.vector
            def _(dve):
                BODY = 2 * CHUNK

                def mul_mask(t, j, slot, k):
                    dve.wait_ge(turn_done, t + 1 + MASKS * CHUNK)
                    dve.wait_ge(lo_ready, t + 1)
                    nc.vector.scalar_tensor_tensor(
                        out=qm[:, k % QS, :], in0=r_bc[:, slot, :], scalar=q_all[:, bass.ds(j, 1)],
                        in1=turned[:, k % CHUNK, 0:ROWS], op0=ALU.max, op1=ALU.mult).then_inc(q_made, 1)

                def low_part(t, k):
                    dve.wait_ge(hi_ready, t + 1)
                    dve.wait_ge(split_free, t + 1)
                    nc.vector.tensor_tensor(q_lo[:, k % SPLITS, :], qm[:, k % QS, :], q_hi[:, k % SPLITS, :].bitcast(F32),
                                            ALU.subtract).then_inc(lo_ready, 1)

                fast = dve.value_load(flag[0:1, 0:1], min_val=0, max_val=1)
                with dve.If(fast == 1):
                    dve.sem_inc(q_made, CHUNK)
                    dve.sem_inc(lo_ready, QS)
                    with dve.Fori(0, GROUPS // 2) as gg:
                        for slot in range(2):
                            with dve.Fori(0, TILES // BODY) as b:
                                dve.wait_ge(r_in, gg * 32 + 16 * (slot + 1))
                                base = gg * (2 * TILES) + slot * TILES + b * BODY
                                for k in range(BODY):
                                    mul_mask(base + k, b * BODY + k, slot, k)
                                    if k >= 1:
                                        low_part(base + (k - 1), k - 1)
                                low_part(base + (BODY - 1), BODY - 1)
                with dve.Else():
                    slow["vector"](dve)

            @block.scalar
            def _(act):
                BODY = 2 * CHUNK

                def high_part(t, k):
                    act.wait_ge(q_made, t + 1 + CHUNK)
                    act.wait_ge(split_free, t + 1)
                    nc.scalar.copy(q_hi[:, k % SPLITS, :], qm[:, k % QS, :]).then_inc(hi_ready, 1)

                def evacuate(g):
                    for s in range(STRIPS):
                        if s == 0:
                            act.wait_ge(stage_stored, (g + 1) * (16 * STRIPS))
                            act.wait_ge(split_free, (g + 1) * TILES + SPLITS)
                        nc.scalar.copy(stage[:, s, :], acc[:, s, 0:FE]).then_inc(acc_free, 1)
                    for s in range(STRIPS):
                        act.wait_ge(acc_free, g * STRIPS + s + 1 + STRIPS)
                        act.dma_start(att_v[bass.ds(g, 1), s, :, :].rearrange("g p c -> (g p) c"), stage[:, s, :]).then_inc(stage_stored, 16)

                def body(base, g_out=None):
                    for k in range(BODY):
                        high_part(base + k, k)
                        if g_out is not None and k == 3:
                            evacuate(g_out)

                fast = act.value_load(flag[0:1, 0:1], min_val=0, max_val=1)
                with act.If(fast == 1):
                    act.sem_inc(acc_free, STRIPS)
                    act.sem_inc(stage_stored, 16 * STRIPS)
                    for k in range(BODY):
                        high_part(k, k)
                    with act.Fori(0, GROUPS - 1) as g:
                        with act.Fori(1, TILES // BODY) as b:
                            body(g * TILES + b * BODY)
                        body(g * TILES + TILES, g_out=g)
                    with act.Fori(1, TILES // BODY) as b:
                        body((GROUPS - 1) * TILES + b * BODY)
                    evacuate(GROUPS - 1)
                    act.wait_ge(stage_stored, 16 * STRIPS * (GROUPS + 1))
                with act.Else():
                    slow["scalar"](act)
        clear(nc, sems)


def split_parts(nc, dims, keep, wh_all, g_hi, g_lo):
    TILES = dims["TILES"]
    f_all = keep["f"]
    with nc.semaphore("sp_hi_made") as hi_made, nc.semaphore("sp_lo_made") as lo_made:
        def tile(t, at):
            return t[:, bass.ds(at, 1), :].rearrange("p a f -> p (a f)")

        BODY = 8
        with nc.Block() as block:
            @block.scalar
            def _(act):
                with act.Fori(0, TILES // BODY) as b:
                    for t in (b * BODY + k for k in range(BODY)):
                        nc.scalar.activation(tile(g_hi, t), tile(wh_all, t), ACT.Copy, scale=f_all[:, bass.ds(t, 1)]).then_inc(hi_made, 1)

            @block.vector
            def _(dve):
                with dve.Fori(0, TILES // BODY) as b:
                    for t in (b * BODY + k for k in range(BODY)):
                        dve.wait_ge(hi_made, t + 1)
                        nc.vector.scalar_tensor_tensor(
                            out=tile(g_lo, t), in0=tile(wh_all, t), scalar=f_all[:, bass.ds(t, 1)],
                            in1=tile(g_hi, t).bitcast(F32), op0=ALU.mult, op1=ALU.subtract).then_inc(lo_made, 1)


def slow_path(nc, dims, adj, keep, wh_rows, att_rows, dsh_row, sem, sb, buf, acc, turned):
    TILES, FE = dims["TILES"], dims["FE"]
    W = CHUNK * P
    C = dims["N"] // W
    ident, s_all, ext = keep["ident"], keep["s"], keep["ext"]
    nbr = buf["adj"][:, 0, 0, :]
    whc = buf["adj"][:, 1, :, :].rearrange("p s j -> p (s j)").bitcast(F32)[:, 0:CHUNK * FE].rearrange("p (k f) -> p k f", k=CHUNK)
    dsh, wt = buf["r_bc"][:, 0, :], buf["r_bc"][:, 1, :]
    picked, z, lz, ex = (buf["qm"][:, i, :] for i in range(4))
    total = buf["stage"][:, 0, :]
    ps_t = turned[:, 0, :].bitcast(F32)
    mx = sb("sl_mx", [P, C])
    row = sb("sl_row", [P, 6])

    in1, in2, stored = sem("sl_in1"), sem("sl_in2"), sem("sl_stored")
    pick1 = sem("sl_pick1")
    max_done = sem("sl_max_done")
    row_step = sem("sl_row_step")
    z_done, lz_done, ex_done, pick2 = sem("sl_z_done"), sem("sl_lz_done"), sem("sl_ex_done"), sem("sl_pick2")
    turn, wt_done, prod = sem("sl_turn"), sem("sl_wt_done"), sem("sl_prod")
    add_done = sem("sl_add_done")
    zeroed = sem("sl_zeroed")
    settled = sem("sl_settled")

    def sync(sp):
        def load(t, c, signal):
            sp.dma_start(nbr, adj[bass.ds(t * P, P), bass.ds(c * W, W)]).then_inc(signal, 16)
            sp.dma_start(dsh, dsh_row[bass.ds(c * W, W)].partition_broadcast(P)).then_inc(signal, 16)

        with sp.Fori(0, TILES) as t:
            with sp.Fori(0, C) as c:
                sp.wait_ge(max_done, t * C + c + 1)
                sp.sem_inc(settled, 1)
                sp.wait_ge(add_done, t * C + 1)
                sp.sem_inc(settled, 1)
                load(t, c, in1)
            with sp.Fori(0, C) as c:
                sp.wait_ge(max_done, t * C + C + 1)
                sp.sem_inc(settled, 1)
                sp.wait_ge(add_done, t * C + c + 1)
                sp.sem_inc(settled, 1)
                load(t, c, in2)
                sp.dma_start(whc, wh_rows[bass.ds(c * W, W), :].rearrange("(k p) f -> p k f", p=P)).then_inc(in2, 16)
            sp.wait_ge(add_done, t * C + C + 1)
            sp.sem_inc(settled, 1)
            sp.dma_start(att_rows[bass.ds(t * P, P), :], total).then_inc(stored, 16)
        sp.wait_ge(stored, 16 * (TILES + 1))

    def pool(eng):
        eng.sem_inc(stored, 16)
        eng.sem_inc(max_done, 1)
        eng.sem_inc(add_done, 1)
        eng.sem_inc(row_step, 6)

    def tensor(pe):
        with pe.Fori(0, TILES) as t:
            with pe.Fori(0, C) as c:
                n = t * C + c
                pe.wait_ge(pick2, n + 1)
                for k in range(CHUNK):
                    last = nc.tensor.transpose(ps_t[:, k * P:(k + 1) * P], picked[:, k * P:(k + 1) * P], ident[:, :])
                last.then_inc(turn, 1)
                pe.wait_ge(wt_done, n + 1)
                for k in range(CHUNK):
                    last = nc.tensor.matmul(acc[:, 0, 0:FE], wt[:, k * P:(k + 1) * P], whc[:, k, :],
                                            start=(k == 0), stop=(k == CHUNK - 1))
                last.then_inc(prod, 1)

    def scalar(act):
        with act.Fori(0, TILES) as t:
            with act.Fori(0, C) as c:
                act.wait_ge(lz_done, t * C + c + 1)
                nc.scalar.activation(ex, lz, ACT.Exp, bias=row[:, 5:6]).then_inc(ex_done, 1)

    def vector(dve):
        def neighbours(src, signal, count):
            nc.vector.scalar_tensor_tensor(out=picked, in0=nbr, scalar=0.0, in1=src, op0=ALU.is_gt, op1=ALU.mult).then_inc(signal, 1)
            dve.wait_ge(signal, count)

        with dve.Fori(0, TILES) as t:
            with dve.Fori(0, C) as c:
                dve.wait_ge(in1, (t * C + c) * 32 + 32)
                neighbours(dsh, pick1, t * C + c + 1)
                nc.vector.tensor_reduce(mx[:, bass.ds(c, 1)], picked, AX.X, ALU.max).then_inc(max_done, 1)

            def step(i, ins):
                ins.then_inc(row_step, 1)
                dve.wait_ge(row_step, t * 6 + (i + 7))

            dve.wait_ge(max_done, t * C + C + 1)
            step(0, nc.vector.tensor_scalar(row[:, 0:1], s_all[:, bass.ds(t, 1)], ext[:, 1:2], None, ALU.subtract))
            step(1, nc.vector.tensor_reduce(row[:, 1:2], mx[:, :], AX.X, ALU.max))
            step(2, nc.vector.tensor_tensor(row[:, 2:3], row[:, 0:1], row[:, 1:2], ALU.add))
            step(3, nc.vector.tensor_scalar(row[:, 3:4], row[:, 2:3], 1.0, None, ALU.add))
            step(4, nc.vector.scalar_tensor_tensor(out=row[:, 4:5], in0=row[:, 2:3], scalar=SLOPE, in1=row[:, 2:3],
                                                   op0=ALU.mult, op1=ALU.max))
            step(5, nc.vector.tensor_scalar(row[:, 5:6], row[:, 4:5], -1.0, None, ALU.mult))
            dve.wait_ge(stored, t * 16 + 16)
            nc.vector.memset(total, 0.0).then_inc(zeroed, 1)
            with dve.Fori(0, C) as c:
                n = t * C + c
                dve.wait_ge(in2, n * 48 + 48)
                nc.vector.tensor_scalar(z, dsh, row[:, 0:1], row[:, 3:4], ALU.add, ALU.min).then_inc(z_done, 1)
                dve.wait_ge(z_done, n + 1)
                nc.vector.scalar_tensor_tensor(out=lz, in0=z, scalar=SLOPE, in1=z, op0=ALU.mult, op1=ALU.max).then_inc(lz_done, 1)
                dve.wait_ge(ex_done, n + 1)
                neighbours(ex, pick2, n + 1)
                dve.wait_ge(turn, n + 1)
                nc.vector.tensor_copy(wt, ps_t[:, :]).then_inc(wt_done, 1)
                dve.wait_ge(prod, n + 1)
                dve.wait_ge(zeroed, t + 1)
                dve.wait_ge(add_done, n + 1)
                nc.vector.tensor_tensor(total, total, acc[:, 0, 0:FE], ALU.add).then_inc(add_done, 1)

    return dict(sync=sync, pool=pool, tensor=tensor, scalar=scalar, vector=vector)


def fuse(nc, dims, x, w, keep, wh_rows, att_rows, out):
    F, GROUPS, FE, FK, N = (dims[k] for k in ("F", "GROUPS", "FE", "FK", "N"))
    S = w["abp_w"].shape[0]
    DI = w["fe1_w"].shape[1]
    G1 = w["g1_w"].shape[1]
    ident, whsum = keep["ident"], keep["whsum"]
    mats = {n: (w[n], w[n].shape[0] // P, w[n].shape[1])
            for n in ("fe1_w", "W_bcdt", "abp_w", "fe2_w", "W_hz", "out_w", "g1_w", "g2_w")}
    bias_of = {"fe1_w": "fe1_b", "W_bcdt": "b_bcdt", "abp_w": "abp_b", "fe2_w": "fe2_b", "W_hz": "b_hz",
               "out_w": "out_b", "g1_w": "g1_b", "g2_w": "g2_b"}
    bias_at, NB = {}, 0
    for n in mats:
        bias_at[n] = NB
        NB += mats[n][2]
    spread = ("fe_ln_g", "fe_ln_b", "g_ln_g", "g_ln_b", "ln_g", "ln_b")
    LO_ROW = 32

    with ExitStack() as ctx:
        def sb(name, shape, dt=F32):
            return ctx.enter_context(nc.sbuf_tensor(name, shape, dt))

        hi = {n: sb(n + "_hi", [P, k, c], F32R) for n, (_, k, c) in mats.items()}
        lo = {n: sb(n + "_lo", [P, k, c], F32R) for n, (_, k, c) in mats.items()}
        brow = sb("brow", [P, NB], F32R)
        ones = sb("ones_r", [P, P], F32R)
        vec = {n: sb(n + "_bc", [P, w[n].shape[0]]) for n in spread}
        cpw = sb("cpw_bc", [P, S])
        cpb1 = sb("cpb1", [P, 1])
        d2 = sb("d2", [P, 1])
        half = sb("minus_half", [P, 1])
        prepare(nc, w, mats, bias_of, bias_at, NB, LO_ROW, hi, lo, brow, ones, vec, cpw, cpb1, d2, half)

        def rows(name, width, dt=F32):
            return sb(name, [P, STRIPS, width], dt)

        wh, xr, num = rows("wh_in", FE), rows("x_in", F), rows("att_in", FE)
        wht_hi, wht_lo = rows("wht_hi", F, F32R), rows("wht_lo", F, F32R)
        vt_hi, vt_lo = rows("vt_hi", DI, F32R), rows("vt_lo", DI, F32R)
        abt_hi, abt_lo = rows("abt_hi", S, F32R), rows("abt_lo", S, F32R)
        v, th = rows("v", DI), rows("th", DI)
        ab, e = rows("ab", S), rows("e", S)
        hs0 = rows("hs0", F)
        ha, hs, he, fused = rows("ha", F), rows("hs", F), rows("he", F), rows("fused", F)
        tg = rows("tg", F)
        cj = rows("cj", S)
        st = {n: rows("st_" + n, 6) for n in ("fe", "g", "f", "o")}
        mv = {n: rows("mv_" + n, 2) for n in ("fe", "g", "f", "o")}
        ve = {n: rows("ve_" + n, 3) for n in ("fe", "g", "f", "o")}
        sc = rows("sc", 8)
        ps = ctx.enter_context(nc.psum_tensor("ps", [P, 8, 512], F32))

        steps = ["in_wh", "in_x", "in_att",
                 "t_wh", "hi_wh", "lo_wh", "fe1", "fe_st", "fe_mv", "fe_ve", "fe_rs", "fe_nm", "fe_xh", "fe_g", "fe_n", "fe_th", "fe_v",
                 "bc", "mx", "e", "es", "ab", "t_ab", "hi_ab", "lo_ab", "abp", "hs0", "t_fe", "hi_fe", "lo_fe", "fe2", "he",
                 "t_hs0", "hi_hs0", "lo_hs0", "hz_h", "hz_z", "z_th", "w", "u", "t_u", "hi_u", "lo_u", "cd", "c1", "out", "hs",
                 "nn", "ws", "wr", "hn", "ha", "t_co", "hi_co", "lo_co", "g1", "g_st", "g_mv", "g_ve", "g_rs", "g_nm", "g_xh", "g_g", "g_n", "g_th", "g_v",
                 "t_g", "hi_g", "lo_g", "g2", "tg", "dl", "hh", "m", "f", "f_st", "f_mv", "f_ve", "f_rs", "f_nm", "f_xh", "f_g", "f_n", "y",
                 "o_st", "o_mv", "o_ve", "o_rs", "o_nm", "o_out", "settled", "stored"]
        dma_steps = ("in_wh", "in_x", "in_att", "stored")
        sems = {n: ctx.enter_context(nc.semaphore("fu_" + n)) for n in steps if n not in dma_steps}
        for n in dma_steps:
            for s in range(STRIPS):
                sems[n, s] = ctx.enter_context(nc.semaphore(f"fu_{n}{s}"))

        class Strip:
            def __init__(self, eng, g, s):
                self.eng, self.g, self.s = eng, g, s

            def need(self, *names):
                for n in names:
                    if n in dma_steps:
                        self.eng.wait_ge(sems[n, self.s], self.g * 16 + 32)
                    else:
                        self.eng.wait_ge(sems[n], self.g * STRIPS + (self.s + 1 + STRIPS))

            def free(self, *names):
                for n in names:
                    if n in dma_steps:
                        self.eng.wait_ge(sems[n, self.s], self.g * 16 + 16)
                    else:
                        self.eng.wait_ge(sems[n], self.g * STRIPS + (self.s + 1))

            def settle(self):
                self.eng.sem_inc(sems["settled"], 1)

            def done(self, name, ins):
                if name in dma_steps:
                    ins.then_inc(sems[name, self.s], 16)
                else:
                    ins.then_inc(sems[name], 1)

        def step(work):
            def maybe(k, *more):
                if k is not None:
                    work(k, *more)
            return maybe

        def strips(eng, g):
            return [Strip(eng, g, s) for s in range(STRIPS)]

        def run(eng, body):
            none = [None] * STRIPS
            body(*strips(eng, 0), *none)
            with eng.Fori(1, GROUPS) as g:
                body(*strips(eng, g), *strips(eng, g - 1))
            body(*none, *strips(eng, GROUPS - 1))

        with nc.Block() as block:
            @block.sync
            def _(sp):
                for n in steps:
                    if n in dma_steps:
                        for s in range(STRIPS):
                            sp.sem_inc(sems[n, s], 16)
                    else:
                        sp.sem_inc(sems[n], STRIPS)

        xg = x.rearrange("(g s p) f -> g s p f", s=STRIPS, p=P)
        whg = wh_rows.rearrange("(g s p) f -> g s p f", s=STRIPS, p=P)
        attg = att_rows.rearrange("(g s p) f -> g s p f", s=STRIPS, p=P)
        outg = out.rearrange("(g s p) f -> g s p f", s=STRIPS, p=P)

        with nc.Block() as block:
            @block.sync
            def _(sp):
                def load(name, k, dst, src):
                    k.done(name, sp.dma_start(dst[:, k.s, :], src[bass.ds(k.g, 1), k.s].rearrange("g p f -> (g p) f")))

                @step
                def in_wh(k):
                    k.free("hs0", "t_wh")
                    load("in_wh", k, wh, whg)

                @step
                def in_att(k):
                    k.free("hn", "wr")
                    load("in_att", k, num, attg)

                @step
                def in_x(k):
                    k.free("y")
                    load("in_x", k, xr, xg)

                def body(a, b, c, d, pa, pb, pc, pd):
                    in_wh(a), in_att(a), in_x(a), in_wh(b), in_att(b), in_wh(c), in_x(b), in_att(c), in_wh(d)
                    in_att(d), in_x(c), in_x(d)

                run(sp, body)

            half_of = dict(t_wh=0, fe1=0, bc=1, t_fe=0, fe2=0, t_ab=1, abp=1, t_hs0=1, hz_h=0, hz_z=1, t_u=0, out=1,
                           t_co=0, g1=1, t_g=0, g2=1)

            def bank(name, k):
                return ps[:, half_of[name] * STRIPS + k.s, :]

            def blocks(t, k, n):
                return [t[:, k.s, i * P:(i + 1) * P] for i in range(n)]

            @block.tensor
            def _(pe):
                def turn(k, name, parts):
                    for i, b in enumerate(parts):
                        last = nc.tensor.transpose(bank(name, k)[:, i * P:(i + 1) * P], b, ident[:, :])
                    k.done(name, last)

                def product(k, name, mat, left_hi, left_lo, c0=0, c1=None):
                    _, nk, nc_ = mats[mat]
                    c1 = nc_ if c1 is None else c1
                    o = bank(name, k)[:, 0:c1 - c0]
                    nc.tensor.matmul(o, ones[:, :], brow[:, bias_at[mat] + c0:bias_at[mat] + c1], start=True, stop=False)
                    for i in range(nk):
                        a_hi, a_lo = left_hi[:, k.s, i * P:(i + 1) * P], left_lo[:, k.s, i * P:(i + 1) * P]
                        nc.tensor.matmul(o, a_hi, hi[mat][:, i, c0:c1], start=False, stop=False)
                        nc.tensor.matmul(o, a_hi, lo[mat][:, i, c0:c1], start=False, stop=False)
                        last = nc.tensor.matmul(o, a_lo, hi[mat][:, i, c0:c1], start=False, stop=i == nk - 1)
                    k.done(name, last)

                @step
                def t_wh(k):
                    k.need("in_wh")
                    k.free("lo_g")
                    turn(k, "t_wh", blocks(wh, k, FK))

                @step
                def fe1(k):
                    product(k, "fe1", "fe1_w", wht_hi, wht_lo)

                @step
                def bc(k):
                    k.need("lo_wh")
                    k.free("tg")
                    product(k, "bc", "W_bcdt", wht_hi, wht_lo)

                @step
                def t_fe(k):
                    k.need("fe_v")
                    turn(k, "t_fe", blocks(v, k, DI // P))

                @step
                def fe2(k):
                    k.need("lo_fe")
                    product(k, "fe2", "fe2_w", vt_hi, vt_lo)

                @step
                def t_ab(k):
                    k.need("ab")
                    turn(k, "t_ab", [ab[:, k.s, :]])

                @step
                def abp(k):
                    k.need("lo_ab")
                    product(k, "abp", "abp_w", abt_hi, abt_lo)

                @step
                def t_hs0(k):
                    k.need("hs0")
                    turn(k, "t_hs0", blocks(hs0, k, FK))

                @step
                def hz_z(k):
                    k.need("lo_hs0")
                    product(k, "hz_z", "W_hz", wht_hi, wht_lo, DI, 2 * DI)

                @step
                def hz_h(k):
                    k.need("he")
                    product(k, "hz_h", "W_hz", wht_hi, wht_lo, 0, DI)

                @step
                def t_u(k):
                    k.need("u")
                    turn(k, "t_u", blocks(v, k, DI // P))

                @step
                def out_(k):
                    k.need("lo_u")
                    product(k, "out", "out_w", vt_hi, vt_lo)

                @step
                def t_co(k):
                    k.need("hs", "ha")
                    turn(k, "t_co", blocks(ha, k, FK) + blocks(hs, k, FK))

                @step
                def g1(k):
                    k.need("lo_co")
                    product(k, "g1", "g1_w", vt_hi, vt_lo)

                @step
                def t_g(k):
                    k.need("g_v")
                    turn(k, "t_g", blocks(v, k, G1 // P))

                @step
                def g2(k):
                    k.need("lo_g")
                    product(k, "g2", "g2_w", vt_hi, vt_lo)

                def body(a, b, c, d, pa, pb, pc, pd):
                    t_fe(pc), g2(pa), t_co(pb), t_ab(pd), fe2(pc), g1(pb), t_wh(a), hz_h(pc), abp(pd)
                    t_fe(pd), bc(a), fe1(a), t_hs0(pd), fe2(pd), t_u(pc), hz_z(pd), hz_h(pd), t_g(pb), t_ab(a)
                    out_(pc), t_u(pd), g2(pb), t_co(pc), abp(a), t_wh(b), out_(pd), t_hs0(a), g1(pc), t_co(pd)
                    t_fe(a), hz_z(a), bc(b), fe2(a), g1(pd), hz_h(a), t_ab(b), fe1(b), t_g(pc), t_u(a), abp(b)
                    g2(pc), t_wh(c), t_hs0(b), out_(a), t_g(pd), hz_z(b), t_co(a), bc(c), g2(pd), t_fe(b)
                    g1(a), t_ab(c), fe1(c), fe2(b), t_wh(d), abp(c), hz_h(b), t_hs0(c), bc(d), fe1(d), t_u(b)
                    hz_z(c), t_g(a), out_(b)

                run(pe, body)

            @block.scalar
            def _(act):
                def high(k, name, dst, width, scale=1.0):
                    k.need("t_" + name)
                    k.done("hi_" + name, nc.scalar.activation(dst[:, k.s, 0:width], bank("t_" + name, k)[:, 0:width], ACT.Copy, scale=scale))

                def normal(k, n, dst, src):
                    k.need(n + "_nm")
                    k.done({"fe": "fe_xh", "g": "g_xh", "f": "f_xh", "o": "o_out"}[n],
                           nc.scalar.activation(dst, src, ACT.Identity, scale=ve[n][:, k.s, 1:2], bias=ve[n][:, k.s, 2:3]))

                @step
                def hi_wh(k):
                    k.free("hz_h")
                    high(k, "wh", wht_hi, F)

                @step
                def fe_xh(k):
                    k.free("t_g")
                    normal(k, "fe", v[:, k.s, :], bank("fe1", k))

                @step
                def e_(k):
                    k.need("mx")
                    k.done("e", nc.scalar.activation(e[:, k.s, :], bank("bc", k)[:, 2 * S:3 * S], ACT.Exp,
                                                     bias=sc[:, k.s, 0:1], accum_out=sc[:, k.s, 1:2]))

                @step
                def fe_th(k):
                    k.need("fe_n")
                    k.done("fe_th", nc.scalar.activation(th[:, k.s, :], v[:, k.s, :], ACT.Tanh, scale=0.5))

                @step
                def hi_fe(k):
                    k.free("g2")
                    high(k, "fe", vt_hi, DI, 0.5)

                @step
                def hi_ab(k):
                    high(k, "ab", abt_hi, S)

                @step
                def he_(k):
                    k.need("fe2")
                    k.free("f")
                    k.done("he", nc.scalar.copy(he[:, k.s, :], bank("fe2", k)[:, 0:F]))

                @step
                def hi_hs0(k):
                    high(k, "hs0", wht_hi, F)

                @step
                def z_th(k):
                    k.need("hz_z", "fe_v")
                    k.done("z_th", nc.scalar.activation(th[:, k.s, :], bank("hz_z", k), ACT.Tanh, scale=0.5))

                @step
                def hi_u(k):
                    high(k, "u", vt_hi, DI, 0.5)

                @step
                def hs_(k):
                    k.need("out", "c1")
                    k.done("hs", nc.scalar.activation(hs[:, k.s, :], bank("out", k)[:, 0:F], ACT.Copy, scale=sc[:, k.s, 4:5]))

                @step
                def hi_co(k):
                    high(k, "co", vt_hi, G1)

                @step
                def g_xh(k):
                    normal(k, "g", v[:, k.s, :], bank("g1", k))

                @step
                def g_th(k):
                    k.need("g_n")
                    k.done("g_th", nc.scalar.activation(th[:, k.s, :], v[:, k.s, :], ACT.Tanh, scale=0.5))

                @step
                def hi_g(k):
                    high(k, "g", vt_hi, G1, 0.5)

                @step
                def tg_(k):
                    k.need("g2")
                    k.free("m")
                    k.done("tg", nc.scalar.activation(tg[:, k.s, :], bank("g2", k)[:, 0:F], ACT.Tanh, scale=0.5))

                @step
                def f_xh(k):
                    normal(k, "f", fused[:, k.s, :], fused[:, k.s, :])

                @step
                def o_out(k):
                    normal(k, "o", fused[:, k.s, :], fused[:, k.s, :])

                @step
                def store(k):
                    k.need("o_out")
                    k.done("stored", act.dma_start(outg[bass.ds(k.g, 1), k.s].rearrange("g p f -> (g p) f"), fused[:, k.s, :]))

                def body(a, b, c, d, pa, pb, pc, pd):
                    hs_(pb), hi_fe(pc), fe_xh(pd), tg_(pa), hi_co(pb), hi_ab(pd), he_(pc), fe_th(pd), f_xh(pa)
                    hi_wh(a), hi_fe(pd), g_xh(pb), e_(a), hi_hs0(pd), he_(pd), g_th(pb), hi_u(pc), o_out(pa)
                    z_th(pd), store(pa), fe_xh(a), hi_g(pb), hi_ab(a), hs_(pc), hi_u(pd), tg_(pb), hi_co(pc)
                    fe_th(a), hi_wh(b), hs_(pd), hi_hs0(a), f_xh(pb), hi_co(pd), hi_fe(a), z_th(a), g_xh(pc)
                    e_(b), he_(a), g_th(pc), o_out(pb), store(pb), hi_ab(b), g_xh(pd), hi_g(pc), hi_u(a)
                    fe_xh(b), g_th(pd), tg_(pc), hi_wh(c), hi_hs0(b), hs_(a), fe_th(b), hi_g(pd), hi_co(a)
                    z_th(b), e_(c), tg_(pd), f_xh(pc), hi_fe(b), hi_ab(c), f_xh(pd), he_(b), g_xh(a), hi_wh(d)
                    o_out(pc), store(pc), hi_hs0(c), fe_xh(c), g_th(a), e_(d), hi_u(b), fe_th(c), hi_g(a)
                    o_out(pd), z_th(c), store(pd)

                run(act, body)
                for s in range(STRIPS):
                    act.wait_ge(sems["stored", s], 16 * (GROUPS + 1))

            @block.gpsimd
            def _(pool):
                @step
                def inverse_std(k, n):
                    k.need(n + "_mv")
                    k.settle()
                    k.done(n + "_ve", nc.gpsimd.tensor_scalar(ve[n][:, k.s, 0:1], mv[n][:, k.s, 1:2], EPS, None, ALU.add))
                    k.need(n + "_ve")
                    k.done(n + "_rs", nc.gpsimd.tensor_tensor(ve[n][:, k.s, 1:2], ve[n][:, k.s, 0:1], half[:, :], ALU.pow))
                    k.need(n + "_rs")
                    k.settle()
                    k.done(n + "_nm", nc.gpsimd.tensor_scalar(ve[n][:, k.s, 2:3], mv[n][:, k.s, 0:1], ve[n][:, k.s, 1:2], -1.0,
                                                              ALU.mult, ALU.mult))

                @step
                def fe_n(k):
                    k.need("fe_g")
                    k.done("fe_n", nc.gpsimd.tensor_tensor(v[:, k.s, :], v[:, k.s, :], vec["fe_ln_b"][:, :], ALU.add))

                @step
                def g_n(k):
                    k.need("g_g")
                    k.done("g_n", nc.gpsimd.tensor_tensor(v[:, k.s, :], v[:, k.s, :], vec["g_ln_b"][:, :], ALU.add))

                @step
                def f_n(k):
                    k.need("f_g")
                    k.done("f_n", nc.gpsimd.tensor_tensor(fused[:, k.s, :], fused[:, k.s, :], vec["ln_b"][:, :], ALU.add))

                @step
                def y(k):
                    k.need("f_n", "in_x")
                    k.done("y", nc.gpsimd.tensor_tensor(fused[:, k.s, :], fused[:, k.s, :], xr[:, k.s, :], ALU.add))

                @step
                def differences(k):
                    k.need("hs", "ha", "he", "t_co")
                    k.done("dl", nc.gpsimd.tensor_tensor(ha[:, k.s, :], ha[:, k.s, :], hs[:, k.s, :], ALU.subtract))
                    k.done("hh", nc.gpsimd.tensor_tensor(he[:, k.s, :], he[:, k.s, :], hs[:, k.s, :], ALU.add))

                def body(a, b, c, d, pa, pb, pc, pd):
                    inverse_std(pd, "fe"), differences(pb), fe_n(pd), inverse_std(pa, "f"), f_n(pa)
                    inverse_std(pb, "g"), y(pa), g_n(pb), inverse_std(pa, "o"), inverse_std(a, "fe"), fe_n(a)
                    differences(pc), inverse_std(pb, "f"), differences(pd), inverse_std(pc, "g"), f_n(pb)
                    y(pb), g_n(pc), inverse_std(pb, "o"), inverse_std(pd, "g"), inverse_std(b, "fe"), g_n(pd)
                    fe_n(b), differences(a), inverse_std(pc, "f"), f_n(pc), y(pc), inverse_std(pd, "f")
                    inverse_std(a, "g"), inverse_std(pc, "o"), f_n(pd), inverse_std(c, "fe"), g_n(a), y(pd)
                    fe_n(c), inverse_std(pd, "o")

                run(pool, body)

            @block.vector
            def _(dve):
                def low(k, name, dst, hi_t, width, scale=1.0):
                    k.need("hi_" + name)
                    k.done("lo_" + name, nc.vector.scalar_tensor_tensor(
                        out=dst[:, k.s, 0:width], in0=bank("t_" + name, k)[:, 0:width], scalar=scale,
                        in1=hi_t[:, k.s, 0:width].bitcast(F32), op0=ALU.mult, op1=ALU.subtract))

                def moments(k, n, made, src):
                    k.need(made)
                    k.done(n + "_st", nc.vector.bn_stats(st[n][:, k.s, :], src))

                def mean_var(k, n):
                    k.need(n + "_st")
                    k.settle()
                    k.done(n + "_mv", nc.vector.bn_aggr(mv[n][:, k.s, :], st[n][:, k.s, :]))

                def gain(k, n, t, by):
                    k.need(n + "_xh")
                    k.done(n + "_g", nc.vector.tensor_tensor(t[:, k.s, :], t[:, k.s, :], vec[by][:, :], ALU.mult))

                def twice_silu(k, n):
                    k.need(n + "_th")
                    k.done(n + "_v", nc.vector.scalar_tensor_tensor(out=v[:, k.s, :], in0=th[:, k.s, :], scalar=1.0, in1=v[:, k.s, :],
                                                                    op0=ALU.add, op1=ALU.mult))

                @step
                def lo_wh(k):
                    low(k, "wh", wht_lo, wht_hi, F)

                @step
                def fe_st(k):
                    moments(k, "fe", "fe1", bank("fe1", k))

                @step
                def fe_mv(k):
                    mean_var(k, "fe")

                @step
                def fe_g(k):
                    gain(k, "fe", v, "fe_ln_g")

                @step
                def mx(k):
                    k.need("bc")
                    k.done("mx", nc.vector.tensor_reduce(sc[:, k.s, 0:1], bank("bc", k)[:, 2 * S:3 * S], AX.X, ALU.max, negate=True))

                @step
                def c_dot(k):
                    k.need("e")
                    k.free("cd")
                    k.done("cd", nc.vector.scalar_tensor_tensor(out=cj[:, k.s, :], in0=bank("bc", k)[:, S:2 * S], scalar=1.0, in1=cpw[:, :],
                                                                op0=ALU.mult, op1=ALU.mult, accum_out=sc[:, k.s, 3:4]))

                @step
                def ab_(k):
                    k.done("es", nc.vector.reciprocal(sc[:, k.s, 2:3], sc[:, k.s, 1:2]))
                    k.need("es")
                    k.done("ab", nc.vector.scalar_tensor_tensor(out=ab[:, k.s, :], in0=e[:, k.s, :], scalar=sc[:, k.s, 2:3],
                                                                in1=bank("bc", k)[:, 0:S], op0=ALU.mult, op1=ALU.mult))

                @step
                def c1(k):
                    k.need("cd")
                    k.done("c1", nc.vector.tensor_tensor(sc[:, k.s, 4:5], sc[:, k.s, 3:4], cpb1[:, :], ALU.add))

                @step
                def fe_v(k):
                    twice_silu(k, "fe")

                @step
                def lo_fe(k):
                    low(k, "fe", vt_lo, vt_hi, DI, 0.5)

                @step
                def lo_ab(k):
                    low(k, "ab", abt_lo, abt_hi, S)

                @step
                def hs0_(k):
                    k.need("abp")
                    k.done("hs0", nc.vector.tensor_tensor(hs0[:, k.s, :], bank("abp", k)[:, 0:F], wh[:, k.s, 0:F], ALU.mult))

                @step
                def lo_hs0(k):
                    low(k, "hs0", wht_lo, wht_hi, F)

                @step
                def attention(k):
                    k.need("in_att")
                    k.done("nn", nc.vector.tensor_scalar(sc[:, k.s, 5:6], num[:, k.s, F:F + 1], 0.0, None, ALU.is_equal))
                    k.need("nn")
                    k.done("ws", nc.vector.scalar_tensor_tensor(out=sc[:, k.s, 6:7], in0=sc[:, k.s, 5:6], scalar=float(N),
                                                                in1=num[:, k.s, F:F + 1], op0=ALU.mult, op1=ALU.add))
                    k.free("m")
                    k.done("hn", nc.vector.scalar_tensor_tensor(out=ha[:, k.s, :], in0=whsum[:, :], scalar=sc[:, k.s, 5:6],
                                                                in1=num[:, k.s, 0:F], op0=ALU.mult, op1=ALU.add))
                    k.need("ws")
                    k.done("wr", nc.vector.reciprocal(sc[:, k.s, 7:8], sc[:, k.s, 6:7]))
                    k.need("wr", "hn")
                    k.done("ha", nc.vector.tensor_scalar(ha[:, k.s, :], ha[:, k.s, :], sc[:, k.s, 7:8], None, ALU.mult))

                @step
                def u_(k):
                    k.need("z_th", "hz_h")
                    k.done("w", nc.vector.scalar_tensor_tensor(out=v[:, k.s, :], in0=th[:, k.s, :], scalar=1.0, in1=bank("hz_z", k),
                                                               op0=ALU.add, op1=ALU.mult))
                    k.need("w")
                    k.done("u", nc.vector.scalar_tensor_tensor(out=v[:, k.s, :], in0=v[:, k.s, :], scalar=d2[:, :], in1=bank("hz_h", k),
                                                               op0=ALU.add, op1=ALU.mult))

                @step
                def lo_u(k):
                    low(k, "u", vt_lo, vt_hi, DI, 0.5)

                @step
                def lo_co(k):
                    low(k, "co", vt_lo, vt_hi, G1)

                @step
                def g_st(k):
                    moments(k, "g", "g1", bank("g1", k))

                @step
                def g_mv(k):
                    mean_var(k, "g")

                @step
                def g_g(k):
                    gain(k, "g", v, "g_ln_g")

                @step
                def g_v(k):
                    twice_silu(k, "g")

                @step
                def lo_g(k):
                    low(k, "g", vt_lo, vt_hi, G1, 0.5)

                @step
                def m(k):
                    k.need("tg", "dl")
                    k.done("m", nc.vector.scalar_tensor_tensor(out=tg[:, k.s, :], in0=tg[:, k.s, :], scalar=1.0, in1=ha[:, k.s, :],
                                                               op0=ALU.add, op1=ALU.mult))

                @step
                def f(k):
                    k.need("m", "hh")
                    k.free("stored")
                    k.done("f", nc.vector.scalar_tensor_tensor(out=fused[:, k.s, :], in0=tg[:, k.s, :], scalar=0.5, in1=he[:, k.s, :],
                                                               op0=ALU.mult, op1=ALU.add))

                @step
                def f_st(k):
                    moments(k, "f", "f", fused[:, k.s, :])

                @step
                def f_mv(k):
                    mean_var(k, "f")

                @step
                def f_g(k):
                    gain(k, "f", fused, "ln_g")

                @step
                def o_st(k):
                    moments(k, "o", "y", fused[:, k.s, :])

                @step
                def o_mv(k):
                    mean_var(k, "o")

                def body(a, b, c, d, pa, pb, pc, pd):
                    fe_mv(pd), c_dot(pd), ab_(pd), lo_fe(pc), fe_g(pd), m(pa), lo_co(pb), f(pa), lo_ab(pd)
                    f_st(pa), f_mv(pa), fe_v(pd), g_st(pb), f_g(pa), lo_wh(a), g_mv(pb), u_(pc), hs0_(pd)
                    lo_fe(pd), mx(a), o_st(pa), g_g(pb), o_mv(pa), fe_st(a), c_dot(a), lo_hs0(pd), fe_mv(a)
                    ab_(a), c1(pd), attention(pd), g_v(pb), lo_u(pc), u_(pd), lo_g(pb), lo_ab(a), fe_g(a)
                    lo_u(pd), m(pb), hs0_(a), lo_co(pc), f(pb), fe_v(a), f_st(pb), lo_wh(b), f_mv(pb)
                    lo_hs0(a), c1(a), attention(a), g_st(pc), g_mv(pc), f_g(pb), lo_co(pd), lo_fe(a), mx(b)
                    g_g(pc), o_st(pb), c_dot(b), o_mv(pb), ab_(b), g_st(pd), g_v(pc), g_mv(pd), u_(a)
                    lo_ab(b), fe_st(b), fe_mv(b), g_g(pd), lo_g(pc), lo_u(a), hs0_(b), fe_g(b), g_v(pd), m(pc)
                    lo_hs0(b), f(pc), c1(b), lo_wh(c), f_st(pc), attention(b), f_mv(pc), lo_g(pd), fe_v(b)
                    lo_co(a), mx(c), c_dot(c), ab_(c), m(pd), f_g(pc), f(pd), lo_fe(b), f_st(pd), f_mv(pd)
                    g_st(a), lo_ab(c), o_st(pc), g_mv(a), o_mv(pc), fe_st(c), fe_mv(c), f_g(pd), hs0_(c)
                    g_g(a), lo_wh(d), u_(b), lo_hs0(c), fe_g(c), c1(c), mx(d), o_st(pd), g_v(a), o_mv(pd)
                    attention(c), lo_u(b), fe_v(c), fe_st(d), lo_g(a)

                run(dve, body)


def prepare(nc, w, mats, bias_of, bias_at, NB, LO_ROW, hi, lo, brow, ones, vec, cpw, cpb1, d2, half):
    with ExitStack() as ctx:
        def sb(name, shape, dt=F32):
            return ctx.enter_context(nc.sbuf_tensor(name, shape, dt))

        def sem(name):
            return ctx.enter_context(nc.semaphore(name))

        raw = {n: sb(n + "_raw", [P, k, c]) for n, (_, k, c) in mats.items()}
        braw = sb("braw", [LO_ROW + 1, NB])
        bhi = sb("bhi", [LO_ROW + 1, NB], F32R)
        small = sb("small", [P, 2])
        araw = sb("araw", [LO_ROW + 1, cpw.shape[1]])
        raw_in = {n: sem("wp_in_" + n) for n in mats}
        vec_in = sem("wp_vec_in")
        bias_in = sem("wp_bias_in")
        cleared = sem("wp_cleared")
        hi_made = sem("wp_hi_made")
        lo_made = sem("wp_lo_made")
        bias_hi = sem("wp_bias_hi")
        summed = sem("wp_summed")
        bias_again = sem("wp_bias_again")
        done = sem("wp_done")
        S = cpw.shape[1]
        DT = bias_at["W_bcdt"] + 2 * S
        n_vec = len(vec) + 3
        n_bias = len(mats) + 1
        with nc.Block() as block:
            @block.sync
            def _(sp):
                for n, (m, k, c) in mats.items():
                    sp.dma_start(raw[n][:, :, :], m.rearrange("(k p) c -> p k c", p=P)).then_inc(raw_in[n], 16)
                for n, t in vec.items():
                    sp.dma_start(t[:, :], w[n].partition_broadcast(P)).then_inc(vec_in, 16)
                sp.dma_start(cpw[:, :], w["cp_w"].rearrange("s o -> (s o)").partition_broadcast(P)).then_inc(vec_in, 16)
                sp.dma_start(small[:, 0:1], w["cp_b"].partition_broadcast(P)).then_inc(vec_in, 16)
                sp.dma_start(small[:, 1:2], w["D"].partition_broadcast(P)).then_inc(vec_in, 16)

            @block.scalar
            def _(act):
                for n in mats:
                    row = w[bias_of[n]].rearrange("(o c) -> o c", o=1)
                    at = slice(bias_at[n], bias_at[n] + mats[n][2])
                    act.dma_start(braw[0:1, at], row).then_inc(bias_in, 16)
                act.dma_start(araw[0:1, :], w["A"].rearrange("(o c) -> o c", o=1)).then_inc(bias_in, 16)
                for i, n in enumerate(mats):
                    act.wait_ge(raw_in[n], 16)
                    nc.scalar.copy(hi[n][:, :, :], raw[n][:, :, :]).then_inc(hi_made, 1)
                    if i == 1:
                        act.wait_ge(summed, 1)
                        act.dma_start(braw[LO_ROW:LO_ROW + 1, :], braw[0:1, :]).then_inc(bias_again, 16)
                    if i == 4:
                        act.wait_ge(bias_again, 16)
                        nc.scalar.copy(bhi[LO_ROW:LO_ROW + 1, :], braw[LO_ROW:LO_ROW + 1, :]).then_inc(bias_hi, 1)
                act.wait_ge(cleared, 1)
                nc.scalar.copy(brow[0:1, :], braw[0:1, :]).then_inc(bias_hi, 1)

            @block.gpsimd
            def _(pool):
                nc.gpsimd.memset(brow[:, :].bitcast(F32), 0.0).then_inc(cleared, 1)
                nc.gpsimd.memset(half[:, :], -0.5).then_inc(cleared, 1)

            @block.vector
            def _(dve):
                nc.vector.memset(ones[:, :].bitcast(F32), 1.0).then_inc(done, 1)
                dve.wait_ge(bias_in, 16 * n_bias)
                nc.vector.tensor_tensor(braw[0:1, DT:DT + S], braw[0:1, DT:DT + S], araw[0:1, :], ALU.add).then_inc(summed, 1)
                for i, n in enumerate(mats):
                    dve.wait_ge(hi_made, i + 1)
                    nc.vector.tensor_tensor(lo[n][:, :, :], raw[n][:, :, :], hi[n][:, :, :].bitcast(F32),
                                            ALU.subtract).then_inc(lo_made, 1)
                    if i == 4:
                        dve.wait_ge(bias_hi, 1)
                        dve.wait_ge(cleared, 1)
                        nc.vector.tensor_tensor(brow[LO_ROW:LO_ROW + 1, :], braw[LO_ROW:LO_ROW + 1, :],
                                                bhi[LO_ROW:LO_ROW + 1, :].bitcast(F32), ALU.subtract).then_inc(done, 1)
                dve.wait_ge(vec_in, 16 * n_vec)
                nc.vector.tensor_scalar(cpb1[:, :], small[:, 0:1], 1.0, None, ALU.add).then_inc(done, 1)
                nc.vector.tensor_scalar(d2[:, :], small[:, 1:2], 2.0, None, ALU.mult).then_inc(done, 1)


_W = ["W", "a_src", "a_dst", "W_bcdt", "b_bcdt", "abp_w", "abp_b", "cp_w", "cp_b", "W_hz", "b_hz", "out_w", "out_b",
      "fe1_w", "fe1_b", "fe_ln_g", "fe_ln_b", "fe2_w", "fe2_b", "A", "D", "g1_w", "g1_b", "g_ln_g", "g_ln_b", "g2_w",
      "g2_b", "ln_g", "ln_b"]


def kernel(**inputs):
    import numpy as _np
    import concourse.bacc as _bacc
    from concourse import mybir as _mybir
    from concourse.bass_utils import run_bass_kernel_spmd as _run

    nc = _bacc.Bacc("TRN2", target_bir_lowering=False, num_devices=1)
    arrays, aps = {}, {}
    for name in ["x", "adj"] + ["L0_gnn_" + n for n in _W]:
        a = _np.ascontiguousarray(inputs[name])
        arrays[f"in_{name}"] = a
        aps[name] = nc.dram_tensor(f"in_{name}", a.shape, _mybir.dt.from_np(a.dtype), kind="ExternalInput").ap()
    out = nc.dram_tensor("out_0", aps["x"].shape, _mybir.dt.float32, kind="ExternalOutput").ap()
    build(nc, aps["x"], aps["adj"], {n: aps["L0_gnn_" + n] for n in _W}, out)
    r = _run(nc, [arrays], core_ids=[0])
    return r.results[0]["out_0"]
```
